# Optimizing a Trainium2 kernel written in Bass

```python
import numpy as np
import jax
import jax.numpy as jnp

def _softmax(x, axis=-1):
    return jax.nn.softmax(x, axis=axis)

def _gelu(x):
    return jax.nn.gelu(x, approximate=True)

def _silu(x):
    return jax.nn.silu(x)

def _sigmoid(x):
    return jax.nn.sigmoid(x)

def _layernorm(x, axis=-1, eps=1e-05):
    m = jnp.mean(x, axis=axis, keepdims=True)
    v = jnp.var(x, axis=axis, keepdims=True)
    return (x - m) / jnp.sqrt(v + eps)

def _scatter_add(tgt, idx, src, axis=0):
    return tgt.at[idx].add(src)

def _segment_sum(src, seg, n):
    return jax.ops.segment_sum(src, seg, n)
kernel_name = 'mk_flamingo_gated_d4_seqx_r8_f1fc28'

def setup_inputs(seed: int=0):
    np.random.seed(seed)
    _w = jnp.asarray

    def _rec_inputs():
        import jax
        import jax.numpy as jnp
        _rk = jax.random.key(seed)
        x = -0.0002928 + 1 * jax.random.normal(jax.random.fold_in(_rk, 1), (32, 128, 128), jnp.float32)
        _lenS = 128 - jax.random.randint(jax.random.fold_in(_rk, 7), (32,), 0, max(1, 128 // 4) + 1, jnp.int32)
        _lenS2 = 128 - jax.random.randint(jax.random.fold_in(_rk, 8), (32,), 0, max(1, 128 // 4) + 1, jnp.int32)
        _ctx_1024P = jax.random.normal(jax.random.fold_in(_rk, 11), (32, 16, 128), jnp.float32)
        _ctx_1024c = jax.random.dirichlet(jax.random.fold_in(_rk, 511), 0.3 * jnp.ones((16,), jnp.float32), (32, 128))
        _ctx_1024t = jnp.einsum('bsk,bkd->bsd', _ctx_1024c, _ctx_1024P)
        _ctx_1024t = _ctx_1024t * jax.lax.rsqrt(jnp.mean(jnp.square(_ctx_1024t)) + 1e-12) * 0.953939
        ctx_1024 = -1.39393e-06 + 0.999914 * (_ctx_1024t + 0.3 * jax.random.normal(jax.random.fold_in(_rk, 611), (32, 128, 128), jnp.float32))
        _g = jax.random.normal(jax.random.fold_in(_rk, 9001), (2, 4), jnp.float32)
        _g = jnp.sign(_g) * jnp.maximum(jnp.abs(_g), 1.0) + (_g == 0) * 1.0
        g_xattn = _g[0]
        g_ffn = _g[1]
        return (x, ctx_1024, g_xattn, g_ffn)
    x, ctx_1024, g_xattn, g_ffn = _rec_inputs()

    def _L0_xattn_setup():
        import jax, jax.numpy as jnp
        import numpy as np
        import math
        EMBED_DIM = 128
        NUM_HEADS = 16
        HEAD_DIM = EMBED_DIM // NUM_HEADS
        ROPE_BASE = 10000.0

        def _rope_cache(S, D, dtype):
            inv_freq = 1.0 / ROPE_BASE ** (jnp.arange(0, D, 2, dtype=jnp.float32) / D)
            t = jnp.arange(S, dtype=jnp.float32)
            freqs = t[:, None] * inv_freq[None, :]
            return (jnp.cos(freqs).astype(dtype), jnp.sin(freqs).astype(dtype))

        def _apply_rope(x, cos, sin):
            x_even = x[..., 0::2]
            x_odd = x[..., 1::2]
            rot_even = x_even * cos - x_odd * sin
            rot_odd = x_odd * cos + x_even * sin
            return jnp.stack([rot_even, rot_odd], axis=-1).reshape(x.shape)
        key = jax.random.key(seed)
        ks = jax.random.split(key, 11)
        B, S, E = (2, 256, EMBED_DIM)
        s = 1.0 / math.sqrt(E)
        return {'query': jax.random.normal(ks[0], (B, S, E), jnp.float32), 'key': jax.random.normal(ks[1], (B, S, E), jnp.float32), 'value': jax.random.normal(ks[2], (B, S, E), jnp.float32), 'Wq': jax.random.normal(ks[3], (E, E), jnp.float32) * s, 'bq': jnp.zeros((E,), jnp.float32), 'Wk': jax.random.normal(ks[4], (E, E), jnp.float32) * s, 'bk': jnp.zeros((E,), jnp.float32), 'Wv': jax.random.normal(ks[5], (E, E), jnp.float32) * s, 'bv': jnp.zeros((E,), jnp.float32), 'Wo': jax.random.normal(ks[6], (E, E), jnp.float32) * s, 'bo': jnp.zeros((E,), jnp.float32)}
    _L0_xattn_all = _L0_xattn_setup()
    _L0_xattn_in = {k: v for k, v in _L0_xattn_all.items() if k in ('Wq', 'bq', 'Wk', 'bk', 'Wv', 'bv', 'Wo', 'bo')}
    del _L0_xattn_all

    def _L0_ffn_setup():
        import jax, jax.numpy as jnp
        import numpy as np
        B, S, D_MODEL, D_HIDDEN = (4, 256, 128, 512)

        def act_quant(x):
            scale = 127.0 / jnp.clip(jnp.max(jnp.abs(x), axis=-1, keepdims=True), 1e-05)
            return jnp.clip(jnp.round(x * scale), -128, 127) / scale

        def weight_quant(w):
            scale = 1.0 / jnp.clip(jnp.mean(jnp.abs(w)), 1e-05)
            return jnp.clip(jnp.round(w * scale), -1, 1) / scale

        def bit_linear(x, w):
            xq = x + jax.lax.stop_gradient(act_quant(x) - x)
            wq = w + jax.lax.stop_gradient(weight_quant(w) - w)
            return jnp.einsum('bsd,hd->bsh', xq, wq)

        def depthwise_conv1d(x_bcl, w, b):
            y = jax.lax.conv_general_dilated(x_bcl, w, window_strides=(1,), padding=[(1, 1)], dimension_numbers=('NCH', 'OIH', 'NCH'), feature_group_count=x_bcl.shape[1])
            return y + b[None, :, None]
        key = jax.random.key(seed)
        ks = jax.random.split(key, 5)
        lim1 = 1.0 / np.sqrt(D_MODEL)
        lim2 = 1.0 / np.sqrt(D_HIDDEN)
        limc = 1.0 / np.sqrt(3.0)
        return {'x': jax.random.normal(ks[0], (B, S, D_MODEL), dtype=jnp.float32), 'w1': jax.random.uniform(ks[1], (D_HIDDEN, D_MODEL), jnp.float32, -lim1, lim1), 'conv_w': jax.random.uniform(ks[2], (D_HIDDEN, 1, 3), jnp.float32, -limc, limc), 'conv_b': jax.random.uniform(ks[3], (D_HIDDEN,), jnp.float32, -limc, limc), 'w2': jax.random.uniform(ks[4], (D_MODEL, D_HIDDEN), jnp.float32, -lim2, lim2)}
    _L0_ffn_all = _L0_ffn_setup()
    _L0_ffn_in = {k: v for k, v in _L0_ffn_all.items() if k in ('w1', 'conv_w', 'conv_b', 'w2')}
    del _L0_ffn_all

    def _L1_xattn_setup():
        import jax, jax.numpy as jnp
        import numpy as np
        D_MODEL = 128
        NUM_HEADS = 16
        D_K = D_MODEL // NUM_HEADS
        key = jax.random.key(seed)
        ks = jax.random.split(key, 11)
        B, S, D = (4, 256, D_MODEL)
        scale = 1.0 / np.sqrt(D)
        return {'Q': jax.random.normal(ks[0], (B, S, D), jnp.float32), 'K': jax.random.normal(ks[1], (B, S, D), jnp.float32), 'V': jax.random.normal(ks[2], (B, S, D), jnp.float32), 'Wq': jax.random.normal(ks[3], (D, D), jnp.float32) * scale, 'bq': jnp.zeros((D,), jnp.float32), 'Wk': jax.random.normal(ks[4], (D, D), jnp.float32) * scale, 'bk': jnp.zeros((D,), jnp.float32), 'Wv': jax.random.normal(ks[5], (D, D), jnp.float32) * scale, 'bv': jnp.zeros((D,), jnp.float32), 'Wo': jax.random.normal(ks[6], (D, D), jnp.float32) * scale, 'bo': jnp.zeros((D,), jnp.float32)}
    _L1_xattn_all = _L1_xattn_setup()
    _L1_xattn_in = {k: v for k, v in _L1_xattn_all.items() if k in ('Wq', 'bq', 'Wk', 'bk', 'Wv', 'bv', 'Wo', 'bo')}
    del _L1_xattn_all

    def _L1_ffn_setup():
        import jax, jax.numpy as jnp
        import numpy as np
        B, S, D, H = (8, 128, 128, 512)
        E, R = (3, 8)
        SCALING = 1.0 / R

        def _mole(x, W, b, A, Bm, Rw):
            gates = jax.nn.softmax(jnp.einsum('bsd,de->bse', x, Rw), axis=-1)
            base = jnp.einsum('bsd,dh->bsh', x, W) + b
            z = jnp.einsum('bsd,edr->ebsr', x, A)
            zg = z * jnp.transpose(gates, (2, 0, 1))[..., None]
            lora = jnp.einsum('ebsr,erh->bsh', zg, Bm)
            return base + SCALING * lora
        key = jax.random.key(seed)
        ks = jax.random.split(key, 12)
        s = lambda k, shape, scale: jax.random.normal(k, shape, dtype=jnp.float32) * scale
        return {'x': s(ks[0], (B, S, D), 1.0), 'W1': s(ks[1], (D, H), D ** (-0.5)), 'b1': jnp.zeros((H,), jnp.float32), 'A1': s(ks[2], (E, D, R), D ** (-0.5)), 'B1': s(ks[3], (E, R, H), 0.0) + s(ks[4], (E, R, H), R ** (-0.5)), 'R1': s(ks[5], (D, E), D ** (-0.5)), 'W2': s(ks[6], (H, D), H ** (-0.5)), 'b2': jnp.zeros((D,), jnp.float32), 'A2': s(ks[7], (E, H, R), H ** (-0.5)), 'B2': s(ks[8], (E, R, D), R ** (-0.5)), 'R2': s(ks[9], (H, E), H ** (-0.5))}
    _L1_ffn_all = _L1_ffn_setup()
    _L1_ffn_in = {k: v for k, v in _L1_ffn_all.items() if k in ('W1', 'b1', 'A1', 'B1', 'R1', 'W2', 'b2', 'A2', 'B2', 'R2')}
    del _L1_ffn_all

    def _L2_xattn_setup():
        import jax, jax.numpy as jnp
        import numpy as np
        B, L_ENC, L_DEC, D = (16, 64, 128, 128)
        key = jax.random.key(seed)
        k1, k2, k3, k4, k5, k6 = jax.random.split(key, 6)
        encoder_hc = jax.random.normal(k1, (B, L_ENC, D), dtype=jnp.float32)
        decoder_hq = jax.random.normal(k2, (B, L_DEC, D), dtype=jnp.float32)
        w_sim = jax.random.normal(k3, (3 * D,), dtype=jnp.float32) * 0.02
        b_sim = jax.random.normal(k4, (1,), dtype=jnp.float32) * 0.02
        W_qv = jax.random.normal(k5, (4 * D, D), dtype=jnp.float32) * 0.02
        b_qv = jax.random.normal(k6, (D,), dtype=jnp.float32) * 0.02
        return {'encoder_hc': encoder_hc, 'decoder_hq': decoder_hq, 'w_sim': w_sim, 'b_sim': b_sim, 'W_qv': W_qv, 'b_qv': b_qv}
    _L2_xattn_all = _L2_xattn_setup()
    _L2_xattn_in = {k: v for k, v in _L2_xattn_all.items() if k in ('w_sim', 'b_sim', 'W_qv', 'b_qv')}
    del _L2_xattn_all

    def _L2_ffn_setup():
        import jax, jax.numpy as jnp
        import numpy as np
        D_MODEL = 128
        D_FF = 512
        N_EXPERTS = 8
        INIT_SCALE = 0.1

        def _trunc_normal(key, shape, std):
            return std * jax.random.truncated_normal(key, -2.0, 2.0, shape, dtype=jnp.float32)
        key = jax.random.key(seed)
        ks = jax.random.split(key, 5)
        x = jax.random.normal(ks[0], (4, 128, D_MODEL), dtype=jnp.float32)
        router_W = _trunc_normal(ks[1], (D_MODEL, N_EXPERTS), INIT_SCALE / np.sqrt(D_MODEL))
        router_b = jnp.zeros((N_EXPERTS,), dtype=jnp.float32)
        W1 = _trunc_normal(ks[2], (N_EXPERTS, D_MODEL, D_FF), INIT_SCALE / np.sqrt(D_MODEL))
        b1 = jnp.zeros((N_EXPERTS, D_FF), dtype=jnp.float32)
        W2 = _trunc_normal(ks[3], (N_EXPERTS, D_FF, D_MODEL), INIT_SCALE / np.sqrt(D_FF))
        b2 = jnp.zeros((N_EXPERTS, D_MODEL), dtype=jnp.float32)
        return {'x': x, 'router_W': router_W, 'router_b': router_b, 'W1': W1, 'b1': b1, 'W2': W2, 'b2': b2}
    _L2_ffn_all = _L2_ffn_setup()
    _L2_ffn_in = {k: v for k, v in _L2_ffn_all.items() if k in ('router_W', 'router_b', 'W1', 'b1', 'W2', 'b2')}
    del _L2_ffn_all

    def _L3_xattn_setup():
        import jax, jax.numpy as jnp
        import numpy as np
        MAX_BITS = 256.0

        def _quantize_kernel(kern):
            qmin = jnp.minimum(jnp.float32(10000000000.0), jnp.min(kern))
            qmax = jnp.maximum(jnp.float32(-10000000000.0), jnp.max(kern))
            s = 2.0 * jnp.maximum(jnp.abs(qmin), jnp.abs(qmax)) / MAX_BITS
            return jnp.round(kern / s) * s
        key = jax.random.key(seed)
        ks = jax.random.split(key, 9)
        B, S, D_IN, D_MODEL = (4, 256, 128, 128)
        sc = 0.02
        return {'q': jax.random.normal(ks[0], (B, S, D_IN), jnp.float32), 'k': jax.random.normal(ks[1], (B, S, D_IN), jnp.float32), 'v': jax.random.normal(ks[2], (B, S, D_IN), jnp.float32), 'Wq': jax.random.normal(ks[3], (D_IN, D_MODEL), jnp.float32) * sc, 'bq': jax.random.normal(ks[4], (D_MODEL,), jnp.float32) * sc, 'Wk': jax.random.normal(ks[5], (D_IN, D_MODEL), jnp.float32) * sc, 'bk': jax.random.normal(ks[6], (D_MODEL,), jnp.float32) * sc, 'Wv': jax.random.normal(ks[7], (D_IN, D_MODEL), jnp.float32) * sc, 'bv': jax.random.normal(ks[8], (D_MODEL,), jnp.float32) * sc}
    _L3_xattn_all = _L3_xattn_setup()
    _L3_xattn_in = {k: v for k, v in _L3_xattn_all.items() if k in ('Wq', 'bq', 'Wk', 'bk', 'Wv', 'bv')}
    del _L3_xattn_all

    def _L3_ffn_setup():
        import jax, jax.numpy as jnp
        import numpy as np
        B, T, C, H, E, MIN_E = (4, 256, 128, 128, 16, 2)
        IS_CAUSAL = False

        def _forward(hidden_states, sim_matrix, gates, q_proj, k_proj, v_proj, o_proj):
            b, t, c = hidden_states.shape
            n = b * t
            x = hidden_states.reshape(n, c)
            xn = x / jnp.maximum(jnp.linalg.norm(x, axis=-1, keepdims=True), 1e-12)
            sn = sim_matrix / jnp.maximum(jnp.linalg.norm(sim_matrix, axis=0, keepdims=True), 1e-12)
            logits = xn @ sn - jax.nn.sigmoid(gates)
            gated = jax.nn.relu(logits)
            hard = (gated > 0).astype(gated.dtype)
            mask = gated + jax.lax.stop_gradient(hard - gated)
            inactive = jnp.sum(hard, axis=1) == 0
            _, fb_idx = jax.lax.top_k(logits, MIN_E)
            fb = jnp.zeros((n, logits.shape[1]), gated.dtype).at[jnp.arange(n)[:, None], fb_idx].set(1.0)
            put = jax.lax.stop_gradient(inactive[:, None].astype(gated.dtype) * fb)
            mask = mask * (1.0 - put) + put
            masked = jnp.where(mask > 0, gated, -jnp.inf)
            w = jax.nn.softmax(masked, axis=-1)

            def moe_proj(p):
                y = jnp.einsum('nc,ech->neh', x, p)
                return jnp.einsum('ne,neh->nh', w, y)
            q = moe_proj(q_proj).reshape(b, t, -1)
            k = moe_proj(k_proj).reshape(b, t, -1)
            v = moe_proj(v_proj).reshape(b, t, -1)
            h = q.shape[-1]
            scores = jnp.einsum('bth,bsh->bts', q, k) / jnp.sqrt(jnp.asarray(h, q.dtype))
            if IS_CAUSAL and t > 1:
                causal = jnp.tril(jnp.ones((t, t), bool))
                scores = jnp.where(causal[None], scores, -jnp.inf)
            attn = jax.nn.softmax(scores, axis=-1)
            o = jnp.einsum('bts,bsh->bth', attn, v).reshape(n, h)
            z = jnp.einsum('ne,nh->enh', w, o)
            out = jnp.einsum('enh,ehc->nc', z, o_proj)
            return out.reshape(b, t, c)
        key = jax.random.key(seed)
        ks = jax.random.split(key, 6)
        lim_qkv = float(np.sqrt(6.0 / (C + H)))
        inp = {'hidden_states': jax.random.normal(ks[0], (B, T, C), jnp.float32), 'sim_matrix': jax.random.normal(ks[1], (C, E), jnp.float32), 'gates': jnp.zeros((E,), jnp.float32), 'q_proj': jax.random.uniform(ks[2], (E, C, H), jnp.float32, -lim_qkv, lim_qkv), 'k_proj': jax.random.uniform(ks[3], (E, C, H), jnp.float32, -lim_qkv, lim_qkv), 'v_proj': jax.random.uniform(ks[4], (E, C, H), jnp.float32, -lim_qkv, lim_qkv), 'o_proj': jax.random.uniform(ks[5], (E, H, C), jnp.float32, -lim_qkv, lim_qkv)}
        return inp
    _L3_ffn_all = _L3_ffn_setup()
    _L3_ffn_in = {k: v for k, v in _L3_ffn_all.items() if k in ('sim_matrix', 'gates', 'q_proj', 'k_proj', 'v_proj', 'o_proj')}
    del _L3_ffn_all
    return {'x': x, 'ctx_1024': ctx_1024, 'g_xattn': g_xattn, 'g_ffn': g_ffn, 'L0_xattn_Wq': _L0_xattn_in['Wq'], 'L0_xattn_bq': _L0_xattn_in['bq'], 'L0_xattn_Wk': _L0_xattn_in['Wk'], 'L0_xattn_bk': _L0_xattn_in['bk'], 'L0_xattn_Wv': _L0_xattn_in['Wv'], 'L0_xattn_bv': _L0_xattn_in['bv'], 'L0_xattn_Wo': _L0_xattn_in['Wo'], 'L0_xattn_bo': _L0_xattn_in['bo'], 'L0_ffn_w1': _L0_ffn_in['w1'], 'L0_ffn_conv_w': _L0_ffn_in['conv_w'], 'L0_ffn_conv_b': _L0_ffn_in['conv_b'], 'L0_ffn_w2': _L0_ffn_in['w2'], 'L1_xattn_Wq': _L1_xattn_in['Wq'], 'L1_xattn_bq': _L1_xattn_in['bq'], 'L1_xattn_Wk': _L1_xattn_in['Wk'], 'L1_xattn_bk': _L1_xattn_in['bk'], 'L1_xattn_Wv': _L1_xattn_in['Wv'], 'L1_xattn_bv': _L1_xattn_in['bv'], 'L1_xattn_Wo': _L1_xattn_in['Wo'], 'L1_xattn_bo': _L1_xattn_in['bo'], 'L1_ffn_W1': _L1_ffn_in['W1'], 'L1_ffn_b1': _L1_ffn_in['b1'], 'L1_ffn_A1': _L1_ffn_in['A1'], 'L1_ffn_B1': _L1_ffn_in['B1'], 'L1_ffn_R1': _L1_ffn_in['R1'], 'L1_ffn_W2': _L1_ffn_in['W2'], 'L1_ffn_b2': _L1_ffn_in['b2'], 'L1_ffn_A2': _L1_ffn_in['A2'], 'L1_ffn_B2': _L1_ffn_in['B2'], 'L1_ffn_R2': _L1_ffn_in['R2'], 'L2_xattn_w_sim': _L2_xattn_in['w_sim'], 'L2_xattn_b_sim': _L2_xattn_in['b_sim'], 'L2_xattn_W_qv': _L2_xattn_in['W_qv'], 'L2_xattn_b_qv': _L2_xattn_in['b_qv'], 'L2_ffn_router_W': _L2_ffn_in['router_W'], 'L2_ffn_router_b': _L2_ffn_in['router_b'], 'L2_ffn_W1': _L2_ffn_in['W1'], 'L2_ffn_b1': _L2_ffn_in['b1'], 'L2_ffn_W2': _L2_ffn_in['W2'], 'L2_ffn_b2': _L2_ffn_in['b2'], 'L3_xattn_Wq': _L3_xattn_in['Wq'], 'L3_xattn_bq': _L3_xattn_in['bq'], 'L3_xattn_Wk': _L3_xattn_in['Wk'], 'L3_xattn_bk': _L3_xattn_in['bk'], 'L3_xattn_Wv': _L3_xattn_in['Wv'], 'L3_xattn_bv': _L3_xattn_in['bv'], 'L3_ffn_sim_matrix': _L3_ffn_in['sim_matrix'], 'L3_ffn_gates': _L3_ffn_in['gates'], 'L3_ffn_q_proj': _L3_ffn_in['q_proj'], 'L3_ffn_k_proj': _L3_ffn_in['k_proj'], 'L3_ffn_v_proj': _L3_ffn_in['v_proj'], 'L3_ffn_o_proj': _L3_ffn_in['o_proj']}

def reference(x, ctx_1024, g_xattn, g_ffn, L0_xattn_Wq, L0_xattn_bq, L0_xattn_Wk, L0_xattn_bk, L0_xattn_Wv, L0_xattn_bv, L0_xattn_Wo, L0_xattn_bo, L0_ffn_w1, L0_ffn_conv_w, L0_ffn_conv_b, L0_ffn_w2, L1_xattn_Wq, L1_xattn_bq, L1_xattn_Wk, L1_xattn_bk, L1_xattn_Wv, L1_xattn_bv, L1_xattn_Wo, L1_xattn_bo, L1_ffn_W1, L1_ffn_b1, L1_ffn_A1, L1_ffn_B1, L1_ffn_R1, L1_ffn_W2, L1_ffn_b2, L1_ffn_A2, L1_ffn_B2, L1_ffn_R2, L2_xattn_w_sim, L2_xattn_b_sim, L2_xattn_W_qv, L2_xattn_b_qv, L2_ffn_router_W, L2_ffn_router_b, L2_ffn_W1, L2_ffn_b1, L2_ffn_W2, L2_ffn_b2, L3_xattn_Wq, L3_xattn_bq, L3_xattn_Wk, L3_xattn_bk, L3_xattn_Wv, L3_xattn_bv, L3_ffn_sim_matrix, L3_ffn_gates, L3_ffn_q_proj, L3_ffn_k_proj, L3_ffn_v_proj, L3_ffn_o_proj):
    import jax
    import jax.numpy as jnp

    def _L0_xattn_ref(query, key, value, Wq, bq, Wk, bk, Wv, bv, Wo, bo):
        import jax, jax.numpy as jnp
        import numpy as np
        import math
        EMBED_DIM = 128
        NUM_HEADS = 16
        HEAD_DIM = EMBED_DIM // NUM_HEADS
        ROPE_BASE = 10000.0

        def _rope_cache(S, D, dtype):
            inv_freq = 1.0 / ROPE_BASE ** (jnp.arange(0, D, 2, dtype=jnp.float32) / D)
            t = jnp.arange(S, dtype=jnp.float32)
            freqs = t[:, None] * inv_freq[None, :]
            return (jnp.cos(freqs).astype(dtype), jnp.sin(freqs).astype(dtype))

        def _apply_rope(x, cos, sin):
            x_even = x[..., 0::2]
            x_odd = x[..., 1::2]
            rot_even = x_even * cos - x_odd * sin
            rot_odd = x_odd * cos + x_even * sin
            return jnp.stack([rot_even, rot_odd], axis=-1).reshape(x.shape)
        B, S, E = query.shape
        H, D = (NUM_HEADS, HEAD_DIM)
        q = (query @ Wq.T + bq).reshape(B, S, H, D).transpose(0, 2, 1, 3)
        k = (key @ Wk.T + bk).reshape(B, S, H, D).transpose(0, 2, 1, 3)
        v = (value @ Wv.T + bv).reshape(B, S, H, D).transpose(0, 2, 1, 3)
        cos, sin = _rope_cache(S, D, q.dtype)
        q = _apply_rope(q, cos, sin)
        k = _apply_rope(k, cos, sin)
        scores = jnp.einsum('bhsd,bhtd->bhst', q, k) / math.sqrt(D)
        attn = jax.nn.softmax(scores, axis=-1)
        out = jnp.einsum('bhst,bhtd->bhsd', attn, v)
        out = out.transpose(0, 2, 1, 3).reshape(B, S, E)
        return out @ Wo.T + bo

    def _L0_ffn_ref(x, w1, conv_w, conv_b, w2):
        import jax, jax.numpy as jnp
        import numpy as np
        B, S, D_MODEL, D_HIDDEN = (4, 256, 128, 512)

        def act_quant(x):
            scale = 127.0 / jnp.clip(jnp.max(jnp.abs(x), axis=-1, keepdims=True), 1e-05)
            return jnp.clip(jnp.round(x * scale), -128, 127) / scale

        def weight_quant(w):
            scale = 1.0 / jnp.clip(jnp.mean(jnp.abs(w)), 1e-05)
            return jnp.clip(jnp.round(w * scale), -1, 1) / scale

        def bit_linear(x, w):
            xq = x + jax.lax.stop_gradient(act_quant(x) - x)
            wq = w + jax.lax.stop_gradient(weight_quant(w) - w)
            return jnp.einsum('bsd,hd->bsh', xq, wq)

        def depthwise_conv1d(x_bcl, w, b):
            y = jax.lax.conv_general_dilated(x_bcl, w, window_strides=(1,), padding=[(1, 1)], dimension_numbers=('NCH', 'OIH', 'NCH'), feature_group_count=x_bcl.shape[1])
            return y + b[None, :, None]
        h = bit_linear(x, w1)
        h = depthwise_conv1d(h.transpose(0, 2, 1), conv_w, conv_b)
        h = h.transpose(0, 2, 1)
        h = jax.nn.silu(h)
        return bit_linear(h, w2)

    def _L1_xattn_ref(Q, K, V, Wq, bq, Wk, bk, Wv, bv, Wo, bo):
        import jax, jax.numpy as jnp
        import numpy as np
        D_MODEL = 128
        NUM_HEADS = 16
        D_K = D_MODEL // NUM_HEADS
        B, S, D = Q.shape
        H, Dk = (NUM_HEADS, D_K)

        def proj(x, W, b):
            y = jnp.einsum('bsd,de->bse', x, W.T) + b
            return y.reshape(B, -1, H, Dk).transpose(0, 2, 1, 3)
        q = proj(Q, Wq, bq)
        k = proj(K, Wk, bk)
        v = proj(V, Wv, bv)
        scores = jnp.einsum('bhqd,bhkd->bhqk', q, k) / np.sqrt(Dk)
        attn = jax.nn.softmax(scores, axis=-1)
        out = jnp.einsum('bhqk,bhkd->bhqd', attn, v)
        out = out.transpose(0, 2, 1, 3).reshape(B, -1, D)
        return jnp.einsum('bsd,de->bse', out, Wo.T) + bo

    def _L1_ffn_ref(x, W1, b1, A1, B1, R1, W2, b2, A2, B2, R2):
        import jax, jax.numpy as jnp
        import numpy as np
        B, S, D, H = (8, 128, 128, 512)
        E, R = (3, 8)
        SCALING = 1.0 / R

        def _mole(x, W, b, A, Bm, Rw):
            gates = jax.nn.softmax(jnp.einsum('bsd,de->bse', x, Rw), axis=-1)
            base = jnp.einsum('bsd,dh->bsh', x, W) + b
            z = jnp.einsum('bsd,edr->ebsr', x, A)
            zg = z * jnp.transpose(gates, (2, 0, 1))[..., None]
            lora = jnp.einsum('ebsr,erh->bsh', zg, Bm)
            return base + SCALING * lora
        h = _mole(x, W1, b1, A1, B1, R1)
        h = jax.nn.relu(h)
        return _mole(h, W2, b2, A2, B2, R2)

    def _L2_xattn_ref(encoder_hc, decoder_hq, w_sim, b_sim, W_qv, b_qv):
        import jax, jax.numpy as jnp
        import numpy as np
        B, L_ENC, L_DEC, D = (16, 64, 128, 128)
        d = encoder_hc.shape[-1]
        w1, w2, w3 = (w_sim[:d], w_sim[d:2 * d], w_sim[2 * d:])
        Sim = (encoder_hc @ w1)[:, :, None] + (decoder_hq @ w2)[:, None, :] + jnp.einsum('bid,bjd->bij', encoder_hc * w3, decoder_hq) + b_sim[0]
        A = jax.nn.softmax(Sim, axis=2)
        hq_hat = jnp.einsum('bij,bjd->bid', A, decoder_hq)
        Batt = jax.nn.softmax(jnp.max(Sim, axis=2), axis=1)
        hc_bar = jnp.einsum('bi,bid->bd', Batt, encoder_hc)[:, None, :]
        hc_hat = jnp.broadcast_to(hc_bar, encoder_hc.shape)
        feats = jnp.concatenate([encoder_hc, hq_hat, encoder_hc * hq_hat, encoder_hc * hc_hat], axis=-1)
        hcq = feats @ W_qv + b_qv
        return hcq

    def _L2_ffn_ref(x, router_W, router_b, W1, b1, W2, b2):
        import jax, jax.numpy as jnp
        import numpy as np
        D_MODEL = 128
        D_FF = 512
        N_EXPERTS = 8
        INIT_SCALE = 0.1

        def _trunc_normal(key, shape, std):
            return std * jax.random.truncated_normal(key, -2.0, 2.0, shape, dtype=jnp.float32)
        logits = jnp.einsum('bsd,de->bse', x.astype(jnp.float32), router_W) + router_b
        probs = jax.nn.softmax(logits, axis=-1)
        top1 = jnp.argmax(probs, axis=-1)
        mask = jax.nn.one_hot(top1, N_EXPERTS, dtype=x.dtype)
        gates = mask * probs.astype(x.dtype)
        h = jax.nn.relu(jnp.einsum('bsd,edf->besf', x, W1) + b1[:, None, :])
        y = jnp.einsum('besf,efd->besd', h, W2) + b2[:, None, :]
        out = jnp.einsum('bse,besd->bsd', gates, y)
        return out

    def _L3_xattn_ref(q, k, v, Wq, bq, Wk, bk, Wv, bv):
        import jax, jax.numpy as jnp
        import numpy as np
        MAX_BITS = 256.0

        def _quantize_kernel(kern):
            qmin = jnp.minimum(jnp.float32(10000000000.0), jnp.min(kern))
            qmax = jnp.maximum(jnp.float32(-10000000000.0), jnp.max(kern))
            s = 2.0 * jnp.maximum(jnp.abs(qmin), jnp.abs(qmax)) / MAX_BITS
            return jnp.round(kern / s) * s
        qp = jnp.einsum('bsi,id->bsd', q, _quantize_kernel(Wq)) + bq
        kp = jnp.einsum('bsi,id->bsd', k, _quantize_kernel(Wk)) + bk
        vp = jnp.einsum('bsi,id->bsd', v, _quantize_kernel(Wv)) + bv
        dk = jnp.float32(kp.shape[-1])
        logits = jnp.einsum('bqd,bkd->bqk', qp, kp) / jnp.sqrt(dk)
        attn = jax.nn.softmax(logits, axis=-1)
        return jnp.einsum('bqk,bkd->bqd', attn, vp)

    def _L3_ffn_ref(hidden_states, sim_matrix, gates, q_proj, k_proj, v_proj, o_proj):
        import jax, jax.numpy as jnp
        import numpy as np
        B, T, C, H, E, MIN_E = (4, 256, 128, 128, 16, 2)
        IS_CAUSAL = False

        def _forward(hidden_states, sim_matrix, gates, q_proj, k_proj, v_proj, o_proj):
            b, t, c = hidden_states.shape
            n = b * t
            x = hidden_states.reshape(n, c)
            xn = x / jnp.maximum(jnp.linalg.norm(x, axis=-1, keepdims=True), 1e-12)
            sn = sim_matrix / jnp.maximum(jnp.linalg.norm(sim_matrix, axis=0, keepdims=True), 1e-12)
            logits = xn @ sn - jax.nn.sigmoid(gates)
            gated = jax.nn.relu(logits)
            hard = (gated > 0).astype(gated.dtype)
            mask = gated + jax.lax.stop_gradient(hard - gated)
            inactive = jnp.sum(hard, axis=1) == 0
            _, fb_idx = jax.lax.top_k(logits, MIN_E)
            fb = jnp.zeros((n, logits.shape[1]), gated.dtype).at[jnp.arange(n)[:, None], fb_idx].set(1.0)
            put = jax.lax.stop_gradient(inactive[:, None].astype(gated.dtype) * fb)
            mask = mask * (1.0 - put) + put
            masked = jnp.where(mask > 0, gated, -jnp.inf)
            w = jax.nn.softmax(masked, axis=-1)

            def moe_proj(p):
                y = jnp.einsum('nc,ech->neh', x, p)
                return jnp.einsum('ne,neh->nh', w, y)
            q = moe_proj(q_proj).reshape(b, t, -1)
            k = moe_proj(k_proj).reshape(b, t, -1)
            v = moe_proj(v_proj).reshape(b, t, -1)
            h = q.shape[-1]
            scores = jnp.einsum('bth,bsh->bts', q, k) / jnp.sqrt(jnp.asarray(h, q.dtype))
            if IS_CAUSAL and t > 1:
                causal = jnp.tril(jnp.ones((t, t), bool))
                scores = jnp.where(causal[None], scores, -jnp.inf)
            attn = jax.nn.softmax(scores, axis=-1)
            o = jnp.einsum('bts,bsh->bth', attn, v).reshape(n, h)
            z = jnp.einsum('ne,nh->enh', w, o)
            out = jnp.einsum('enh,ehc->nc', z, o_proj)
            return out.reshape(b, t, c)
        return _forward(hidden_states, sim_matrix, gates, q_proj, k_proj, v_proj, o_proj)
    x = x + jnp.tanh(g_xattn[0]) * _L0_xattn_ref(_layernorm(x, axis=-1), ctx_1024, ctx_1024, L0_xattn_Wq, L0_xattn_bq, L0_xattn_Wk, L0_xattn_bk, L0_xattn_Wv, L0_xattn_bv, L0_xattn_Wo, L0_xattn_bo)
    x = x + jnp.tanh(g_ffn[0]) * _L0_ffn_ref(_layernorm(x, axis=-1), L0_ffn_w1, L0_ffn_conv_w, L0_ffn_conv_b, L0_ffn_w2)
    x = x + jnp.tanh(g_xattn[1]) * _L1_xattn_ref(_layernorm(x, axis=-1), ctx_1024, ctx_1024, L1_xattn_Wq, L1_xattn_bq, L1_xattn_Wk, L1_xattn_bk, L1_xattn_Wv, L1_xattn_bv, L1_xattn_Wo, L1_xattn_bo)
    x = x + jnp.tanh(g_ffn[1]) * _L1_ffn_ref(_layernorm(x, axis=-1), L1_ffn_W1, L1_ffn_b1, L1_ffn_A1, L1_ffn_B1, L1_ffn_R1, L1_ffn_W2, L1_ffn_b2, L1_ffn_A2, L1_ffn_B2, L1_ffn_R2)
    x = x + jnp.tanh(g_xattn[2]) * _L2_xattn_ref(_layernorm(x, axis=-1), ctx_1024, L2_xattn_w_sim, L2_xattn_b_sim, L2_xattn_W_qv, L2_xattn_b_qv)
    x = x + jnp.tanh(g_ffn[2]) * _L2_ffn_ref(_layernorm(x, axis=-1), L2_ffn_router_W, L2_ffn_router_b, L2_ffn_W1, L2_ffn_b1, L2_ffn_W2, L2_ffn_b2)
    x = x + jnp.tanh(g_xattn[3]) * _L3_xattn_ref(_layernorm(x, axis=-1), ctx_1024, ctx_1024, L3_xattn_Wq, L3_xattn_bq, L3_xattn_Wk, L3_xattn_bk, L3_xattn_Wv, L3_xattn_bv)
    x = x + jnp.tanh(g_ffn[3]) * _L3_ffn_ref(_layernorm(x, axis=-1), L3_ffn_sim_matrix, L3_ffn_gates, L3_ffn_q_proj, L3_ffn_k_proj, L3_ffn_v_proj, L3_ffn_o_proj)
    return x

_drawn_inputs = setup_inputs


def setup_inputs(seed=0):
    import zlib

    import numpy as np

    out = dict(_drawn_inputs(seed))
    spreads = {'L0_xattn_bq': (0.0, 0.384),
     'L0_xattn_bk': (0.0, 0.693),
     'L0_xattn_bv': (0.0, 0.1),
     'L0_xattn_bo': (0.0, 0.1),
     'L1_xattn_bq': (0.0, 0.328),
     'L1_xattn_bk': (0.0, 0.8),
     'L1_xattn_bv': (0.0, 0.1),
     'L1_xattn_bo': (0.0, 0.1),
     'L1_ffn_b1': (0.0, 0.1),
     'L1_ffn_b2': (0.0, 0.1),
     'L2_ffn_router_b': (0.0, 0.8),
     'L2_ffn_b1': (0.0, 0.8),
     'L2_ffn_b2': (0.0, 0.644),
     'L3_ffn_gates': (0.0, 0.1)}
    factors = {'L1_ffn_R2': 2.942,
     'L2_xattn_w_sim': 3.525,
     'L2_xattn_b_qv': 3.147,
     'L2_ffn_router_W': 5.305,
     'L2_ffn_W1': 8.0,
     'L2_ffn_W2': 8.0,
     'L3_xattn_Wq': 8.0,
     'L3_xattn_bq': 8.0,
     'L3_xattn_Wk': 8.0,
     'L3_xattn_bk': 8.0,
     'L3_xattn_bv': 3.742,
     'L3_ffn_q_proj': 3.195,
     'L3_ffn_k_proj': 3.199}
    for name, (base, spread) in spreads.items():
        noise = np.random.default_rng([zlib.crc32(name.encode()), seed]).standard_normal(out[name].shape)
        drawn = base * np.exp(spread * noise) if base else spread * noise
        out[name] = jnp.asarray(drawn.astype(out[name].dtype))
    for name, factor in factors.items():
        out[name] = (out[name] * factor).astype(out[name].dtype)
    return out
```

```python
from contextlib import ExitStack

import numpy as np
import concourse.bass as bass
from concourse import mybir

F32 = mybir.dt.float32
F32R = mybir.dt.float32r
BF16 = mybir.dt.bfloat16
I32 = mybir.dt.int32
ALU = mybir.AluOpType
ACT = mybir.ActivationFunctionType
AX = mybir.AxisListType.X

P = 128
NSEQ = 32
GS = 4
NG = NSEQ // GS
T = GS * P
HEADS, HD = 16, 8
HID = 512
NHB = HID // P
LN_EPS = 1e-5
MAGIC = 12582912.0


class Ring:

    def __init__(self, sem, depth):
        self.sem, self.depth = sem, depth

    def grant(self, eng):
        eng.sem_inc(self.sem, self.depth)

    def wait_free(self, eng, unit):
        eng.wait_ge(self.sem, unit + 1)

    def wait_done(self, eng, unit):
        eng.wait_ge(self.sem, unit + 1 + self.depth)


class Chain:

    def __init__(self, eng, sem, links, it):
        self.eng, self.sem, self.links, self.it, self.n = eng, sem, links, it, 0

    def __call__(self, ins):
        self.n += 1
        ins.then_inc(self.sem, 1)
        self.eng.wait_ge(self.sem, self.it * self.links + self.n)


class Core:
    pass


def seq(c):
    return slice(c * P, (c + 1) * P)


def bcast(ap, shape):
    return ap.broadcast_to(shape)


def ln_tensors(k, sb, sem):
    k.stats = sb("ln_stats", [P, GS, 6], F32)
    k.mv = sb("ln_mean_var", [P, GS, 2], F32)
    k.rstd = sb("ln_rstd", [P, GS], F32)
    k.xn = sb("xn", [P, GS, P], F32)
    k.xnT = sb("xnT", [P, 2, T], F32)
    k.s_rows = sem("ln_rows_counted")
    k.s_stats = sem("ln_stats_ready")
    k.s_vare = sem("ln_var_plus_eps")
    k.s_rstd = sem("ln_rstd_ready")
    k.s_xn = sem("xn_ready")
    k.r_xnT_psum = Ring(sem("xnT_in_psum"), 1)
    k.r_xnT = Ring(sem("xnT_ready"), 1)
    k.r_xnT_used = Ring(sem("xnT_used"), 2)


def ln_stats(k, dve, g):
    for c in range(GS):
        ins = dve.bn_stats(k.stats[:, c, :], k.x_sb[:, bass.ds((g * GS + c) * P, P)])
    ins.then_inc(k.s_rows, 1)
    dve.wait_ge(k.s_rows, g + 1)
    dve.tensor_copy(k.one_cell[:, :], k.eps[:, 0:1])
    for c in range(GS):
        ins = dve.bn_aggr(k.mv[:, c, :], k.stats[:, c, :])
    ins.then_inc(k.s_stats, 1)


def ln_rstd(k, pool, g):
    pool.wait_ge(k.s_stats, g + 1)
    pool.tensor_tensor(k.rstd[:, :], k.mv[:, :, 1], k.eps[:, :], ALU.add).then_inc(k.s_vare, 1)
    pool.wait_ge(k.s_vare, g + 1)
    pool.tensor_tensor(k.rstd[:, :], k.rstd[:, :], k.minus_half[:, 0:GS], ALU.pow).then_inc(k.s_rstd, 1)


def ln_apply(k, dve, g):
    dve.wait_ge(k.s_rstd, g + 1)
    k.r_xnT_psum.wait_free(dve, g)
    for c in range(GS):
        ins = dve.tensor_scalar(k.xn[:, c, :], k.x_sb[:, bass.ds((g * GS + c) * P, P)],
                                k.mv[:, c, 0:1], k.rstd[:, c:c + 1], ALU.subtract, ALU.mult)
    ins.then_inc(k.s_xn, 1)


def ln_transpose(k, pe, g, bank):
    pe.wait_ge(k.s_xn, g + 1)
    k.r_xnT.wait_free(pe, g)
    for c in range(GS):
        ins = pe.transpose(bank[:, seq(c)], k.xn[:, c, :], k.ident[:, :])
    ins.then_inc(k.r_xnT_psum.sem, 1)


def ln_evacuate(k, act, g, par, bank):
    k.r_xnT_psum.wait_done(act, g)
    k.r_xnT_used.wait_free(act, g)
    act.activation(k.xnT[:, par, :], bank[:, :], ACT.Copy).then_inc(k.r_xnT.sem, 1)


def groups(eng, body, chain_sem=None, links=0):
    links = links if isinstance(links, tuple) else (links, links)
    per_pair = links[0]

    def two(it, last):
        chain = Chain(eng, chain_sem, per_pair, it)
        for par in range(2):
            body(2 * it + par, par, not (last and par), chain)
        assert chain.n == links[last], f"{chain.n} links, not {links[last]}"

    with eng.Fori(0, NG // 2 - 1) as it:
        two(it, False)
    two(NG // 2 - 1, True)


NPART = 3
SROWS = NPART * NPART * HD
AROWS = SROWS + NPART


def heads_attention(nc, k, name, rope, gain):
    with ExitStack() as ctx:
        sb, sem = k.local(ctx, name)
        ln_tensors(k, sb, sem)
        w = {n[len(name) + 1:]: t for n, t in k.w.items() if n.startswith(name + "_")}
        ctxT = sb("ctxT", [P, 2, T], F32)
        gb = sb("tanh_g_bias", [P, GS, P], F32)
        bias = sb("out_bias", [P, P], F32)
        turned = {n: [sb(f"{n}_turned{i}", [P, T], F32) for i in range(2)] for n in "kq"} if rope else None
        full = {n: sb(f"{n}_full", [P, T], F32) for n in "kq"}
        rest = sb("rest", [P, T], F32)
        parts = {n: sb(f"{n}_parts", [P, NPART, T], BF16) for n in "kq"}
        stack = {n: sb(f"{n}_stack", [AROWS, 2, HEADS, T], BF16) for n in "kq"}
        vm = sb("v_by_head", [P, 2, GS, 4, P], F32)
        nm = sb("minus_max", [P, GS, HEADS], F32)
        nm_rest = sb("minus_max_rest", [P, HEADS], F32)
        mp = sb("minus_max_parts", [P, GS, NPART * HEADS], BF16)
        mT = sb("minus_max_T", [NPART * HEADS, T], BF16)
        pT = sb("probsT", [P, 2, HEADS, P], F32)
        rz = sb("rsum", [P, P], F32)
        aT = sb("aT", [P, 2, P], F32)
        ones8 = sb("ones_by_head", [P, 4, 32], F32)
        bankS, bankT = [k.bank(0), k.bank(1)], [k.bank(2), k.bank(3)]
        bankA, bankP0, bankP1, bankM = (k.bank(i) for i in range(4, 8))
        scale = float(HD) ** -0.5
        scratch = {n: nc.dram_tensor(f"{name}_{n}_scratch", (2, P, NPART, T), BF16).ap() for n in "kq"}
        scratch_m = nc.dram_tensor(f"{name}_max_scratch", (2, NPART * HEADS, T), BF16).ap()

        s_fill = sem("fills_done")
        s_bias = sem("bias_step")
        s_bp = sem("v_bias_in_psum")
        s_chain = sem("dve_step")
        s_split = sem("pool_step")
        s_ctx = [sem(f"ctxT_in_{p}") for p in range(2)]
        r_ctx = Ring(sem("ctxT_used"), 2)
        s_proj = {n: sem(f"{n}_in_psum") for n in "kqv"}
        r_out = {n: Ring(sem(f"{n}_emptied"), 1) for n in "kq"}
        r_v = Ring(sem("v_ready"), 1)
        r_full = {n: Ring(sem(f"{n}_split"), 1) for n in "kq"}
        s_stack = [sem(f"stack_in_{p}") for p in range(2)]
        s_head = sem("pool_head_step")
        s_nm = sem("minus_max_ready")
        s_s = sem("scores_in_psum")
        r_red = Ring(sem("maxima_taken"), 2)
        r_mp = Ring(sem("minus_max_split"), GS)
        r_mT = Ring(sem("minus_maxT_in_psum"), 1)
        r_mTs = Ring(sem("minus_maxT_ready"), 1)
        s_parts_out = {n: sem(f"{n}_parts_in_dram") for n in "kq"}
        s_mT_out = sem("minus_maxT_in_dram")
        s_shift = [sem(f"shift_rows_in_{p}") for p in range(2)]
        s_t = sem("scoresT_in_psum")
        r_exp = Ring(sem("exp_done"), 2)
        r_av = Ring(sem("attn_in_psum"), 2)
        r_aT = Ring(sem("aT_ready"), 1)
        r_o = Ring(sem("out_in_psum"), 2)
        r_x = Ring(sem("x_updated"), 1)

        def landed(eng, sems, g, par, dmas):
            eng.wait_ge(sems[par], (g - par) * 8 * dmas + 16 * dmas)

        block = ctx.enter_context(nc.Block())

        @block.sync
        def _(sp):
            def load_ctx(g, par):
                r_ctx.wait_free(sp, g)
                sp.dma_start(ctxT[:, par, :], k.dram["ctxT"][:, bass.ds(g * T, T)]).then_inc(s_ctx[par], 16)

            def build_stacks(g, par):
                for n in "kq":
                    r_full[n].wait_done(sp, g)
                    sp.dma_start(scratch[n][par], parts[n][:, :, :]).then_inc(s_parts_out[n], 16)
                for n in "kq":
                    sp.wait_ge(s_parts_out[n], 16 * (g + 1))
                    for a in range(NPART):
                        for b in range(NPART):
                            rows = slice((a * NPART + b) * HD, (a * NPART + b + 1) * HD)
                            part = scratch[n][par][:, a if n == "q" else b, :].rearrange("(h d) t -> d h t", d=HD)
                            sp.dma_start(stack[n][rows, par, :, :], part).then_inc(s_stack[par], 16)

            def shift_rows(g, par):
                r_mTs.wait_done(sp, g)
                sp.dma_start(scratch_m[par], mT[:, :]).then_inc(s_mT_out, 16)
                sp.wait_ge(s_mT_out, 16 * (g + 1))
                sp.dma_start(stack["q"][SROWS:AROWS, par, :, :],
                             scratch_m[par].rearrange("(a h) t -> a h t", a=NPART)).then_inc(s_shift[par], 16)

            sp.wait_ge(s_fill, 5)
            load_ctx(0, 0)
            load_ctx(1, 1)
            build_stacks(0, 0)
            shift_rows(0, 0)
            build_stacks(1, 1)

            def body(t, par, more, chain):
                if not isinstance(t, int):
                    load_ctx(t + 2, par)
                if more:
                    shift_rows(t + 1, 1 - par)
                if not isinstance(t, int):
                    build_stacks(t + 2, par)

            groups(sp, body)

        @block.tensor
        def _(pe):
            for r in (k.r_xnT_psum, k.r_xnT_used, r_ctx, r_mT, r_av, r_o):
                r.grant(pe)
            k.wait_weights(pe, name)
            pe.matmul(bankM[:, 0:P], bcast(w["bv"][:, 0:1], [P, P]), w["wo"][:, :], start=True, stop=True)\
              .then_inc(s_bp, 1)
            pe.wait_ge(s_bias, 1)
            pe.wait_ge(s_fill, 5)

            def project(n, g, par, src):
                last = None
                for bank, kind in ((bankP0, ""), (bankP1, "s"))[:2 if rope else 1]:
                    last = pe.matmul(bank[:, :], w[f"w{n}{kind}"][:, :], src, start=True, stop=True)
                last.then_inc(s_proj[n], 1)

            def front_a(g, par):
                r_out["q"].wait_free(pe, g)
                ln_transpose(k, pe, g, bankP1)
                r_v.wait_free(pe, g)
                landed(pe, s_ctx, g, par, 1)
                k.r_xnT.wait_done(pe, g)
                project("k", g, par, ctxT[:, par, :])

            def front_b(g, par):
                r_out["k"].wait_done(pe, g)
                project("q", g, par, k.xnT[:, par, :])
                r_out["q"].wait_done(pe, g)
                pe.sem_inc(k.r_xnT_used.sem, 1)
                for c in range(GS):
                    ins = pe.matmul(bankP0[:, seq(c)], ctxT[:, par, seq(c)], w["wv"][:, :], start=True, stop=True)
                ins.then_inc(s_proj["v"], 1)
                r_v.wait_done(pe, g)
                pe.sem_inc(r_ctx.sem, 1)

            def scores(g, par, c):
                if c == 0:
                    landed(pe, s_stack, g, par, 2 * NPART * NPART)
                for u in range(4):
                    unit = (g * GS + c) * 4 + u
                    r_red.wait_free(pe, unit)
                    for j in range(4):
                        h = 4 * u + j
                        ins = pe.matmul(bankS[u % 2][:, seq(j)], stack["q"][0:SROWS, par, h, seq(c)],
                                        stack["k"][0:SROWS, par, h, seq(c)], start=True, stop=True)
                    ins.then_inc(s_s, 1)

            def turn_max(g):
                r_mp.wait_done(pe, g * GS + GS - 1)
                r_x.wait_free(pe, g * GS)
                for c in range(GS):
                    ins = pe.matmul(bankM[0:NPART * HEADS, seq(c)], mp[:, c, :], k.ident_bf[:, :], start=True,
                                    stop=True)
                ins.then_inc(r_mT.sem, 1)

            def scoresT(g, par, c):
                if c == 0:
                    landed(pe, s_shift, g, par, 1)
                for u in range(4):
                    r_exp.wait_free(pe, (g * GS + c) * 4 + u)
                    for j in range(4):
                        h = 4 * u + j
                        ins = pe.matmul(bankT[u % 2][:, seq(j)], stack["k"][:, par, h, seq(c)],
                                        stack["q"][:, par, h, seq(c)], start=True, stop=True)
                    ins.then_inc(s_t, 1)

            def attend(g, par, c):
                unit = g * GS + c
                r_exp.wait_done(pe, unit * 4 + 3)
                r_aT.wait_free(pe, unit)
                for cols, lhs in ((slice(0, P), lambda i, j: vm[:, par, c, j, 32 * i:32 * i + 32]),
                                  (slice(P, 2 * P), lambda i, j: ones8[:, j, :])):
                    for j in range(4):
                        for i in range(4):
                            ins = pe.matmul(bankA[32 * i:32 * i + 32, cols], lhs(i, j), pT[:, c % 2, 4 * i + j, :],
                                            start=(j == 0), stop=(j == 3))
                ins.then_inc(r_av.sem, 1)

            def out(g, c):
                unit = g * GS + c
                r_aT.wait_done(pe, unit)
                if c == 0:
                    r_mTs.wait_done(pe, g)
                r_x.wait_free(pe, unit)
                pe.matmul(bankM[:, 0:P], aT[:, c % 2, :], w["wo"][:, :], start=True, stop=True).then_inc(r_o.sem, 1)

            front_a(0, 0)
            front_b(0, 0)
            for c in range(GS):
                scores(0, 0, c)
            turn_max(0)
            front_a(1, 1)
            front_b(1, 1)

            def body(t, par, more, chain):
                nxt = (t + 1, 1 - par)
                after = not isinstance(t, int)
                sc = lambda c: scores(*nxt, c) if more else None
                scoresT(t, par, 0)
                scoresT(t, par, 1)
                attend(t, par, 0)
                sc(0)
                out(t, 0)
                attend(t, par, 1)
                scoresT(t, par, 2)
                sc(1)
                out(t, 1)
                attend(t, par, 2)
                scoresT(t, par, 3)
                sc(2)
                out(t, 2)
                sc(3)
                attend(t, par, 3)
                if after:
                    front_a(t + 2, par)
                out(t, 3)
                if after:
                    front_b(t + 2, par)
                if more:
                    turn_max(t + 1)

            groups(pe, body)

        @block.scalar
        def _(act):
            for r in (k.r_xnT, r_v, r_mTs, r_exp) + (() if rope else (r_out["k"], r_out["q"])):
                r.grant(act)
            k.wait_weights(act, name)
            act.wait_ge(s_fill, 5)

            def front(g, par):
                ln_evacuate(k, act, g, par, bankP1)
                if not rope:
                    for n in "kq":
                        act.wait_ge(s_proj[n], g + 1)
                        r_full[n].wait_free(act, g)
                        act.activation(full[n][:, :], bankP0[:, :], ACT.Identity, bias=w["b" + n][:, :])\
                           .then_inc(r_out[n].sem, 1)
                act.wait_ge(s_proj["v"], g + 1)
                if not isinstance(g, int):
                    act.wait_ge(r_av.sem, (g - 1) * GS + 2)
                for j in range(4):
                    src = bankP0.rearrange("p (c i j d) -> p c i j d", c=GS, i=4, j=4)[:, :, :, j, :]
                    dst = vm[:, par, :, j, :].rearrange("p c (i j d) -> p c i j d", i=4, j=4)[:, :, :, j, :]
                    ins = act.activation(dst, src, ACT.Copy)
                ins.then_inc(r_v.sem, 1)

            def max_out(g):
                r_mT.wait_done(act, g)
                act.activation(mT[:, :], bankM[0:NPART * HEADS, :], ACT.Copy).then_inc(r_mTs.sem, 1)

            def exps(g, c):
                unit = g * GS + c
                r_av.wait_free(act, unit)
                for u in range(4):
                    act.wait_ge(s_t, unit * 4 + u + 1)
                    act.activation(pT[:, c % 2, 4 * u:4 * u + 4, :], bankT[u % 2].rearrange("p (j q) -> p j q", j=4),
                                   ACT.Exp, scale=scale).then_inc(r_exp.sem, 1)

            front(0, 0)
            max_out(0)
            front(1, 1)

            def body(t, par, more, chain):
                for c in range(GS):
                    exps(t, c)
                if not isinstance(t, int):
                    front(t + 2, par)
                if more:
                    act.wait_ge(s_mT_out, 16 * (t + 1))
                    max_out(t + 1)

            groups(act, body)

        @block.gpsimd
        def _(pool):
            for r in (r_full["k"], r_full["q"], r_mp):
                r.grant(pool)
            pool.memset(vm[:, 0, :, :, :], 0.0).then_inc(s_fill, 1)
            pool.memset(vm[:, 1, :, :, :], 0.0).then_inc(s_fill, 1)

            def split(g, par, chain):
                for n in "kq":
                    if rope:
                        pool.wait_ge(r_out[n].sem, g + 2)
                        chain(pool.tensor_tensor(full[n][:, :], turned[n][0][:, :], turned[n][1][:, :], ALU.add))
                    else:
                        r_out[n].wait_done(pool, g)
                    if not isinstance(g, int) or g > 0:
                        pool.wait_ge(s_parts_out[n], 16 * g)
                    p = [parts[n][:, a, :] for a in range(NPART)]
                    chain(pool.tensor_tensor(p[0], full[n][:, :], bcast(k.ones[:, 0:1], [P, T]), ALU.mult))
                    chain(pool.tensor_tensor(rest[:, :], full[n][:, :], p[0], ALU.subtract))
                    chain(pool.tensor_tensor(p[1], rest[:, :], bcast(k.ones[:, 0:1], [P, T]), ALU.mult))
                    pool.tensor_tensor(p[2], rest[:, :], p[1], ALU.subtract).then_inc(r_full[n].sem, 1)
                    r_full[n].wait_done(pool, g)

            def split_max(g, c, chain):
                unit = g * GS + c
                pool.wait_ge(s_nm, unit + 1)
                if c == 0:
                    r_mT.wait_free(pool, g)
                part = lambda a: mp[:, c, a * HEADS:(a + 1) * HEADS]
                chain(pool.tensor_tensor(part(0), nm[:, c, :], k.ones[:, 0:HEADS], ALU.mult))
                chain(pool.tensor_tensor(nm_rest[:, :], nm[:, c, :], part(0), ALU.subtract))
                chain(pool.tensor_tensor(part(1), nm_rest[:, :], k.ones[:, 0:HEADS], ALU.mult))
                pool.tensor_tensor(part(2), nm_rest[:, :], part(1), ALU.subtract).then_inc(r_mp.sem, 1)
                r_mp.wait_done(pool, unit)

            head = Chain(pool, s_head, 0, 0)
            ln_rstd(k, pool, 0)
            split(0, 0, head)
            for c in range(GS):
                split_max(0, c, head)
            ln_rstd(k, pool, 1)
            split(1, 1, head)

            def body(t, par, more, chain):
                if not isinstance(t, int):
                    ln_rstd(k, pool, t + 2)
                if more:
                    for c in range(GS):
                        split_max(t + 1, c, chain)
                if not isinstance(t, int):
                    split(t + 2, par, chain)

            groups(pool, body, s_split, (36 + 4 * rope, 12))

        @block.vector
        def _(dve):
            r_red.grant(dve)
            r_aT.grant(dve)
            r_x.grant(dve)
            if rope:
                r_out["k"].grant(dve)
                r_out["q"].grant(dve)
            dve.memset(stack["k"][64:AROWS, :, :, :], 1.0).then_inc(s_fill, 1)
            dve.memset(ones8[:, :, :], 0.0).then_inc(s_fill, 1)
            dve.wait_ge(s_fill, 4)
            for j in range(4):
                ins = dve.memset(ones8[:, j, 8 * j:8 * j + 8], 1.0)
            ins.then_inc(s_fill, 1)
            k.wait_weights(dve, name)
            dve.wait_ge(s_bp, 1)
            dve.tensor_tensor(bias[:, :], bankM[:, 0:P], w["bo"][:, :], ALU.add).then_inc(s_bias, 1)
            dve.wait_ge(s_bias, 1)
            for c in range(GS):
                ins = dve.tensor_scalar(gb[:, c, :], bias[:, :], k.tanh_g[:, gain:gain + 1], None, ALU.mult)
            ins.then_inc(s_bias, 1)
            dve.wait_ge(s_bias, 2)

            def norm(g):
                ln_stats(k, dve, g)
                ln_apply(k, dve, g)
                dve.wait_ge(k.s_xn, g + 1)
                xs = k.x_sb[:, bass.ds(g * T, T)]
                dve.tensor_tensor(xs, xs, gb[:, :, :].rearrange("p c d -> p (c d)"), ALU.add)

            def rotate(g):
                if not rope:
                    return
                for n in "kq":
                    dve.wait_ge(s_proj[n], g + 1)
                    r_full[n].wait_free(dve, g)
                    dve.scalar_tensor_tensor(turned[n][0][:, :], bankP0[:, :], w["b" + n][:, :], w["cos"][:, :],
                                             ALU.add, ALU.mult)
                    dve.scalar_tensor_tensor(turned[n][1][:, :], bankP1[:, :], w["b" + n + "s"][:, :],
                                             w["sin"][:, :], ALU.add, ALU.mult).then_inc(r_out[n].sem, 1)

            def maxima(g, c):
                r_mp.wait_free(dve, g * GS + c)
                for u in range(4):
                    unit = (g * GS + c) * 4 + u
                    dve.wait_ge(s_s, unit + 1)
                    dve.tensor_reduce(nm[:, c, 4 * u:4 * u + 4], bankS[u % 2].rearrange("p (j t) -> p j t", j=4), AX,
                                      ALU.max, negate=True).then_inc(r_red.sem, 1)
                r_red.wait_done(dve, (g * GS + c) * 4 + 3)
                dve.sem_inc(s_nm, 1)

            def normalise(g, c, chain):
                unit = g * GS + c
                r_av.wait_done(dve, unit)
                chain(dve.reciprocal(rz[:, :], bankA[:, P:2 * P]))
                r_o.wait_free(dve, unit)
                dve.tensor_tensor(aT[:, c % 2, :], bankA[:, 0:P], rz[:, :], ALU.mult).then_inc(r_aT.sem, 1)

            def update(g, c):
                unit = g * GS + c
                r_o.wait_done(dve, unit)
                xc = k.x_sb[:, bass.ds(unit * P, P)]
                dve.scalar_tensor_tensor(xc, bankM[:, 0:P], k.tanh_g[:, gain:gain + 1], xc, ALU.mult, ALU.add)\
                   .then_inc(r_x.sem, 1)

            norm(0)
            rotate(0)
            for c in range(GS):
                maxima(0, c)
            norm(1)
            rotate(1)

            def body(t, par, more, chain):
                after = not isinstance(t, int)
                if after:
                    norm(t + 2)
                for c in range(GS):
                    if c < 3:
                        normalise(t, c, chain)
                        if more:
                            maxima(t + 1, c)
                        update(t, c)
                    else:
                        if more:
                            maxima(t + 1, c)
                        normalise(t, c, chain)
                        if after:
                            rotate(t + 2)
                        update(t, c)

            groups(dve, body, s_chain, (2 * GS, 2 * GS))


def layer0_attention(nc, k):
    heads_attention(nc, k, "l0x", True, 0)


def layer1_attention(nc, k):
    heads_attention(nc, k, "l1x", False, 1)


def layer0_ffn(nc, k):
    with ExitStack() as ctx:
        sb, sem = k.local(ctx, "l0f")
        ln_tensors(k, sb, sem)
        w = k.w
        wsum = sb("abs_sums", [P, 2], F32)
        wmean = sb("abs_mean", [P, 2], F32)
        winv = sb("abs_rmean", [P, 2], F32)
        wr = sb("w_steps", [P, 2, HID], F32)
        w1q = sb("w1q", [P, HID], BF16)
        w2q = sb("w2q", [P, NHB, P], BF16)
        amax = sb("amax", [P, GS], F32)
        qs = sb("q_scale", [P, GS], F32)
        dq = sb("q_step", [P, GS], F32)
        xr = sb("xn_steps", [P, GS, P], F32)
        xq = sb("xq", [P, GS, P], BF16)
        xqT = sb("xqT", [P, T], BF16)
        srow = sb("q_step_rows", [P, GS, P], F32)
        hs = sb("h_scaled", [P, 2, GS, P], F32)
        cv = sb("convolved", [P, 2, GS, P], F32)
        hT = sb("hT", [P, NHB, T], F32)
        hm = sb("h_absmax", [P, T], F32)
        qr = sb("q2_steps", [P, NHB, T], F32)
        q2 = sb("q2", [P, NHB, T], BF16)
        top = sb("row_scales", [P, 6, GS], F32)
        gw = sb("tanh_g_w2_step", [P, 1], F32)
        bankX, bankR, bankH0, bankH1, bankM, bankS, bankY, bankT = (k.bank(i) for i in range(8))
        bankH = [bankH0, bankH1]

        s_prep = sem("prep_step")
        s_wsum = sem("abs_sums_spread")
        s_chain = sem("dve_step")
        s_first = sem("first_quant_step")
        s_quant = sem("xq_ready")
        r_qT = Ring(sem("xqT_in_psum"), 1)
        s_qT = sem("xqT_ready")
        s_srow = sem("q_step_spread")
        s_srs = sem("q_step_rows_ready")
        s_h = sem("h_in_psum")
        r_hs = Ring(sem("h_scaled_ready"), 2)
        s_cv = sem("convolved_ready")
        r_act = Ring(sem("hT_ready"), 2)
        s_hm = sem("h_absmax_ready")
        s_hmT = sem("h_absmaxT_in_psum")
        s_sc = sem("row_scales_ready")
        s_scr = sem("row_scales_spread")
        s_q2 = sem("q2_ready")
        r_y = Ring(sem("y_in_psum"), 1)
        r_out = Ring(sem("x_updated"), 1)

        block = ctx.enter_context(nc.Block())

        @block.tensor
        def _(pe):
            for r in (r_qT, k.r_xnT_used, r_y):
                r.grant(pe)
            k.wait_weights(pe, "l0f")
            pe.wait_ge(s_prep, 1)
            pe.matmul(bankM[:, 0:2], k.ones[:, :], wsum[:, :], start=True, stop=True).then_inc(s_wsum, 1)
            pe.wait_ge(s_prep, 6)

            def turn_q(g):
                pe.wait_ge(s_quant, g + 1)
                for c in range(GS):
                    pe.matmul(bankS[:, seq(c)], bcast(dq[:, c:c + 1], [P, P]), k.ident[:, :], start=True, stop=True)
                for c in range(GS):
                    ins = pe.transpose(bankX.bitcast(BF16)[:, seq(c)], xq[:, c, :], k.ident_bf[:, :])
                ins.then_inc(r_qT.sem, 1)

            turn_q(0)

            def body(g, par, more, chain):
                pe.wait_ge(s_qT, g + 1)
                for n in range(NHB):
                    r_hs.wait_free(pe, g * NHB + n)
                    pe.matmul(bankH[n % 2][:, :], w1q[:, seq(n)], xqT[:, :], start=True, stop=True).then_inc(s_h, 1)
                pe.wait_ge(s_hm, g + 1)
                for c in range(GS):
                    ins = pe.transpose(bankT[:, seq(c)], hm[:, seq(c)], k.ident[:, :])
                ins.then_inc(s_hmT, 1)
                pe.wait_ge(s_sc, g + 1)
                for c in range(GS):
                    ins = pe.matmul(bankR[:, seq(c)], bcast(top[:, 3, c:c + 1], [P, P]), k.ident[:, :],
                                    start=True, stop=True)
                ins.then_inc(s_scr, 1)
                if more:
                    turn_q(g + 1)
                pe.wait_ge(s_q2, g + 1)
                r_out.wait_free(pe, g)
                for c in range(GS):
                    for n in range(NHB):
                        ins = pe.matmul(bankY[:, seq(c)], q2[:, n, seq(c)], w2q[:, n, :], start=(n == 0),
                                        stop=(n == NHB - 1))
                ins.then_inc(r_y.sem, 1)

            groups(pe, body)

        @block.scalar
        def _(act):
            r_act.grant(act)

            def body(g, par, more, chain):
                r_qT.wait_done(act, g)
                act.activation(xqT[:, :], bankX.bitcast(BF16)[:, 0:T], ACT.Copy).then_inc(s_qT, 1)
                act.activation(srow[:, :, :], bankS.rearrange("p (c t) -> p c t", c=GS), ACT.Copy)\
                   .then_inc(s_srs, 1)
                for n in range(NHB):
                    act.wait_ge(s_cv, g * NHB + n + 1)
                    act.activation(hT[:, n, :], cv[:, n % 2, :, :].rearrange("p c t -> p (c t)"), ACT.Silu,
                                   bias=w["l0f_cb"][:, n:n + 1]).then_inc(r_act.sem, 1)

            groups(act, body)

        @block.gpsimd
        def _(pool):
            ln_rstd(k, pool, 0)
            groups(pool, lambda g, par, more, chain: ln_rstd(k, pool, g + 1) if more else None)

        @block.vector
        def _(dve):
            r_hs.grant(dve)
            r_out.grant(dve)
            k.wait_weights(dve, "l0f")
            prep = Chain(dve, s_prep, 0, 0)
            dve.tensor_reduce(wsum[:, 0:1], w["l0f_w1"][:, :], AX, ALU.add, apply_absolute_value=True)
            prep(dve.tensor_reduce(wsum[:, 1:2], w["l0f_w2"][:, :, :].rearrange("p n d -> p (n d)"), AX, ALU.add,
                                   apply_absolute_value=True))
            dve.wait_ge(s_wsum, 1)
            prep(dve.tensor_scalar(wmean[:, :], bankM[:, 0:2], 1.0 / (P * HID), 1e-5, ALU.mult, ALU.max))
            prep(dve.reciprocal(winv[:, :], wmean[:, :]))
            dve.tensor_scalar(wr[:, 0, :], w["l0f_w1"][:, :], winv[:, 0:1], MAGIC, ALU.mult, ALU.add)
            prep(dve.tensor_scalar(wr[:, 1, :], w["l0f_w2"][:, :, :].rearrange("p n d -> p (n d)"), winv[:, 1:2],
                                   MAGIC, ALU.mult, ALU.add))
            prep(dve.tensor_scalar(wr[:, :, :], wr[:, :, :], -MAGIC, 1.0, ALU.add, ALU.min))
            dve.tensor_scalar(w1q[:, :], wr[:, 0, :], -1.0, None, ALU.max)
            dve.tensor_scalar(gw[:, :], k.tanh_g[:, 4:5], wmean[:, 1:2], 1.0 / 127.0, ALU.mult, ALU.mult)
            prep(dve.tensor_scalar(w2q[:, :, :].rearrange("p n d -> p (n d)"), wr[:, 1, :], -1.0, None, ALU.max))

            def quantise(g, chain):
                dve.wait_ge(s_done_xn, g + 1)
                chain(dve.tensor_reduce(amax[:, :], k.xn[:, :, :], AX, ALU.max, apply_absolute_value=True))
                chain(dve.tensor_scalar(amax[:, :], amax[:, :], 1e-5, None, ALU.max))
                chain(dve.reciprocal(qs[:, :], amax[:, :]))
                chain(dve.tensor_scalar(qs[:, :], qs[:, :], 127.0, None, ALU.mult))
                r_qT.wait_free(dve, g)
                dve.tensor_scalar(dq[:, :], amax[:, :], 1.0 / 127.0, wmean[:, 0:1], ALU.mult, ALU.mult)
                for c in range(GS):
                    ins = dve.tensor_scalar(xr[:, c, :], k.xn[:, c, :], qs[:, c:c + 1], MAGIC, ALU.mult, ALU.add)
                chain(ins)
                dve.tensor_scalar(xq[:, :, :], xr[:, :, :], -MAGIC, None, ALU.add).then_inc(s_quant, 1)

            s_done_xn = k.s_xn
            k.r_xnT_psum = r_qT
            ln_stats(k, dve, 0)
            ln_apply(k, dve, 0)
            quantise(0, Chain(dve, s_first, 0, 0))

            def body(g, par, more, chain):
                dve.wait_ge(s_srs, g + 1)
                for n in range(NHB):
                    h, y = hs[:, n % 2, :, :], cv[:, n % 2, :, :]
                    tap = lambda i: w["l0f_cw"][:, 3 * n + i:3 * n + i + 1]
                    dve.wait_ge(s_h, g * NHB + n + 1)
                    ins = dve.tensor_tensor(h, bankH[n % 2].rearrange("p (c t) -> p c t", c=GS), srow[:, :, :],
                                            ALU.mult)
                    ins.then_inc(r_hs.sem, 1)
                    r_hs.wait_done(dve, g * NHB + n)
                    r_act.wait_free(dve, g * NHB + n)
                    chain(dve.tensor_scalar(y, h, tap(1), None, ALU.mult))
                    chain(dve.scalar_tensor_tensor(y[:, :, 1:P], h[:, :, 0:P - 1], tap(0), y[:, :, 1:P],
                                                   ALU.mult, ALU.add))
                    dve.scalar_tensor_tensor(y[:, :, 0:P - 1], h[:, :, 1:P], tap(2), y[:, :, 0:P - 1],
                                             ALU.mult, ALU.add).then_inc(s_cv, 1)
                if more:
                    ln_stats(k, dve, g + 1)
                r_act.wait_done(dve, g * NHB + 3)
                dve.tensor_reduce(hm[:, :], hT[:, :, :].rearrange("p n t -> p t n"), AX, ALU.max,
                                  apply_absolute_value=True).then_inc(s_hm, 1)
                if more:
                    ln_apply(k, dve, g + 1)
                dve.wait_ge(s_hmT, g + 1)
                chain(dve.tensor_reduce(top[:, 0, :], bankT.rearrange("p (c t) -> p c t", c=GS), AX, ALU.max,
                                        apply_absolute_value=True))
                chain(dve.tensor_scalar(top[:, 1, :], top[:, 0, :], 1e-5, None, ALU.max))
                chain(dve.reciprocal(top[:, 2, :], top[:, 1, :]))
                dve.tensor_scalar(top[:, 3, :], top[:, 2, :], 127.0, None, ALU.mult).then_inc(s_sc, 1)
                chain(dve.tensor_scalar(top[:, 4, :], top[:, 1, :], gw[:, 0:1], None, ALU.mult))
                if more:
                    quantise(g + 1, chain)
                dve.wait_ge(s_scr, g + 1)
                rows = bcast(bankR.unsqueeze(1), [P, NHB, T])
                chain(dve.tensor_tensor(qr[:, :, :], hT[:, :, :], rows, ALU.mult))
                chain(dve.tensor_scalar(qr[:, :, :], qr[:, :, :], MAGIC, None, ALU.add))
                r_y.wait_free(dve, g)
                dve.tensor_scalar(q2[:, :, :], qr[:, :, :], -MAGIC, None, ALU.add).then_inc(s_q2, 1)
                r_y.wait_done(dve, g)
                for c in range(GS):
                    xc = k.x_sb[:, bass.ds((g * GS + c) * P, P)]
                    ins = dve.scalar_tensor_tensor(xc, bankY[:, seq(c)], top[:, 4, c:c + 1], xc, ALU.mult, ALU.add)
                ins.then_inc(r_out.sem, 1)

            groups(dve, body, s_chain, (38, 33))


NE1, RANK = 3, 8
NZ = NE1 * RANK
NZL = NZ + NE1
ZW = 32


def layer1_ffn(nc, k):
    with ExitStack() as ctx:
        sb, sem = k.local(ctx, "l1f")
        ln_tensors(k, sb, sem)
        shifted = sb("shifted", [P, GS, NE1], F32)
        expd = sb("expd", [P, GS, NE1], F32)
        small = sb("small", [P, 4, GS], F32)
        gate = sb("gate", [P, GS, NE1], F32)
        zg = sb("zg", [P, GS, ZW], F32)
        zgT = sb("zgT", [P, T], F32)
        hT = sb("hT", [P, NHB, T], F32)
        bankX, bankZ, bankZT, bankH, bankY, bankR = (
            k.bank(0), k.bank(1), k.bank(2), [k.bank(3), k.bank(4)], k.banks(5, 2), k.bank(7))
        zview = bankZ.rearrange("p (c w) -> p c w", c=GS)[:, :, 0:NZL]
        WY = P + NZL
        yview = bankY.rearrange("p (a w) -> p a w", a=2)[:, :, 0:2 * WY].rearrange("p a (b w) -> p a b w", b=2)

        s_const = sem("zg_const_ready")
        s_chain = sem("dve_step")
        s_z = sem("z_in_psum")
        s_shift = sem("logits_shifted")
        s_exp = sem("gates_exp")
        s_zg = sem("zg_ready")
        r_zT = Ring(sem("zgT_in_psum"), 1)
        r_zTs = Ring(sem("zgT_ready"), 1)
        r_lora = Ring(sem("lora_done"), 1)
        s_h = sem("h_in_psum")
        r_h = Ring(sem("h_ready"), 2)
        r_y = Ring(sem("y_in_psum"), 1)
        r_out = Ring(sem("x_updated"), 1)

        block = ctx.enter_context(nc.Block())

        @block.tensor
        def _(pe):
            r_zT.grant(pe)
            r_lora.grant(pe)
            r_y.grant(pe)
            k.r_xnT_psum.grant(pe)
            k.r_xnT_used.grant(pe)
            k.wait_weights(pe, "l1f")
            ln_transpose(k, pe, 0, bankX)

            def turn_zg(unit):
                pe.wait_ge(s_zg, unit + 1)
                r_zTs.wait_free(pe, unit)
                for c in range(GS):
                    ins = pe.transpose(bankZT[0:ZW, seq(c)], zg[:, c, :], k.ident[:, :])
                ins.then_inc(r_zT.sem, 1)

            def body(g, par, more, chain):
                xnT = k.xnT[:, par, :]
                k.r_xnT.wait_done(pe, g)
                for c in range(GS):
                    ins = pe.matmul(zview[:, c, :], xnT[:, seq(c)], k.w["l1f_ar1"][:, :], start=True, stop=True)
                ins.then_inc(s_z, 1)

                def base(n):
                    r_h.wait_free(pe, g * NHB + n)
                    return pe.matmul(bankH[n % 2][:, :], k.w["l1f_w1"][:, seq(n)], xnT, start=True, stop=False)

                def lora(n):
                    return pe.matmul(bankH[n % 2][:, :], k.w["l1f_b1"][:, seq(n)], zgT[:, :],
                                     start=False, stop=True)

                base(0)
                base(1)
                turn_zg(2 * g)
                r_zTs.wait_done(pe, 2 * g)
                lora(0).then_inc(s_h, 1)
                lora(1).then_inc(s_h, 1)
                base(2)
                lora(2).then_inc(s_h, 1)
                base(3).then_inc(k.r_xnT_used.sem, 1)
                ins = lora(3)
                ins.then_inc(s_h, 1)
                if more:
                    ln_transpose(k, pe, g + 1, bankX)
                r_out.wait_free(pe, g)
                r_h.wait_done(pe, g * NHB + NHB - 1)
                for c in range(GS):
                    for n in range(NHB):
                        ins = pe.matmul(yview[:, c // 2, c % 2, :], hT[:, n, seq(c)], k.w["l1f_w2ar"][:, n, :],
                                        start=(n == 0), stop=(n == NHB - 1))
                ins.then_inc(r_y.sem, 1)
                turn_zg(2 * g + 1)
                r_zTs.wait_done(pe, 2 * g + 1)
                for c in range(GS):
                    ins = pe.matmul(bankR[:, seq(c)], zgT[:, seq(c)], k.w["l1f_b2"][:, :], start=True, stop=True)
                ins.then_inc(r_lora.sem, 1)

            groups(pe, body)

        @block.scalar
        def _(act):
            r_zTs.grant(act)
            r_h.grant(act)
            k.r_xnT.grant(act)
            act.wait_ge(s_const, 2)
            ln_evacuate(k, act, 0, 0, bankX)

            def gates(unit):
                act.wait_ge(s_shift, unit + 1)
                act.activation(expd[:, :, :], shifted[:, :, :], ACT.Exp).then_inc(s_exp, 1)
                r_zT.wait_done(act, unit)

            def body(g, par, more, chain):
                gates(2 * g)
                r_lora.wait_free(act, g)
                act.activation(zgT[0:ZW, :], bankZT[0:ZW, :], ACT.Copy).then_inc(r_zTs.sem, 1)
                r_y.wait_free(act, g)
                for n in range(NHB):
                    act.wait_ge(s_h, g * NHB + n + 1)
                    act.activation(hT[:, n, :], bankH[n % 2][:, :], ACT.Relu).then_inc(r_h.sem, 1)
                if more:
                    ln_evacuate(k, act, g + 1, 1 - par, bankX)
                gates(2 * g + 1)
                act.activation(zgT[0:ZW, :], bankZT[0:ZW, :], ACT.Copy).then_inc(r_zTs.sem, 1)

            groups(act, body)

        @block.gpsimd
        def _(pool):
            pool.memset(zgT[:, :], 0.0).then_inc(s_const, 1)
            ln_rstd(k, pool, 0)
            groups(pool, lambda g, par, more, chain: ln_rstd(k, pool, g + 1) if more else None)

        @block.vector
        def _(dve):
            r_out.grant(dve)
            dve.memset(zg[:, :, NZ + 1:ZW], 0.0)
            dve.memset(zg[:, :, NZ:NZ + 1], 1.0).then_inc(s_const, 1)
            ln_stats(k, dve, 0)
            ln_apply(k, dve, 0)

            def gates(unit, chain, logits, zs):
                chain(dve.tensor_reduce(small[:, 0, :], logits, AX, ALU.max))
                mx = small[:, 0, :].rearrange("p (a b) -> p a b", a=logits.shape[1]) if len(logits.shape) == 4 \
                    else small[:, 0, :]
                sh = shifted[:, :, :]
                if len(logits.shape) == 4:
                    sh = shifted[:, :, :].rearrange("p (a b) e -> p a b e", a=2)
                dve.tensor_tensor(sh, logits, bcast(mx.unsqueeze(len(mx.shape)), logits.shape),
                                  ALU.subtract).then_inc(s_shift, 1)
                dve.wait_ge(s_exp, unit + 1)
                chain(dve.tensor_reduce(small[:, 1, :], expd[:, :, :], AX, ALU.add))
                chain(dve.tensor_scalar(small[:, 2, :], small[:, 1, :], float(RANK), None, ALU.mult))
                chain(dve.reciprocal(small[:, 3, :], small[:, 2, :]))
                chain(dve.tensor_tensor(gate[:, :, :], expd[:, :, :],
                                        bcast(small[:, 3, :].unsqueeze(2), [P, GS, NE1]), ALU.mult))
                r_zT.wait_free(dve, unit)
                n = GS // len(zs)
                for a, z in enumerate(zs):
                    part = slice(a * n, a * n + n)
                    ins = dve.tensor_tensor(zg[:, part, 0:NZ].rearrange("p c (e r) -> p c e r", e=NE1), z,
                                            bcast(gate[:, part, :].unsqueeze(3), [P, n, NE1, RANK]), ALU.mult)
                ins.then_inc(s_zg, 1)

            def body(g, par, more, chain):
                dve.wait_ge(s_z, g + 1)
                gates(2 * g, chain, zview[:, :, NZ:NZL],
                      [zview[:, :, 0:NZ].rearrange("p c (e r) -> p c e r", e=NE1)])
                if more:
                    ln_stats(k, dve, g + 1)
                    ln_apply(k, dve, g + 1)
                r_y.wait_done(dve, g)
                gates(2 * g + 1, chain, yview[:, :, :, P + NZ:WY],
                      [yview[:, a, :, P:P + NZ].rearrange("p c (e r) -> p c e r", e=NE1) for a in range(2)])
                for a in range(2):
                    xs = k.x_sb[:, bass.ds((g * GS + 2 * a) * P, 2 * P)].rearrange("p (c d) -> p c d", c=2)
                    ins = dve.scalar_tensor_tensor(xs, yview[:, a, :, 0:P], k.tanh_g[:, 5:6], xs, ALU.mult, ALU.add)
                chain(ins)
                r_lora.wait_done(dve, g)
                xs = k.x_sb[:, bass.ds(g * T, T)]
                dve.scalar_tensor_tensor(xs, bankR[:, :], k.tanh_g[:, 5:6], xs, ALU.mult, ALU.add)\
                   .then_inc(r_out.sem, 1)

            groups(dve, body, s_chain, 22)


def layer2_attention(nc, k):
    with ExitStack() as ctx:
        sb, sem = k.local(ctx, "l2x")
        ln_tensors(k, sb, sem)
        ctxT = sb("ctxT", [P, 2, T], F32)
        ctok = sb("ctx_tok", [P, 2, T], F32)
        hwT = sb("h_w3_plus_w2_T", [P, T], F32)
        nmax = sb("minus_max", [P, GS], F32)
        total = sb("total", [P, GS], F32)
        rtot = sb("rtot", [P, GS], F32)
        probs = sb("probs", [P, GS, P], F32)
        attn = sb("attn", [P, GS, P], F32)
        attnT = sb("attnT", [P, T], F32)
        pool_max = sb("row_max", [P, GS], F32)
        pool_nmax = sb("pool_minus_max", [P, GS], F32)
        pool_exp = sb("pool_exp", [P, GS, P], F32)
        pool_tot = sb("pool_total", [P, GS], F32)
        pool_rtot = sb("pool_rtot", [P, GS], F32)
        weighed = sb("weighed", [P, GS, P], F32)
        hsum = sb("h_sum", [P, GS], F32)
        hbar = sb("h_bar", [P, GS], F32)
        aT = sb("aT", [P, T], F32)
        haT = sb("h_times_aT", [P, T], F32)
        hhT = sb("h_times_hbarT", [P, GS, P], F32)
        gb = sb("tanh_g_b", [P, GS, P], F32)
        bankX, bankS, bankE, bankAT, bankA, bankR, bankO = (k.bank(i) for i in range(7))
        w = k.w

        s_chain = sem("dve_step")
        s_gb = sem("bias_ready")
        r_ctx = Ring(sem("ctx_used"), 2)
        s_ctx = [sem(f"ctx_in_{p}") for p in range(2)]
        r_hw = Ring(sem("hwT_ready"), 1)
        r_s = Ring(sem("sim_in_psum"), 1)
        s_nmax = sem("minus_max_ready")
        s_p = sem("probs_ready")
        s_attn = sem("attn_ready")
        r_at = Ring(sem("attnT_in_psum"), 1)
        s_at = sem("attnT_ready")
        s_rmax = sem("row_max_ready")
        s_r = sem("row_max_spread")
        s_pn = sem("pool_minus_max_ready")
        s_pe = sem("pool_exp_ready")
        s_a = sem("aT_in_psum")
        s_aT = sem("aT_ready")
        s_haT = sem("haT_ready")
        s_feat = sem("feats_ready")
        r_o = Ring(sem("out_in_psum"), 1)
        r_out = Ring(sem("x_updated"), 1)

        block = ctx.enter_context(nc.Block())

        @block.sync
        def _(sp):
            with sp.Fori(0, NG // 2) as it:
                for par in range(2):
                    g = 2 * it + par
                    r_ctx.wait_free(sp, g)
                    for buf, src in ((ctxT, "ctxT"), (ctok, "ctx_tok")):
                        sp.dma_start(buf[:, par, :], k.dram[src][:, bass.ds(g * T, T)]).then_inc(s_ctx[par], 16)

        @block.tensor
        def _(pe):
            for r in (k.r_xnT_psum, k.r_xnT_used, r_ctx, r_s, r_at, r_o):
                r.grant(pe)
            k.wait_weights(pe, "l2x")
            ln_transpose(k, pe, 0, bankX)

            def body(g, par, more, chain):
                xnT, cT = k.xnT[:, par, :], ctxT[:, par, :]
                pe.wait_ge(s_ctx[par], (g - par) * 16 + 32)
                r_hw.wait_done(pe, g)
                r_out.wait_free(pe, g)
                for c in range(GS):
                    pe.matmul(bankE[:, c:c + 1], xnT[:, seq(c)], w["l2x_w1"][:, :], start=True, stop=True)
                for c in range(GS):
                    ins = pe.matmul(bankS[:, seq(c)], hwT[:, seq(c)], cT[:, seq(c)], start=True, stop=True)
                ins.then_inc(r_s.sem, 1)
                pe.wait_ge(s_rmax, g + 1)
                for c in range(GS):
                    ins = pe.matmul(bankR[:, seq(c)], bcast(pool_max[:, c:c + 1], [P, P]), k.ident[:, :],
                                    start=True, stop=True)
                ins.then_inc(s_r, 1)
                if more:
                    ln_transpose(k, pe, g + 1, bankX)
                pe.wait_ge(s_attn, g + 1)
                for c in range(GS):
                    ins = pe.transpose(bankAT[:, seq(c)], attn[:, c, :], k.ident[:, :])
                ins.then_inc(r_at.sem, 1)
                pe.wait_ge(s_at, g + 1)
                for c in range(GS):
                    ins = pe.matmul(bankA[:, seq(c)], ctok[:, par, seq(c)], attnT[:, seq(c)], start=True, stop=True)
                ins.then_inc(s_a, 1)
                pe.wait_ge(s_aT, g + 1)
                pe.wait_ge(s_feat, g + 1)
                for c in range(GS):
                    for n, f in enumerate((xnT[:, seq(c)], aT[:, seq(c)], haT[:, seq(c)], hhT[:, c, :])):
                        ins = pe.matmul(bankO[:, seq(c)], f, w["l2x_wqv"][:, n, :], start=(n == 0), stop=(n == 3))
                ins.then_inc(r_o.sem, 1)
                r_o.wait_done(pe, g)
                pe.sem_inc(r_ctx.sem, 1)
                pe.sem_inc(k.r_xnT_used.sem, 1)

            groups(pe, body)

        @block.scalar
        def _(act):
            for r in (k.r_xnT,):
                r.grant(act)
            ln_evacuate(k, act, 0, 0, bankX)

            def body(g, par, more, chain):
                act.wait_ge(s_nmax, g + 1)
                for c in range(GS):
                    ins = act.activation(probs[:, c, :], bankS[:, seq(c)], ACT.Exp, bias=nmax[:, c:c + 1],
                                         accum_out=total[:, c:c + 1])
                ins.then_inc(s_p, 1)
                act.wait_ge(s_pn, g + 1)
                for c in range(GS):
                    ins = act.activation(pool_exp[:, c, :], bankR[:, seq(c)], ACT.Exp,
                                         bias=pool_nmax[:, c:c + 1], accum_out=pool_tot[:, c:c + 1])
                ins.then_inc(s_pe, 1)
                if more:
                    ln_evacuate(k, act, g + 1, 1 - par, bankX)
                r_at.wait_done(act, g)
                act.activation(attnT[:, :], bankAT[:, :], ACT.Copy).then_inc(s_at, 1)
                act.wait_ge(s_haT, g + 1)
                r_o.wait_free(act, g)
                act.activation(aT[:, :], bankA[:, :], ACT.Copy).then_inc(s_aT, 1)

            groups(act, body)

        @block.gpsimd
        def _(pool):
            ln_rstd(k, pool, 0)
            groups(pool, lambda g, par, more, chain: ln_rstd(k, pool, g + 1) if more else None)

        @block.vector
        def _(dve):
            r_hw.grant(dve)
            r_out.grant(dve)
            k.wait_weights(dve, "l2x")
            for c in range(GS):
                ins = dve.tensor_scalar(gb[:, c, :], w["l2x_bqv"][:, :], k.tanh_g[:, 2:3], None, ALU.mult)
            ins.then_inc(s_gb, 1)
            dve.wait_ge(s_gb, 1)
            ln_stats(k, dve, 0)
            ln_apply(k, dve, 0)

            def body(g, par, more, chain):
                xnT = k.xnT[:, par, :]
                xnT3 = xnT.rearrange("p (c t) -> p c t", c=GS)
                k.r_xnT.wait_done(dve, g)
                r_s.wait_free(dve, g)
                dve.tensor_scalar(hwT[:, :], xnT, w["l2x_w3"][:, :], w["l2x_w2"][:, :], ALU.mult, ALU.add)\
                   .then_inc(r_hw.sem, 1)
                r_s.wait_done(dve, g)
                dve.tensor_reduce(nmax[:, :], bankS.rearrange("p (c t) -> p c t", c=GS), AX, ALU.max,
                                  negate=True).then_inc(s_nmax, 1)
                dve.wait_ge(s_nmax, g + 1)
                dve.scalar_tensor_tensor(pool_max[:, :], bankE[:, 0:GS], w["l2x_bsim"][:, 0:1], nmax[:, :],
                                         ALU.add, ALU.subtract).then_inc(s_rmax, 1)
                if more:
                    ln_stats(k, dve, g + 1)
                dve.wait_ge(s_p, g + 1)
                chain(dve.reciprocal(rtot[:, :], total[:, :]))
                dve.tensor_tensor(attn[:, :, :], probs[:, :, :], bcast(rtot[:, :].unsqueeze(2), [P, GS, P]),
                                  ALU.mult).then_inc(s_attn, 1)
                dve.wait_ge(s_r, g + 1)
                dve.tensor_reduce(pool_nmax[:, :], bankR.rearrange("p (c t) -> p c t", c=GS), AX, ALU.max,
                                  negate=True).then_inc(s_pn, 1)
                if more:
                    ln_apply(k, dve, g + 1)
                xs = k.x_sb[:, bass.ds(g * T, T)]
                dve.tensor_tensor(xs, xs, gb[:, :, :].rearrange("p c d -> p (c d)"), ALU.add)
                dve.wait_ge(s_pe, g + 1)
                chain(dve.tensor_tensor(weighed[:, :, :], xnT3, pool_exp[:, :, :], ALU.mult))
                dve.tensor_reduce(hsum[:, :], weighed[:, :, :], AX, ALU.add)
                chain(dve.reciprocal(pool_rtot[:, :], pool_tot[:, :]))
                chain(dve.tensor_tensor(hbar[:, :], hsum[:, :], pool_rtot[:, :], ALU.mult))
                r_o.wait_free(dve, g)
                dve.tensor_tensor(hhT[:, :, :], xnT3, bcast(hbar[:, :].unsqueeze(2), [P, GS, P]), ALU.mult)\
                   .then_inc(s_feat, 1)
                dve.wait_ge(s_a, g + 1)
                dve.tensor_tensor(haT[:, :], bankA[:, :], xnT, ALU.mult).then_inc(s_haT, 1)
                r_o.wait_done(dve, g)
                dve.scalar_tensor_tensor(xs, bankO[:, :], k.tanh_g[:, 2:3], xs, ALU.mult, ALU.add)\
                   .then_inc(r_out.sem, 1)

            groups(dve, body, s_chain, 8)


NE2 = 8


def layer2_ffn(nc, k):
    with ExitStack() as ctx:
        sb, sem = k.local(ctx, "l2f")
        ln_tensors(k, sb, sem)
        w = k.w
        lg = sb("logits", [P, GS, NE2], F32)
        sh = sb("logits_shifted", [P, GS, NE2], F32)
        ex = sb("gate_exp", [P, GS, NE2], F32)
        ta = sb("select_a", [P, GS, NE2], F32)
        tb = sb("select_b", [P, GS, NE2], F32)
        top = sb("tops", [P, 6, GS], F32)
        gate = sb("gates", [P, 2, GS, NE2], F32)
        gateT = sb("gatesT", [NE2, T], F32)
        hT = sb("hT", [P, 2, NHB, T], F32)
        acc = sb("acc", [P, GS, P], F32)
        bankX, bankM, bankB = k.bank(0), k.bank(1), k.bank(2)
        bankH, bankY = [k.bank(3), k.bank(4)], [k.bank(5), k.bank(6)]

        s_chain = sem("dve_step")
        s_first = sem("first_gates_step")
        s_gates = sem("logits_in_psum")
        s_shift = sem("logits_shifted_ready")
        s_ex = sem("gate_exp_ready")
        s_gate = sem("gates_ready")
        s_gT = sem("gatesT_in_psum")
        r_gT = Ring(sem("gatesT_ready"), 1)
        r_b = Ring(sem("bias_in_psum"), 1)
        s_h = sem("h_in_psum")
        r_h = Ring(sem("hT_ready"), 2)
        r_y = Ring(sem("y_in_psum"), 2)
        r_acc = Ring(sem("y_added"), 2)
        s_acc0 = sem("bias_taken")

        block = ctx.enter_context(nc.Block())

        @block.tensor
        def _(pe):
            for r in (k.r_xnT_psum, k.r_xnT_used, r_b, r_y):
                r.grant(pe)
            k.wait_weights(pe, "l2f")
            ln_transpose(k, pe, 0, bankX)

            def gates(g, par):
                k.r_xnT.wait_done(pe, g)
                for c in range(GS):
                    ins = pe.matmul(bankM[:, c * NE2:(c + 1) * NE2], k.xnT[:, par, seq(c)], w["l2f_router"][:, :],
                                    start=True, stop=True)
                ins.then_inc(s_gates, 1)

            def bias(g, par):
                pe.wait_ge(s_gate, g + 1)
                r_gT.wait_free(pe, g)
                for c in range(GS):
                    ins = pe.transpose(bankB[0:NE2, seq(c)], gate[:, par, c, :], k.ident[:, :])
                ins.then_inc(s_gT, 1)
                r_gT.wait_done(pe, g)
                for c in range(GS):
                    ins = pe.matmul(bankB[:, seq(c)], gateT[:, seq(c)], w["l2f_b2"][:, :], start=True, stop=True)
                ins.then_inc(r_b.sem, 1)

            gates(0, 0)

            def body(g, par, more, chain):
                xnT = k.xnT[:, par, :]

                def up(e):
                    for n in range(NHB):
                        unit = (g * NE2 + e) * NHB + n
                        r_h.wait_free(pe, unit)
                        ins = pe.matmul(bankH[n % 2][:, :], w["l2f_w1"][:, e, seq(n)], xnT, start=True, stop=True)
                        ins.then_inc(s_h, 1)

                def down(e):
                    unit = g * NE2 + e
                    r_h.wait_done(pe, (unit + 1) * NHB - 1)
                    r_acc.wait_free(pe, unit)
                    for c in range(GS):
                        for n in range(NHB):
                            ins = pe.matmul(bankY[e % 2][:, seq(c)], hT[:, e % 2, n, seq(c)], w["l2f_w2"][:, e, n, :],
                                            start=(n == 0), stop=(n == NHB - 1))
                    ins.then_inc(r_y.sem, 1)

                up(0)
                up(1)
                bias(g, par)
                down(0)
                for e in range(2, NE2):
                    up(e)
                    down(e - 1)
                    if e == 3 and more:
                        ln_transpose(k, pe, g + 1, bankX)
                    if e == 5 and more:
                        gates(g + 1, 1 - par)
                down(NE2 - 1)
                pe.sem_inc(k.r_xnT_used.sem, 1)

            groups(pe, body)

        @block.scalar
        def _(act):
            for r in (k.r_xnT, r_gT, r_h):
                r.grant(act)
            ln_evacuate(k, act, 0, 0, bankX)

            def gates(g):
                act.wait_ge(s_shift, g + 1)
                act.activation(ex[:, :, :], sh[:, :, :], ACT.Exp).then_inc(s_ex, 1)

            gates(0)

            def body(g, par, more, chain):
                for e in range(NE2):
                    r_y.wait_free(act, g * NE2 + e)
                    for n in range(NHB):
                        unit = (g * NE2 + e) * NHB + n
                        act.wait_ge(s_h, unit + 1)
                        act.activation(hT[:, e % 2, n, :], bankH[n % 2][:, :], ACT.Relu,
                                       bias=w["l2f_b1"][:, e * NHB + n:e * NHB + n + 1]).then_inc(r_h.sem, 1)
                    if e == 1:
                        act.wait_ge(s_gT, g + 1)
                        r_b.wait_free(act, g)
                        act.activation(gateT[:, :], bankB[0:NE2, :], ACT.Copy).then_inc(r_gT.sem, 1)
                    if e == 3 and more:
                        ln_evacuate(k, act, g + 1, 1 - par, bankX)
                    if e == 5 and more:
                        gates(g + 1)

            groups(act, body)

        @block.gpsimd
        def _(pool):
            ln_rstd(k, pool, 0)
            groups(pool, lambda g, par, more, chain: ln_rstd(k, pool, g + 1) if more else None)

        @block.vector
        def _(dve):
            r_acc.grant(dve)
            k.wait_weights(dve, "l2f")
            ln_stats(k, dve, 0)
            ln_apply(k, dve, 0)

            def both(ap):
                return bcast(ap.unsqueeze(2), [P, GS, NE2])

            def gates(g, par, chain):
                dve.wait_ge(s_gates, g + 1)
                raw = bankM[:, 0:GS * NE2].rearrange("p (c e) -> p c e", c=GS)
                chain(dve.tensor_tensor(lg[:, :, :], raw, bcast(w["l2f_router_b"][:, :].unsqueeze(1), [P, GS, NE2]),
                                        ALU.add))
                chain(dve.tensor_reduce(top[:, 0, :], lg[:, :, :], AX, ALU.max))
                dve.tensor_tensor(sh[:, :, :], lg[:, :, :], both(top[:, 0, :]), ALU.subtract).then_inc(s_shift, 1)
                dve.wait_ge(s_ex, g + 1)
                dve.tensor_reduce(top[:, 1, :], ex[:, :, :], AX, ALU.add)
                chain(dve.tensor_reduce(top[:, 2, :], ex[:, :, :], AX, ALU.max))
                chain(dve.reciprocal(top[:, 3, :], top[:, 1, :]))
                chain(dve.tensor_tensor(ta[:, :, :], ex[:, :, :], both(top[:, 2, :]), ALU.is_equal))
                chain(dve.tensor_tensor(ta[:, :, :], ta[:, :, :], k.descending[:, :, NE3 - NE2:NE3], ALU.mult))
                chain(dve.tensor_reduce(top[:, 4, :], ta[:, :, :], AX, ALU.max))
                chain(dve.tensor_tensor(tb[:, :, :], ta[:, :, :], both(top[:, 4, :]), ALU.is_equal))
                chain(dve.tensor_tensor(tb[:, :, :], tb[:, :, :], ex[:, :, :], ALU.mult))
                dve.tensor_tensor(gate[:, par, :, :], tb[:, :, :], both(top[:, 3, :]), ALU.mult)\
                   .then_inc(s_gate, 1)

            gates(0, 0, Chain(dve, s_first, 0, 0))

            def body(g, par, more, chain):
                r_b.wait_done(dve, g)
                chain(dve.tensor_copy(acc[:, :, :], bankB.rearrange("p (c d) -> p c d", c=GS)))
                for e in range(NE2):
                    r_y.wait_done(dve, g * NE2 + e)
                    for c in range(GS):
                        ins = dve.scalar_tensor_tensor(acc[:, c, :], bankY[e % 2][:, seq(c)],
                                                       gate[:, par, c, e:e + 1], acc[:, c, :], ALU.mult, ALU.add)
                    ins.then_inc(r_acc.sem, 1)
                    r_acc.wait_done(dve, g * NE2 + e)
                    if e == 1 and more:
                        ln_stats(k, dve, g + 1)
                        ln_apply(k, dve, g + 1)
                    if e == 4 and more:
                        gates(g + 1, 1 - par, chain)
                xs = k.x_sb[:, bass.ds(g * T, T)]
                chain(dve.scalar_tensor_tensor(xs, acc[:, :, :].rearrange("p c d -> p (c d)"), k.tanh_g[:, 6:7], xs,
                                               ALU.mult, ALU.add))

            groups(dve, body, s_chain, (22, 13))


def layer3_attention(nc, k):
    with ExitStack() as ctx:
        sb, sem = k.local(ctx, "l3x")
        ln_tensors(k, sb, sem)
        amax = sb("amax", [P, 3], F32)
        amax_all = sb("amax_all", [P, 3], F32)
        step = sb("step", [P, 3], F32)
        inv = sb("inv", [P, 3], F32)
        wr = sb("w_rounded", [P, 3, P], F32)
        wi = sb("w_steps", [P, 3, P], F32)
        gbv = sb("tanh_g_bv", [P, GS, P], F32)
        ctxT = sb("ctxT", [P, 2, T], F32)
        qT = sb("qT", [P, T], F32)
        kT = sb("kT", [P, T], F32)
        v = sb("v", [P, GS, P], F32)
        nmax = sb("nmax", [P, GS], F32)
        nmax_s = sb("nmax_scaled", [P, GS], F32)
        probs = sb("probs", [P, GS, P], F32)
        probsT = sb("probsT", [P, T], F32)
        total = sb("total", [P, GS], F32)
        rtot = sb("rtot", [P, GS], F32)
        rg = sb("rtot_tanh_g", [P, GS], F32)
        bankX, bankQ, bankK, bankV, bankS, bankPT, bankO, bankM = (k.bank(i) for i in range(8))
        scale = float(P) ** -0.5

        s_prep = sem("weights_step")
        s_all = sem("absmax_everywhere")
        s_amT = sem("absmax_turned")
        s_wr = sem("w_rounded_ready")
        s_chain = sem("dve_step")
        r_ctx = Ring(sem("ctxT_used"), 2)
        s_ctx = [sem(f"ctxT_in_{p}") for p in range(2)]
        s_q, s_kk, s_v = sem("q_in_psum"), sem("k_in_psum"), sem("v_in_psum")
        r_proj = Ring(sem("qkv_ready"), 1)
        r_s = Ring(sem("scores_in_psum"), 1)
        s_nmax = sem("minus_max_ready")
        r_p = Ring(sem("probs_ready"), 1)
        r_pt = Ring(sem("probsT_in_psum"), 1)
        r_pts = Ring(sem("probsT_ready"), 1)
        r_o = Ring(sem("out_in_psum"), 1)
        r_out = Ring(sem("x_updated"), 1)
        r_xb = Ring(sem("x_plus_bias"), 1)

        block = ctx.enter_context(nc.Block())

        @block.sync
        def _(sp):
            with sp.Fori(0, NG // 2) as it:
                for par in range(2):
                    g = 2 * it + par
                    r_ctx.wait_free(sp, g)
                    sp.dma_start(ctxT[:, par, :], k.dram["ctxT"][:, bass.ds(g * T, T)]).then_inc(s_ctx[par], 16)

        @block.tensor
        def _(pe):
            for r in (k.r_xnT_psum, k.r_xnT_used, r_ctx, r_s, r_pt, r_o):
                r.grant(pe)
            k.wait_weights(pe, "l3x")
            pe.wait_ge(s_prep, 1)
            pe.transpose(bankM[0:3, 0:P], amax[:, :], k.ident[:, :]).then_inc(s_amT, 1)
            pe.wait_ge(s_prep, 3)
            pe.matmul(bankM[:, P:P + 3], k.ones[0:3, :], wr[0:3, 0, 0:3], start=True, stop=True).then_inc(s_all, 1)
            ln_transpose(k, pe, 0, bankX)
            pe.wait_ge(s_wr, 1)

            def body(g, par, more, chain):
                xnT, cT = k.xnT[:, par, :], ctxT[:, par, :]
                pe.wait_ge(s_ctx[par], (g - par) * 8 + 16)
                r_proj.wait_free(pe, g)
                pe.matmul(bankK[:, :], wr[:, 1, :], cT, start=True, stop=True).then_inc(s_kk, 1)
                k.r_xnT.wait_done(pe, g)
                pe.matmul(bankQ[:, :], wr[:, 0, :], xnT, start=True, stop=True).then_inc(s_q, 1)
                for c in range(GS):
                    ins = pe.matmul(bankV[:, seq(c)], cT[:, seq(c)], wr[:, 2, :], start=True, stop=True)
                ins.then_inc(s_v, 1)
                pe.wait_ge(s_v, g + 1)
                pe.sem_inc(r_ctx.sem, 1)
                pe.sem_inc(k.r_xnT_used.sem, 1)
                r_proj.wait_done(pe, g)
                r_p.wait_free(pe, g)
                for c in range(GS):
                    ins = pe.matmul(bankS[:, seq(c)], qT[:, seq(c)], kT[:, seq(c)], start=True, stop=True)
                ins.then_inc(r_s.sem, 1)
                if more:
                    ln_transpose(k, pe, g + 1, bankX)
                r_p.wait_done(pe, g)
                r_pts.wait_free(pe, g)
                for c in range(GS):
                    ins = pe.transpose(bankPT[:, seq(c)], probs[:, c, :], k.ident[:, :])
                ins.then_inc(r_pt.sem, 1)
                r_pts.wait_done(pe, g)
                r_out.wait_free(pe, g)
                for c in range(GS):
                    ins = pe.matmul(bankO[:, seq(c)], probsT[:, seq(c)], v[:, c, :], start=True, stop=True)
                ins.then_inc(r_o.sem, 1)

            groups(pe, body)

        @block.scalar
        def _(act):
            for r in (k.r_xnT, r_proj, r_p, r_pts):
                r.grant(act)
            ln_evacuate(k, act, 0, 0, bankX)

            def body(g, par, more, chain):
                r_s.wait_free(act, g)
                act.wait_ge(s_kk, g + 1)
                act.activation(kT[:, :], bankK[:, :], ACT.Identity, bias=k.w["l3x_bk"][:, :])
                act.wait_ge(s_q, g + 1)
                act.activation(qT[:, :], bankQ[:, :], ACT.Identity, bias=k.w["l3x_bq"][:, :])
                act.wait_ge(s_v, g + 1)
                r_o.wait_free(act, g)
                act.activation(v[:, :, :], bankV.rearrange("p (c d) -> p c d", c=GS), ACT.Copy)\
                   .then_inc(r_proj.sem, 1)
                if more:
                    ln_evacuate(k, act, g + 1, 1 - par, bankX)
                act.wait_ge(s_nmax, g + 1)
                r_pt.wait_free(act, g)
                for c in range(GS):
                    ins = act.activation(probs[:, c, :], bankS[:, seq(c)], ACT.Exp, bias=nmax_s[:, c:c + 1],
                                         scale=scale, accum_out=total[:, c:c + 1])
                ins.then_inc(r_p.sem, 1)
                r_pt.wait_done(act, g)
                r_o.wait_free(act, g)
                act.activation(probsT[:, :], bankPT[:, :], ACT.Copy).then_inc(r_pts.sem, 1)

            groups(act, body)

        @block.gpsimd
        def _(pool):
            ln_rstd(k, pool, 0)
            groups(pool, lambda g, par, more, chain: ln_rstd(k, pool, g + 1) if more else None)

        @block.vector
        def _(dve):
            r_out.grant(dve)
            k.wait_weights(dve, "l3x")
            prep = Chain(dve, s_prep, 0, 0)
            for i, n in enumerate(("l3x_wq", "l3x_wk", "l3x_wv")):
                ins = dve.tensor_reduce(amax[:, i:i + 1], k.w[n][:, :], AX, ALU.max, apply_absolute_value=True)
            prep(ins)
            ln_stats(k, dve, 0)
            dve.wait_ge(s_amT, 1)
            prep(dve.tensor_reduce(amax_all[0:3, 0:1], bankM[0:3, 0:P], AX, ALU.max))
            prep(dve.tensor_scalar(wr[0:3, 0, 0:3], k.ident[0:3, 0:3], amax_all[0:3, 0:1], None, ALU.mult))
            dve.wait_ge(s_all, 1)
            prep(dve.tensor_scalar(step[:, :], bankM[:, P:P + 3], 2.0 / 256.0, None, ALU.mult))
            prep(dve.reciprocal(inv[:, :], step[:, :]))
            for i, n in enumerate(("l3x_wq", "l3x_wk", "l3x_wv")):
                prep(dve.tensor_scalar(wi[:, i, :], k.w[n][:, :], inv[:, i:i + 1], MAGIC, ALU.mult, ALU.add))
                ins = dve.tensor_scalar(wr[:, i, :], wi[:, i, :], -MAGIC, step[:, i:i + 1], ALU.add, ALU.mult)
            ins.then_inc(s_wr, 1)
            for c in range(GS):
                ins = dve.tensor_scalar(gbv[:, c, :], k.w["l3x_bv"][:, :], k.tanh_g[:, 3:4], None, ALU.mult)
            prep(ins)
            ln_apply(k, dve, 0)

            def body(g, par, more, chain):
                if more:
                    ln_stats(k, dve, g + 1)
                r_s.wait_done(dve, g)
                chain(dve.tensor_reduce(nmax[:, :], bankS.rearrange("p (c w) -> p c w", c=GS), AX, ALU.max,
                                        negate=True))
                dve.tensor_scalar(nmax_s[:, :], nmax[:, :], scale, None, ALU.mult).then_inc(s_nmax, 1)
                if more:
                    ln_apply(k, dve, g + 1)
                xs = k.x_sb[:, bass.ds(g * T, T)]
                dve.tensor_tensor(xs, xs, gbv[:, :, :].rearrange("p c d -> p (c d)"), ALU.add)
                r_p.wait_done(dve, g)
                chain(dve.reciprocal(rtot[:, :], total[:, :]))
                chain(dve.tensor_scalar(rg[:, :], rtot[:, :], k.tanh_g[:, 3:4], None, ALU.mult))
                r_o.wait_done(dve, g)
                for c in range(GS):
                    xc = k.x_sb[:, bass.ds((g * GS + c) * P, P)]
                    ins = dve.scalar_tensor_tensor(xc, bankO[:, seq(c)], rg[:, c:c + 1], xc, ALU.mult, ALU.add)
                ins.then_inc(r_out.sem, 1)

            groups(dve, body, s_chain, 6)


NE3 = 16


def layer3_ffn(nc, k):
    with ExitStack() as ctx:
        sb, sem = k.local(ctx, "l3f")
        ln_tensors(k, sb, sem)
        w = k.w
        sq = sb("sim_squared", [P, NE3], F32)
        cnorm = sb("column_norm", [P, NE3], F32)
        cinv = sb("column_rnorm", [P, NE3], F32)
        sn = sb("sim_normed", [P, NE3], F32)
        sig = sb("sigmoid_gates", [P, NE3], F32)
        sig_e = sb("exp_minus_gates", [P, NE3], F32)
        xsq = sb("xn_squared", [P, GS, P], F32)
        ssum = sb("xn_sum_squares", [P, GS], F32)
        rnorm = sb("xn_rnorm", [P, GS], F32)
        lg = sb("logits", [P, GS, NE3], F32)
        gated = sb("gated", [P, GS, NE3], F32)
        hard = sb("hard", [P, GS, NE3], F32)
        ta = sb("select_a", [P, GS, NE3], F32)
        tb = sb("select_b", [P, GS, NE3], F32)
        tc = sb("select_c", [P, GS, NE3], F32)
        top = sb("tops", [P, 8, GS], F32)
        ex = sb("gate_exp", [P, GS, NE3], F32)
        w3 = sb("w_parts", [P, GS, P], BF16)
        wr1 = sb("w_rest1", [P, GS, NE3], F32)
        wT = sb("w_partsT", [P, 2, T], BF16)
        xe = sb("weighted_T", [P, 2, T], F32)
        qT, kT, vT, oT = (sb(n, [P, T], F32) for n in ("qT", "kT", "vT", "oT"))
        v = sb("v", [P, GS, P], F32)
        nmax = sb("minus_max", [P, GS], F32)
        probs = sb("probs", [P, GS, P], F32)
        probsT = sb("probsT", [P, T], F32)
        attn = sb("attn", [P, GS, P], F32)
        total = sb("total", [P, GS], F32)
        rtot = sb("rtot", [P, GS], F32)
        yT = sb("yT", [P, T], F32)
        bankW = [k.bank(0), k.bank(1)]
        bankQ, bankK, bankV, bankX, bankS, bankM = (k.bank(i) for i in range(2, 8))
        scale = float(P) ** -0.5

        s_prep = sem("prep_step")
        s_csum = sem("column_sums")
        s_cpow = sem("column_rnorm_ready")
        s_sige = sem("exp_minus_gates_ready")
        s_chain = sem("dve_step")
        s_gates = sem("logits_in_psum")
        s_ss = sem("sum_squares_ready")
        s_rn0 = sem("sum_squares_clamped")
        s_rn = sem("xn_rnorm_ready")
        s_gx = sem("gated_shifted")
        s_ex = sem("gate_exp_ready")
        s_w3 = sem("w_parts_ready")
        s_wTp = sem("w_partsT_in_psum")
        r_wT = Ring(sem("w_partsT_ready"), 1)
        r_wTu = Ring(sem("w_partsT_used"), 2)
        s_we = sem("w_e_spread")
        r_xe = Ring(sem("weighted_ready"), 2)
        r_xu = Ring(sem("weighted_used"), 2)
        s_qkv = sem("qkv_in_psum")
        r_qkv = Ring(sem("qkv_ready"), 1)
        s_vt = sem("v_turned")
        r_v = Ring(sem("v_ready"), 1)
        s_s = sem("scores_in_psum")
        s_nmax = sem("minus_max_ready")
        s_p = sem("probs_ready")
        s_attn = sem("attn_ready")
        s_pt = sem("probsT_in_psum")
        s_pts = sem("probsT_ready")
        s_o = sem("oT_in_psum")
        s_oT = sem("oT_ready")
        s_y = sem("yT_in_psum")
        s_yT = sem("yT_ready")
        s_yt = sem("y_in_psum")
        r_out = Ring(sem("x_updated"), 1)

        block = ctx.enter_context(nc.Block())

        @block.tensor
        def _(pe):
            for r in (k.r_xnT_psum, k.r_xnT_used, r_wTu, r_xu):
                r.grant(pe)
            k.wait_weights(pe, "l3f")
            pe.wait_ge(s_prep, 1)
            pe.matmul(bankM[:, 0:NE3], k.ones[:, :], sq[:, :], start=True, stop=True).then_inc(s_csum, 1)
            ln_transpose(k, pe, 0, bankX)
            pe.wait_ge(s_prep, 3)

            def gates(g, par):
                k.r_xnT.wait_done(pe, g)
                for c in range(GS):
                    ins = pe.matmul(bankM[:, c * NE3:(c + 1) * NE3], k.xnT[:, par, seq(c)], sn[:, :],
                                    start=True, stop=True)
                ins.then_inc(s_gates, 1)
                pe.wait_ge(s_w3, g + 1)
                for c in range(GS):
                    ins = pe.transpose(bankM[:, 256:512].bitcast(BF16)[:, seq(c)], w3[:, c, :], k.ident_bf[:, :])
                ins.then_inc(s_wTp, 1)

            def mixture(g, par, half, operands, banks):
                first = (2 * g + half) * NE3

                def spread(e):
                    r_xe.wait_free(pe, first + e)
                    pe.matmul(bankW[e % 2][:, :], k.select[:, e, :], wT[:, par, :], start=True, stop=True)\
                      .then_inc(s_we, 1)

                spread(0)
                for e in range(NE3):
                    if e + 1 < NE3:
                        spread(e + 1)
                    r_xe.wait_done(pe, first + e)
                    for name, bank in zip(operands, banks):
                        ins = pe.matmul(bank[:, :], w[name][:, e, :], xe[:, e % 2, :],
                                        start=(e == 0), stop=(e == NE3 - 1))
                    ins.then_inc(r_xu.sem, 1)
                return ins

            gates(0, 0)

            def body(g, par, more, chain):
                r_wT.wait_done(pe, g)
                r_out.wait_free(pe, g)
                mixture(g, par, 0, ("l3f_q", "l3f_k", "l3f_v"), (bankQ, bankK, bankV))
                r_xu.wait_done(pe, (2 * g + 1) * NE3 - 1)
                pe.sem_inc(s_qkv, 1)
                pe.sem_inc(k.r_xnT_used.sem, 1)
                if more:
                    ln_transpose(k, pe, g + 1, bankX)
                r_qkv.wait_done(pe, g)
                for c in range(GS):
                    ins = pe.transpose(bankV[:, seq(c)], vT[:, seq(c)], k.ident[:, :])
                ins.then_inc(s_vt, 1)
                for c in range(GS):
                    ins = pe.matmul(bankS[:, seq(c)], qT[:, seq(c)], kT[:, seq(c)], start=True, stop=True)
                ins.then_inc(s_s, 1)
                if more:
                    gates(g + 1, 1 - par)
                pe.wait_ge(s_attn, g + 1)
                for c in range(GS):
                    ins = pe.transpose(bankS[:, seq(c)], attn[:, c, :], k.ident[:, :])
                ins.then_inc(s_pt, 1)
                pe.wait_ge(s_pts, g + 1)
                r_v.wait_done(pe, g)
                for c in range(GS):
                    ins = pe.matmul(bankQ[:, seq(c)], v[:, c, :], probsT[:, seq(c)], start=True, stop=True)
                ins.then_inc(s_o, 1)
                pe.wait_ge(s_oT, g + 1)
                mixture(g, par, 1, ("l3f_o",), (bankK,))
                r_xu.wait_done(pe, (2 * g + 2) * NE3 - 1)
                pe.sem_inc(s_y, 1)
                pe.sem_inc(r_wTu.sem, 1)
                pe.wait_ge(s_yT, g + 1)
                for c in range(GS):
                    ins = pe.transpose(bankV[:, seq(c)], yT[:, seq(c)], k.ident[:, :])
                ins.then_inc(s_yt, 1)

            groups(pe, body)

        @block.scalar
        def _(act):
            for r in (k.r_xnT, r_wT, r_qkv, r_v):
                r.grant(act)
            k.wait_weights(act, "l3f")
            act.activation(sig_e[:, :], w["l3f_gates"][:, :], ACT.Exp, scale=-1.0).then_inc(s_sige, 1)
            ln_evacuate(k, act, 0, 0, bankX)

            def gates(g, par):
                act.wait_ge(s_gx, g + 1)
                act.activation(ex[:, :, :], tb[:, :, :], ACT.Exp).then_inc(s_ex, 1)
                act.wait_ge(s_wTp, g + 1)
                r_wTu.wait_free(act, g)
                act.activation(wT[:, par, :], bankM[:, 256:512].bitcast(BF16), ACT.Copy).then_inc(r_wT.sem, 1)

            gates(0, 0)

            def body(g, par, more, chain):
                act.wait_ge(s_qkv, g + 1)
                act.activation(vT[:, :], bankV[:, :], ACT.Copy)
                act.activation(qT[:, :], bankQ[:, :], ACT.Copy)
                act.activation(kT[:, :], bankK[:, :], ACT.Copy).then_inc(r_qkv.sem, 1)
                act.wait_ge(s_vt, g + 1)
                act.activation(v[:, :, :], bankV.rearrange("p (c d) -> p c d", c=GS), ACT.Copy)\
                   .then_inc(r_v.sem, 1)
                if more:
                    ln_evacuate(k, act, g + 1, 1 - par, bankX)
                act.wait_ge(s_nmax, g + 1)
                for c in range(GS):
                    ins = act.activation(probs[:, c, :], bankS[:, seq(c)], ACT.Exp, bias=nmax[:, c:c + 1],
                                         scale=scale, accum_out=total[:, c:c + 1])
                ins.then_inc(s_p, 1)
                if more:
                    gates(g + 1, 1 - par)
                act.wait_ge(s_pt, g + 1)
                act.activation(probsT[:, :], bankS[:, :], ACT.Copy).then_inc(s_pts, 1)
                act.wait_ge(s_o, g + 1)
                act.activation(oT[:, :], bankQ[:, :], ACT.Copy).then_inc(s_oT, 1)
                act.wait_ge(s_y, g + 1)
                act.activation(yT[:, :], bankK[:, :], ACT.Copy).then_inc(s_yT, 1)

            groups(act, body)

        @block.gpsimd
        def _(pool):
            pool.wait_ge(s_prep, 2)
            pool.tensor_tensor(cinv[:, :], cnorm[:, :], k.minus_half[:, 0:NE3], ALU.pow).then_inc(s_cpow, 1)
            ln_rstd(k, pool, 0)

            def norms(g):
                pool.wait_ge(s_ss, g + 1)
                pool.tensor_tensor(rnorm[:, :], ssum[:, :], k.minus_half[:, 0:GS], ALU.pow).then_inc(s_rn, 1)

            norms(0)

            def body(g, par, more, chain):
                if more:
                    ln_rstd(k, pool, g + 1)
                    norms(g + 1)

            groups(pool, body)

        @block.vector
        def _(dve):
            r_xe.grant(dve)
            r_out.grant(dve)
            k.wait_weights(dve, "l3f")
            prep = Chain(dve, s_prep, 0, 0)
            prep(dve.tensor_tensor(sq[:, :], w["l3f_sim"][:, :], w["l3f_sim"][:, :], ALU.mult))
            dve.memset(w3[:, :, :], 0.0)
            dve.wait_ge(s_csum, 1)
            prep(dve.tensor_scalar(cnorm[:, :], bankM[:, 0:NE3], 1e-24, None, ALU.max))
            dve.wait_ge(s_cpow, 1)
            prep(dve.tensor_tensor(sn[:, :], w["l3f_sim"][:, :], cinv[:, :], ALU.mult))
            dve.wait_ge(s_sige, 1)
            prep(dve.tensor_scalar(sig_e[:, :], sig_e[:, :], 1.0, None, ALU.add))
            prep(dve.reciprocal(sig[:, :], sig_e[:, :]))
            ln_stats(k, dve, 0)
            ln_apply(k, dve, 0)

            first = Chain(dve, sem("first_gates_step"), 0, 0)

            def both(ap):
                return bcast(ap.unsqueeze(2), [P, GS, NE3])

            def norms(g, chain):
                dve.wait_ge(k.s_xn, g + 1)
                chain(dve.tensor_tensor(xsq[:, :, :], k.xn[:, :, :], k.xn[:, :, :], ALU.mult))
                chain(dve.tensor_reduce(top[:, 0, :], xsq[:, :, :], AX, ALU.add))
                dve.tensor_scalar(ssum[:, :], top[:, 0, :], 1e-24, None, ALU.max).then_inc(s_ss, 1)

            def gates(g, par, chain):
                raw = bankM[:, 0:GS * NE3].rearrange("p (c e) -> p c e", c=GS)
                dve.wait_ge(s_gates, g + 1)
                dve.wait_ge(s_rn, g + 1)
                chain(dve.tensor_tensor(ta[:, :, :], raw, both(rnorm[:, :]), ALU.mult))
                chain(dve.tensor_tensor(lg[:, :, :], ta[:, :, :], bcast(sig[:, :].unsqueeze(1), [P, GS, NE3]),
                                        ALU.subtract))
                dve.tensor_scalar(hard[:, :, :], lg[:, :, :], 0.0, None, ALU.is_gt)
                chain(dve.tensor_scalar(gated[:, :, :], lg[:, :, :], 0.0, None, ALU.max))
                chain(dve.tensor_reduce(top[:, 1, :], gated[:, :, :], AX, ALU.max))
                dve.tensor_tensor(tb[:, :, :], gated[:, :, :], both(top[:, 1, :]), ALU.subtract).then_inc(s_gx, 1)
                chain(dve.tensor_scalar(top[:, 2, :], top[:, 1, :], 0.0, None, ALU.is_le))
                for n in range(2):
                    chain(dve.tensor_reduce(top[:, 3, :], lg[:, :, :], AX, ALU.max))
                    chain(dve.tensor_tensor(ta[:, :, :], lg[:, :, :], both(top[:, 3, :]), ALU.is_equal))
                    chain(dve.tensor_tensor(ta[:, :, :], ta[:, :, :], k.descending[:, :, :], ALU.mult))
                    chain(dve.tensor_reduce(top[:, 4, :], ta[:, :, :], AX, ALU.max))
                    chain(dve.tensor_tensor(tc[:, :, :], ta[:, :, :], both(top[:, 4, :]), ALU.is_equal))
                    chain(dve.scalar_tensor_tensor(lg[:, :, :], tc[:, :, :], -1e30, lg[:, :, :], ALU.mult, ALU.add))
                    chain(dve.tensor_tensor(ta[:, :, :], tc[:, :, :], both(top[:, 2, :]), ALU.mult))
                    chain(dve.tensor_tensor(hard[:, :, :], hard[:, :, :], ta[:, :, :], ALU.add))
                dve.wait_ge(s_ex, g + 1)
                chain(dve.tensor_tensor(ta[:, :, :], ex[:, :, :], hard[:, :, :], ALU.mult))
                chain(dve.tensor_reduce(top[:, 5, :], ta[:, :, :], AX, ALU.add))
                chain(dve.reciprocal(top[:, 6, :], top[:, 5, :]))
                chain(dve.tensor_tensor(ta[:, :, :], ta[:, :, :], both(top[:, 6, :]), ALU.mult))
                chain(dve.tensor_copy(w3[:, :, 0:NE3], ta[:, :, :]))
                chain(dve.tensor_tensor(wr1[:, :, :], ta[:, :, :], w3[:, :, 0:NE3], ALU.subtract))
                chain(dve.tensor_copy(w3[:, :, NE3:2 * NE3], wr1[:, :, :]))
                dve.tensor_tensor(w3[:, :, 2 * NE3:3 * NE3], wr1[:, :, :], w3[:, :, NE3:2 * NE3], ALU.subtract)\
                   .then_inc(s_w3, 1)

            def weigh(g, half, src):
                first_e = (2 * g + half) * NE3
                for e in range(NE3):
                    dve.wait_ge(s_we, first_e + e + 1)
                    r_xu.wait_free(dve, first_e + e)
                    dve.tensor_tensor(xe[:, e % 2, :], bankW[e % 2][:, :], src, ALU.mult).then_inc(r_xe.sem, 1)

            norms(0, first)
            gates(0, 0, first)

            def body(g, par, more, chain):
                weigh(g, 0, k.xnT[:, par, :])
                if more:
                    ln_stats(k, dve, g + 1)
                    ln_apply(k, dve, g + 1)
                    norms(g + 1, chain)
                dve.wait_ge(s_s, g + 1)
                chain(dve.tensor_reduce(top[:, 7, :], bankS.rearrange("p (c t) -> p c t", c=GS), AX, ALU.max,
                                        negate=True))
                dve.tensor_scalar(nmax[:, :], top[:, 7, :], scale, None, ALU.mult).then_inc(s_nmax, 1)
                dve.wait_ge(s_p, g + 1)
                chain(dve.reciprocal(rtot[:, :], total[:, :]))
                dve.tensor_tensor(attn[:, :, :], probs[:, :, :], bcast(rtot[:, :].unsqueeze(2), [P, GS, P]),
                                  ALU.mult).then_inc(s_attn, 1)
                if more:
                    gates(g + 1, 1 - par, chain)
                dve.wait_ge(s_oT, g + 1)
                weigh(g, 1, oT[:, :])
                dve.wait_ge(s_yt, g + 1)
                xs = k.x_sb[:, bass.ds(g * T, T)]
                dve.scalar_tensor_tensor(xs, bankV[:, :], k.tanh_g[:, 7:8], xs, ALU.mult, ALU.add)\
                   .then_inc(r_out.sem, 1)

            groups(dve, body, s_chain, (LINKS3, LINKS3_LAST))


LINKS3, LINKS3_LAST = 64, 34


def launch_constants():
    freq = (np.float32(1) / np.float32(10000) ** (np.arange(0, HD, 2, dtype=np.float32) / np.float32(HD)))
    angle = np.tile(np.repeat(freq.astype(np.float32), 2), HEADS)[:, None] * np.arange(P, dtype=np.float32)[None]
    sign = np.tile(np.array([-1, 1], np.float32), P // 2)[:, None]
    part_of = np.zeros((P, NE3), np.float32)
    for e in range(NE3):
        part_of[e:3 * NE3:NE3, e] = 1
    return {
        "l0x_cos": np.tile(np.cos(angle), (1, GS)),
        "l0x_sin": np.tile(np.sin(angle) * sign, (1, GS)),
        "c_ident": np.eye(P, dtype=np.float32),
        "c_part_of": part_of,
        "c_descending": np.tile(np.arange(NE3, 0, -1, dtype=np.float32), (P, GS, 1)),
    }


class Global(Core):
    def __init__(self, nc, ctx, dram):
        self.nc, self.ctx, self.dram, self.w, self.due = nc, ctx, dram, {}, {}
        sb = lambda name, shape, dt: ctx.enter_context(nc.sbuf_tensor(name, shape, dt))
        self.psum = ctx.enter_context(nc.psum_tensor("psum", [P, 8 * 512], F32))
        self.x_sb = sb("x_sb", [P, NSEQ * P], F32)
        self.ident = sb("ident", [P, P], F32)
        self.ident_bf = sb("ident_bf", [P, P], BF16)
        self.part_of = sb("part_of", [P, NE3], F32)
        self.select = sb("select", [P, NE3, P], BF16)
        self.descending = sb("descending", [P, GS, NE3], F32)
        self.minus_half = sb("minus_half", [P, 16], F32)
        self.ones = sb("ones", [P, P], F32)
        self.one_cell = sb("one_cell", [P, 1], F32)
        self.eps = sb("eps", [P, GS], F32)
        self.g_in = sb("g_in", [P, 8], F32)
        self.tanh_g = sb("tanh_g", [P, 8], F32)

    def bank(self, i):
        return self.psum[:, i * 512:(i + 1) * 512]

    def banks(self, i, n):
        return self.psum[:, i * 512:(i + n) * 512]

    def local(self, ctx, prefix):
        sb = lambda name, shape, dt: ctx.enter_context(self.nc.sbuf_tensor(f"{prefix}_{name}", shape, dt))
        used = []
        ctx.callback(self.nc.all_engine_barrier)
        ctx.callback(lambda: self.nc.clear_and_free_semaphores(used))

        def sem(name):
            used.append(self.nc.alloc_semaphore(f"{prefix}_{name}"))
            return used[-1]

        return sb, sem

    def weight(self, layer, name, shape, dt=F32):
        self.w[name] = self.ctx.enter_context(self.nc.sbuf_tensor("w_" + name, shape, dt))
        self.due.setdefault(layer, []).append(name)

    def wait_weights(self, eng, layer):
        eng.wait_ge(self.s_weights[layer], 16 * len(self.due[layer]))


ATTN = {"wq": [P, P], "wk": [P, P], "wv": [P, P], "wo": [P, P], "bq": [P, 1], "bk": [P, 1], "bv": [P, 1],
        "bo": [P, P]}
WEIGHTS = {
    "l0x": {"l0x_" + n: s for n, s in (ATTN | {"wqs": [P, P], "wks": [P, P], "bqs": [P, 1], "bks": [P, 1],
                                               "cos": [P, T], "sin": [P, T]}).items()},
    "l1x": {"l1x_" + n: s for n, s in ATTN.items()},
    "l0f": {"l0f_w1": [P, HID], "l0f_w2": [P, NHB, P], "l0f_cw": [P, 3 * NHB], "l0f_cb": [P, NHB]},
    "l2f": {"l2f_router": [P, NE2], "l2f_router_b": [P, NE2], "l2f_w1": [P, NE2, HID], "l2f_b1": [P, NE2 * NHB],
            "l2f_w2": [P, NE2, NHB, P], "l2f_b2": [NE2, P]},
    "l2x": {"l2x_w1": [P, 1], "l2x_w2": [P, 1], "l2x_w3": [P, 1], "l2x_bsim": [P, 1], "l2x_wqv": [P, 4, P],
            "l2x_bqv": [P, P]},
    "l3f": {"l3f_sim": [P, NE3], "l3f_gates": [P, NE3], "l3f_q": [P, NE3, P], "l3f_k": [P, NE3, P],
            "l3f_v": [P, NE3, P], "l3f_o": [P, NE3, P]},
    "l3x": {"l3x_wq": [P, P], "l3x_wk": [P, P], "l3x_wv": [P, P], "l3x_bq": [P, 1], "l3x_bk": [P, 1],
            "l3x_bv": [P, P]},
    "l1f": {"l1f_ar1": [P, NZL], "l1f_w1": [P, HID], "l1f_b1": [P, HID], "l1f_w2ar": [P, NHB, P + NZL],
            "l1f_b2": [P, P]},
}
LAYERS = {"l0x": layer0_attention, "l0f": layer0_ffn, "l1x": layer1_attention, "l1f": layer1_ffn, "l2x": layer2_attention, "l2f": layer2_ffn, "l3x": layer3_attention, "l3f": layer3_ffn}


LATE = ("l2f", "l3f")


def load_weights(k, sp, layers):
    for layer in layers:
        for name in k.due[layer]:
            w, src = k.w[name], k.dram[name]
            if tuple(src.shape) != tuple(w.shape):
                src = bcast(src, w.shape)
            sp.dma_start(w[:], src).then_inc(k.s_weights[layer], 16)


def program(nc, dram, out, layers):
    with ExitStack() as ctx:
        k = Global(nc, ctx, dram)
        k.s_weights = {}
        for layer in layers:
            k.s_weights[layer] = ctx.enter_context(nc.semaphore(f"weights_{layer}_in"))
            if layer not in LATE:
                for name, shape in WEIGHTS[layer].items():
                    k.weight(layer, name, shape)
        s_x = ctx.enter_context(nc.semaphore("x_in"))
        s_const = ctx.enter_context(nc.semaphore("constants_in"))
        k.s_filled = ctx.enter_context(nc.semaphore("fills_ready"))
        s_tanh = ctx.enter_context(nc.semaphore("tanh_g_ready"))
        s_out = ctx.enter_context(nc.semaphore("x_out"))

        with nc.Block() as block:
            @block.sync
            def _(sp):
                for name, t in (("ident", k.ident), ("part_of", k.part_of), ("descending", k.descending)):
                    sp.dma_start(t[:], dram["c_" + name]).then_inc(s_const, 16)
                sp.dma_start(k.g_in[:, :], bcast(dram["gains"], [P, 8])).then_inc(s_const, 16)
                sp.dma_start(k.x_sb[:, :], dram["x"]).then_inc(s_x, 16)
                load_weights(k, sp, [layer for layer in layers if layer not in LATE])

            @block.vector
            def _(dve):
                dve.memset(k.minus_half[:, :], -0.5).then_inc(k.s_filled, 1)
                dve.memset(k.ones[:, :], 1.0).then_inc(k.s_filled, 1)
                dve.memset(k.eps[:, :], LN_EPS).then_inc(k.s_filled, 1)
                dve.wait_ge(s_const, 64)
                dve.tensor_copy(k.ident_bf[:, :], k.ident[:, :]).then_inc(k.s_filled, 1)
                dve.tensor_copy(k.select[:, :, :], bcast(k.part_of[:, :].unsqueeze(2), [P, NE3, P]))\
                   .then_inc(k.s_filled, 1)
                dve.wait_ge(k.s_filled, 5)
                dve.wait_ge(s_x, 16)

            @block.scalar
            def _(act):
                act.wait_ge(s_const, 64)
                act.activation(k.tanh_g[:, :], k.g_in[:, :], ACT.Tanh).then_inc(s_tanh, 1)
                act.wait_ge(s_tanh, 1)

        early = [layer for layer in layers if layer in ("l0x", "l0f", "l1x")]
        late = [layer for layer in layers if layer in LATE]
        for layer in early:
            LAYERS[layer](nc, k)
        for layer in late:
            for name, shape in WEIGHTS[layer].items():
                k.weight(layer, name, shape)
        with nc.Block() as block:
            @block.sync
            def _(sp):
                load_weights(k, sp, late)

        for layer in layers[len(early):]:
            LAYERS[layer](nc, k)

        with nc.Block() as block:
            @block.sync
            def _(sp):
                sp.dma_start(out, k.x_sb[:, :]).then_inc(s_out, 16)
                sp.wait_ge(s_out, 16)


def layouts(i):
    f = lambda a: np.ascontiguousarray(a, dtype=np.float32)
    pad = lambda a, rows: np.concatenate([a, np.zeros((rows - a.shape[0],) + a.shape[1:], np.float32)])
    tok = lambda a: f(np.transpose(a, (1, 0, 2)).reshape(P, NSEQ * P))
    d = launch_constants()
    d["x"] = tok(i["x"])
    d["ctx_tok"] = tok(i["ctx_1024"])
    d["ctxT"] = f(np.transpose(i["ctx_1024"], (2, 0, 1)).reshape(P, NSEQ * P))
    d["gains"] = f(np.concatenate([i["g_xattn"], i["g_ffn"]]).reshape(1, 8))
    swap = np.arange(P) ^ 1
    for n in (0, 1):
        for m in "qk":
            wm, bm = i[f"L{n}_xattn_W{m}"], i[f"L{n}_xattn_b{m}"]
            d[f"l{n}x_w{m}"], d[f"l{n}x_b{m}"] = f(wm.T), f(bm.reshape(P, 1))
            if n == 0:
                d[f"l0x_w{m}s"], d[f"l0x_b{m}s"] = f(wm[swap].T), f(bm[swap].reshape(P, 1))
        d[f"l{n}x_wv"], d[f"l{n}x_wo"] = f(i[f"L{n}_xattn_Wv"].T), f(i[f"L{n}_xattn_Wo"].T)
        d[f"l{n}x_bv"], d[f"l{n}x_bo"] = f(i[f"L{n}_xattn_bv"].reshape(P, 1)), f(i[f"L{n}_xattn_bo"].reshape(1, P))
    d["l0f_w1"] = f(i["L0_ffn_w1"].T)
    d["l0f_w2"] = f(np.transpose(i["L0_ffn_w2"].T.reshape(NHB, P, P), (1, 0, 2)))
    d["l0f_cw"] = f(np.transpose(i["L0_ffn_conv_w"].reshape(NHB, P, 3), (1, 0, 2)).reshape(P, 3 * NHB))
    d["l0f_cb"] = f(i["L0_ffn_conv_b"].reshape(NHB, P).T)
    d["l2f_router"] = f(i["L2_ffn_router_W"])
    d["l2f_router_b"] = f(i["L2_ffn_router_b"].reshape(1, NE2))
    d["l2f_w1"] = f(np.transpose(i["L2_ffn_W1"], (1, 0, 2)))
    d["l2f_b1"] = f(np.transpose(i["L2_ffn_b1"].reshape(NE2 * NHB, P)))
    d["l2f_w2"] = f(np.transpose(i["L2_ffn_W2"].reshape(NE2, NHB, P, P), (2, 0, 1, 3)))
    d["l2f_b2"] = f(i["L2_ffn_b2"])
    for n in range(3):
        d[f"l2x_w{n + 1}"] = f(i["L2_xattn_w_sim"][n * P:(n + 1) * P].reshape(P, 1))
    d["l2x_bsim"] = f(i["L2_xattn_b_sim"].reshape(1, 1))
    d["l2x_wqv"] = f(np.transpose(i["L2_xattn_W_qv"].reshape(4, P, P), (1, 0, 2)))
    d["l2x_bqv"] = f(i["L2_xattn_b_qv"].reshape(1, P))
    for n in "qkvo":
        d[f"l3f_{n}"] = f(np.transpose(i[f"L3_ffn_{n}_proj"], (1, 0, 2)))
    d["l3f_sim"] = f(i["L3_ffn_sim_matrix"])
    d["l3f_gates"] = f(i["L3_ffn_gates"].reshape(1, NE3))
    d["l3x_wq"], d["l3x_wk"], d["l3x_wv"] = (f(i[f"L3_xattn_W{n}"]) for n in "qkv")
    d["l3x_bq"], d["l3x_bk"] = (f(i[f"L3_xattn_b{n}"].reshape(P, 1)) for n in "qk")
    d["l3x_bv"] = f(i["L3_xattn_bv"].reshape(1, P))
    flat_a = lambda a: np.transpose(a, (1, 0, 2)).reshape(a.shape[1], NZ)
    d["l1f_ar1"] = f(np.concatenate([flat_a(i["L1_ffn_A1"]), i["L1_ffn_R1"]], 1))
    d["l1f_w1"] = f(i["L1_ffn_W1"])
    d["l1f_b1"] = f(pad(np.concatenate([i["L1_ffn_B1"].reshape(NZ, HID), i["L1_ffn_b1"][None]]), P))
    w2ar = np.concatenate([i["L1_ffn_W2"], flat_a(i["L1_ffn_A2"]), i["L1_ffn_R2"]], 1)
    d["l1f_w2ar"] = f(np.transpose(w2ar.reshape(NHB, P, P + NZL), (1, 0, 2)))
    d["l1f_b2"] = f(pad(np.concatenate([i["L1_ffn_B2"].reshape(NZ, P), i["L1_ffn_b2"][None]]), P))
    return d


def kernel(**inputs):
    import concourse.bacc as bacc
    from concourse.bass_utils import run_bass_kernel_spmd

    arrays = layouts({n: np.asarray(a) for n, a in inputs.items()})
    nc = bacc.Bacc("TRN2", target_bir_lowering=False, num_devices=1)
    dram = {n: nc.dram_tensor(f"in_{n}", a.shape, mybir.dt.from_np(a.dtype), kind="ExternalInput").ap()
            for n, a in arrays.items()}
    out = nc.dram_tensor("out_x", (P, NSEQ * P), F32, kind="ExternalOutput").ap()
    program(nc, dram, out, list(LAYERS))
    r = run_bass_kernel_spmd(nc, [{f"in_{n}": a for n, a in arrays.items()}], core_ids=[0])
    x = r.results[0]["out_x"]
    return np.ascontiguousarray(x.reshape(P, NSEQ, P).transpose(1, 0, 2))
```

```python
from contextlib import ExitStack

import numpy as np
import concourse.bass as bass
from concourse import mybir

F32 = mybir.dt.float32
F32R = mybir.dt.float32r
BF16 = mybir.dt.bfloat16
I32 = mybir.dt.int32
ALU = mybir.AluOpType
ACT = mybir.ActivationFunctionType
AX = mybir.AxisListType.X

P = 128
NSEQ = 32
GS = 4
NG = NSEQ // GS
T = GS * P
HEADS, HD = 16, 8
HID = 512
NHB = HID // P
LN_EPS = 1e-5
MAGIC = 12582912.0


class Ring:

    def __init__(self, sem, depth):
        self.sem, self.depth = sem, depth

    def grant(self, eng):
        eng.sem_inc(self.sem, self.depth)

    def wait_free(self, eng, unit):
        eng.wait_ge(self.sem, unit + 1)

    def wait_done(self, eng, unit):
        eng.wait_ge(self.sem, unit + 1 + self.depth)


class Chain:

    def __init__(self, eng, sem, links, it):
        self.eng, self.sem, self.links, self.it, self.n = eng, sem, links, it, 0

    def __call__(self, ins):
        self.n += 1
        ins.then_inc(self.sem, 1)
        self.eng.wait_ge(self.sem, self.it * self.links + self.n)


class Core:
    pass


def seq(c):
    return slice(c * P, (c + 1) * P)


def bcast(ap, shape):
    return ap.broadcast_to(shape)


def ln_tensors(k, sb, sem):
    k.stats = sb("ln_stats", [P, GS, 6], F32)
    k.mv = sb("ln_mean_var", [P, GS, 2], F32)
    k.rstd = sb("ln_rstd", [P, GS], F32)
    k.xn = sb("xn", [P, GS, P], F32)
    k.xnT = sb("xnT", [P, 2, T], F32)
    k.s_rows = sem("ln_rows_counted")
    k.s_stats = sem("ln_stats_ready")
    k.s_vare = sem("ln_var_plus_eps")
    k.s_rstd = sem("ln_rstd_ready")
    k.s_xn = sem("xn_ready")
    k.r_xnT_psum = Ring(sem("xnT_in_psum"), 1)
    k.r_xnT = Ring(sem("xnT_ready"), 1)
    k.r_xnT_used = Ring(sem("xnT_used"), 2)


def ln_stats(k, dve, g):
    for c in range(GS):
        ins = dve.bn_stats(k.stats[:, c, :], k.x_sb[:, bass.ds((g * GS + c) * P, P)])
    ins.then_inc(k.s_rows, 1)
    dve.wait_ge(k.s_rows, g + 1)
    dve.tensor_copy(k.one_cell[:, :], k.eps[:, 0:1])
    for c in range(GS):
        ins = dve.bn_aggr(k.mv[:, c, :], k.stats[:, c, :])
    ins.then_inc(k.s_stats, 1)


def ln_rstd(k, pool, g):
    pool.wait_ge(k.s_stats, g + 1)
    pool.tensor_tensor(k.rstd[:, :], k.mv[:, :, 1], k.eps[:, :], ALU.add).then_inc(k.s_vare, 1)
    pool.wait_ge(k.s_vare, g + 1)
    pool.tensor_tensor(k.rstd[:, :], k.rstd[:, :], k.minus_half[:, 0:GS], ALU.pow).then_inc(k.s_rstd, 1)


def ln_apply(k, dve, g):
    dve.wait_ge(k.s_rstd, g + 1)
    k.r_xnT_psum.wait_free(dve, g)
    for c in range(GS):
        ins = dve.tensor_scalar(k.xn[:, c, :], k.x_sb[:, bass.ds((g * GS + c) * P, P)],
                                k.mv[:, c, 0:1], k.rstd[:, c:c + 1], ALU.subtract, ALU.mult)
    ins.then_inc(k.s_xn, 1)


def ln_transpose(k, pe, g, bank):
    pe.wait_ge(k.s_xn, g + 1)
    k.r_xnT.wait_free(pe, g)
    for c in range(GS):
        ins = pe.transpose(bank[:, seq(c)], k.xn[:, c, :], k.ident[:, :])
    ins.then_inc(k.r_xnT_psum.sem, 1)


def ln_evacuate(k, act, g, par, bank):
    k.r_xnT_psum.wait_done(act, g)
    k.r_xnT_used.wait_free(act, g)
    act.activation(k.xnT[:, par, :], bank[:, :], ACT.Copy).then_inc(k.r_xnT.sem, 1)


def groups(eng, body, chain_sem=None, links=0):
    links = links if isinstance(links, tuple) else (links, links)
    per_pair = links[0]

    def two(it, last):
        chain = Chain(eng, chain_sem, per_pair, it)
        for par in range(2):
            body(2 * it + par, par, not (last and par), chain)
        assert chain.n == links[last], f"{chain.n} links, not {links[last]}"

    with eng.Fori(0, NG // 2 - 1) as it:
        two(it, False)
    two(NG // 2 - 1, True)


NPART = 3
SROWS = NPART * NPART * HD
AROWS = SROWS + NPART


def heads_attention(nc, k, name, rope, gain):
    with ExitStack() as ctx:
        sb, sem = k.local(ctx, name)
        ln_tensors(k, sb, sem)
        w = {n[len(name) + 1:]: t for n, t in k.w.items() if n.startswith(name + "_")}
        ctxT = sb("ctxT", [P, 2, T], F32)
        gb = sb("tanh_g_bias", [P, GS, P], F32)
        bias = sb("out_bias", [P, P], F32)
        turned = {n: [sb(f"{n}_turned{i}", [P, T], F32) for i in range(2)] for n in "kq"} if rope else None
        full = {n: sb(f"{n}_full", [P, T], F32) for n in "kq"}
        rest = sb("rest", [P, T], F32)
        parts = {n: sb(f"{n}_parts", [P, NPART, T], BF16) for n in "kq"}
        stack = {n: sb(f"{n}_stack", [AROWS, 2, HEADS, T], BF16) for n in "kq"}
        v1 = sb("v_and_one", [P, 2, GS, HEADS, HD + 1], F32)
        nm = sb("minus_max", [P, GS, HEADS], F32)
        nm_rest = sb("minus_max_rest", [P, HEADS], F32)
        mp = sb("minus_max_parts", [P, GS, NPART * HEADS], BF16)
        mT = sb("minus_max_T", [NPART * HEADS, T], BF16)
        pT = sb("probsT", [P, 2, HEADS, P], F32)
        ae = sb("attn_sums_T", [P, T], F32)
        rz = sb("rsum", [P, HEADS], F32)
        an = sb("attn", [P, P], F32)
        aT = sb("aT", [P, 2, P], F32)
        bankS, bankT = [k.bank(0), k.bank(1)], [k.bank(2), k.bank(3)]
        bankA, bankP0, bankP1 = (k.bank(i) for i in range(4, 7))
        bankM = k.bank(7)
        scale = float(HD) ** -0.5
        scratch = {n: nc.dram_tensor(f"{name}_{n}_scratch", (2,) + lead + (P, T), BF16).ap()
                   for n, lead in (("k", (NPART, NPART)), ("q", (NPART,)))}
        scratch_m = nc.dram_tensor(f"{name}_max_scratch", (2, NPART * HEADS, T), BF16).ap()

        s_fill = sem("fills_done")
        s_bias = sem("bias_step")
        s_bp = sem("v_bias_in_psum")
        s_chain = sem("dve_step")
        s_split = sem("pool_step")
        s_ctx = [sem(f"ctxT_in_{p}") for p in range(2)]
        s_proj = {n: sem(f"{n}_in_psum") for n in "kqv"}
        r_out = {n: Ring(sem(f"{n}_emptied"), 1) for n in "kq"}
        r_v = Ring(sem("v_ready"), 1)
        r_full = {n: Ring(sem(f"{n}_split"), 1) for n in "kq"}
        s_stack = [sem(f"stack_in_{p}") for p in range(2)]
        s_head = sem("pool_head_step")
        s_nm = sem("minus_max_ready")
        s_s = sem("scores_in_psum")
        r_red = Ring(sem("maxima_taken"), 2)
        r_mp = Ring(sem("minus_max_split"), GS)
        r_mT = Ring(sem("minus_maxT_in_psum"), GS)
        r_mTs = Ring(sem("minus_maxT_ready"), 1)
        s_parts_out = {n: sem(f"{n}_parts_in_dram") for n in "kq"}
        s_mT_out = sem("minus_maxT_in_dram")
        s_shift = [[sem(f"shift_rows_in_{p}{i}") for i in range(GS)] for p in range(2)]
        s_t = sem("scoresT_in_psum")
        r_exp = Ring(sem("exp_done"), 2)
        r_av = Ring(sem("attn_in_psum"), 2)
        s_ae = sem("attn_sums_T_ready")
        s_turned = sem("attn_sums_in_psum")
        s_an = sem("attn_ready")
        s_back = sem("aT_in_psum")
        r_aT = Ring(sem("aT_ready"), 1)
        r_o = Ring(sem("out_in_psum"), 2)
        r_x = Ring(sem("x_updated"), 1)

        def landed(eng, sems, g, par, dmas):
            eng.wait_ge(sems[par], (g - par) * 8 * dmas + 16 * dmas)

        block = ctx.enter_context(nc.Block())

        @block.sync
        def _(sp):
            def load_ctx(g, par):
                if not isinstance(g, int):
                    sp.wait_ge(s_proj["v"], g - 1)
                sp.dma_start(ctxT[:, par, :], k.dram["ctxT"][:, bass.ds(g * T, T)]).then_inc(s_ctx[par], 16)

            def parts_out(g, par):
                r_full["k"].wait_done(sp, g)
                for y in range(NPART):
                    sp.dma_start(scratch["k"][par, :, y, :, :].rearrange("x p t -> p x t"), parts["k"][:, :, :])\
                      .then_inc(s_parts_out["k"], 16)
                r_full["q"].wait_done(sp, g)
                sp.dma_start(scratch["q"][par].rearrange("y p t -> p y t"), parts["q"][:, :, :])\
                  .then_inc(s_parts_out["q"], 16)

            def build_stacks(g, par):
                sp.wait_ge(s_parts_out["k"], 16 * NPART * (g + 1))
                sp.dma_start(stack["k"][0:SROWS, par, :, :],
                             scratch["k"][par].rearrange("x y (d h) t -> (x y d) h t", d=HD)).then_inc(s_stack[par], 16)
                sp.wait_ge(s_parts_out["q"], 16 * (g + 1))
                for x in range(NPART):
                    sp.dma_start(stack["q"][x * NPART * HD:(x + 1) * NPART * HD, par, :, :],
                                 scratch["q"][par].rearrange("y (d h) t -> (y d) h t", d=HD)).then_inc(s_stack[par], 16)

            def shift_rows(g, par, c):
                r_mTs.wait_done(sp, g * GS + c)
                sp.dma_start(scratch_m[par][:, seq(c)], mT[:, seq(c)]).then_inc(s_mT_out, 16)
                sp.wait_ge(s_mT_out, 16 * (g * GS + c + 1 + GS))
                sp.dma_start(stack["q"][SROWS:AROWS, par, :, seq(c)],
                             scratch_m[par][:, seq(c)].rearrange("(a h) t -> a h t", a=NPART))\
                  .then_inc(s_shift[par][c], 16)

            sp.sem_inc(s_mT_out, 16 * GS)
            sp.wait_ge(s_fill, 3)
            load_ctx(0, 0)
            load_ctx(1, 1)
            for g in range(2):
                parts_out(g, g)
                build_stacks(g, g)
            for c in range(GS - 1):
                shift_rows(0, 0, c)

            def body(t, par, more, chain):
                after = not isinstance(t, int)
                if after:
                    load_ctx(t + 2, par)
                shift_rows(t, par, GS - 1)
                if after:
                    parts_out(t + 2, par)
                if more:
                    shift_rows(t + 1, 1 - par, 0)
                if after:
                    build_stacks(t + 2, par)
                if more:
                    shift_rows(t + 1, 1 - par, 1)
                    shift_rows(t + 1, 1 - par, 2)

            groups(sp, body)

        @block.tensor
        def _(pe):
            for r in (k.r_xnT_psum, k.r_xnT_used, r_mT, r_av, r_o):
                r.grant(pe)
            k.wait_weights(pe, name)
            pe.matmul(bankM[:, 0:P], bcast(w["bv"][:, 0:1], [P, P]), w["wo"][:, :], start=True, stop=True)\
              .then_inc(s_bp, 1)
            pe.wait_ge(s_bias, 1)
            pe.wait_ge(s_fill, 3)

            def project(n, g, par, src):
                last = None
                for bank, kind in ((bankP0, ""), (bankP1, "s"))[:2 if rope else 1]:
                    last = pe.matmul(bank[:, :], w[f"w{n}{kind}"][:, :], src, start=True, stop=True)
                last.then_inc(s_proj[n], 1)

            def turn_xn(g):
                r_out["q"].wait_free(pe, g)
                if not isinstance(g, int):
                    r_mTs.wait_done(pe, (g - 2) * GS + 3)
                ln_transpose(k, pe, g, bankP1)

            def project_k(g, par):
                r_v.wait_free(pe, g)
                landed(pe, s_ctx, g, par, 1)
                k.r_xnT.wait_done(pe, g)
                project("k", g, par, ctxT[:, par, :])

            def project_q(g, par):
                r_out["k"].wait_done(pe, g)
                project("q", g, par, k.xnT[:, par, :])

            def project_v(g, par):
                r_out["q"].wait_done(pe, g)
                pe.sem_inc(k.r_xnT_used.sem, 1)
                for c in range(GS):
                    ins = pe.matmul(bankP0[:, seq(c)], ctxT[:, par, seq(c)], w["wv"][:, :], start=True, stop=True)
                ins.then_inc(s_proj["v"], 1)

            def scores(g, par, c, u):
                if c == 0 and u == 0:
                    landed(pe, s_stack, g, par, 1 + NPART)
                unit = (g * GS + c) * 4 + u
                r_red.wait_free(pe, unit)
                for j in range(4):
                    h = 4 * u + j
                    ins = pe.matmul(bankS[u % 2][:, seq(j)], stack["q"][0:SROWS, par, h, seq(c)],
                                    stack["k"][0:SROWS, par, h, seq(c)], start=True, stop=True)
                ins.then_inc(s_s, 1)

            def turn_max(g, c, queries_due=None):
                if c == 0 and queries_due is not None:
                    r_out["q"].wait_done(pe, queries_due)
                r_mp.wait_done(pe, g * GS + c)
                r_mTs.wait_free(pe, g * GS + c)
                pe.matmul(bankP1[0:NPART * HEADS, seq(c)], mp[:, c, :], k.ident_bf[:, :], start=True, stop=True)\
                  .then_inc(r_mT.sem, 1)

            def scoresT(g, par, c, u):
                if u == 0:
                    pe.wait_ge(s_shift[par][c], (g - par) * 8 + 16)
                r_exp.wait_free(pe, (g * GS + c) * 4 + u)
                for j in range(4):
                    h = 4 * u + j
                    ins = pe.matmul(bankT[u % 2][:, seq(j)], stack["k"][:, par, h, seq(c)],
                                    stack["q"][:, par, h, seq(c)], start=True, stop=True)
                ins.then_inc(s_t, 1)

            def attend(g, par, c):
                unit = g * GS + c
                r_exp.wait_done(pe, unit * 4 + 3)
                r_aT.wait_free(pe, unit)
                for h in range(HEADS):
                    row = 32 * (h % 4)
                    ins = pe.matmul(bankA[row:row + HD + 1, seq(h // 4)], v1[:, par, c, h, :], pT[:, c % 2, h, :],
                                    start=True, stop=True)
                ins.then_inc(r_av.sem, 1)

            def turn(g, c):
                unit = g * GS + c
                pe.wait_ge(s_ae, unit + 1)
                r_x.wait_free(pe, unit)
                for u in range(4):
                    ins = pe.transpose(bankM[:, seq(u)], ae[:, seq(u)], k.ident[:, :])
                ins.then_inc(s_turned, 1)

            def back(g, c):
                pe.wait_ge(s_an, g * GS + c + 1)
                pe.transpose(bankA[:, 0:P], an[:, :], k.ident[:, :]).then_inc(s_back, 1)

            def out(g, c):
                unit = g * GS + c
                r_aT.wait_done(pe, unit)
                pe.matmul(bankM[:, 0:P], aT[:, c % 2, :], w["wo"][:, :], start=True, stop=True).then_inc(r_o.sem, 1)

            for g in range(2):
                turn_xn(g)
                project_k(g, g)
                project_q(g, g)
                project_v(g, g)
            for c in range(GS):
                for u in range(4):
                    scores(0, 0, c, u)
                if c > 0:
                    turn_max(0, c - 1, 1)

            def body(t, par, more, chain):
                after = not isinstance(t, int)

                def step(ct, cs, *between):
                    for u in range(4):
                        if ct is not None:
                            scoresT(t, par, ct, u)
                        if cs is not None and more:
                            scores(t + 1, 1 - par, cs, u)
                        for at, what in between:
                            if at == u:
                                what()

                att = lambda c: (1, lambda: attend(t, par, c))
                put = lambda c, at=0: (at, lambda: out(t, c))
                step(0, None)
                turn_max(t, 3)
                step(1, None, att(0))
                turn(t, 0)
                if after:
                    turn_xn(t + 2)
                    project_k(t + 2, par)
                back(t, 0)
                step(2, 0, put(0), att(1))
                turn(t, 1)
                if after:
                    project_q(t + 2, par)
                back(t, 1)
                step(3, 1, put(1), att(2))
                turn(t, 2)
                if more:
                    turn_max(t + 1, 0, t + 2 if after else None)
                back(t, 2)
                step(None, 2, put(2), att(3))
                turn(t, 3)
                if more:
                    turn_max(t + 1, 1)
                step(None, 3, (0, lambda: back(t, 3)), put(3, 2))
                if after:
                    project_v(t + 2, par)
                if more:
                    turn_max(t + 1, 2)

            groups(pe, body)

        @block.scalar
        def _(act):
            for r in (k.r_xnT, r_v, r_mTs, r_exp, r_aT) + (() if rope else (r_out["k"], r_out["q"])):
                r.grant(act)
            k.wait_weights(act, name)
            act.wait_ge(s_fill, 3)

            def evacuate(n, g):
                if not rope:
                    act.wait_ge(s_proj[n], g + 1)
                    r_full[n].wait_free(act, g)
                    act.activation(full[n][:, :], bankP0[:, :], ACT.Identity, bias=w["b" + n][:, :])\
                       .then_inc(r_out[n].sem, 1)

            def v_out(g, par):
                act.wait_ge(s_proj["v"], g + 1)
                act.activation(v1[:, par, :, :, 0:HD], bankP0.rearrange("p (c h d) -> p c h d", c=GS, h=HEADS), ACT.Copy)\
                   .then_inc(r_v.sem, 1)

            def max_out(g, c):
                r_mT.wait_done(act, g * GS + c)
                act.wait_ge(s_mT_out, 16 * (g * GS + c + 1))
                act.activation(mT[:, seq(c)], bankP1[0:NPART * HEADS, seq(c)], ACT.Copy).then_inc(r_mTs.sem, 1)

            def exps(g, c, units):
                unit = g * GS + c
                if units[0] == 0:
                    r_av.wait_free(act, unit)
                for u in units:
                    act.wait_ge(s_t, unit * 4 + u + 1)
                    act.activation(pT[:, c % 2, 4 * u:4 * u + 4, :], bankT[u % 2].rearrange("p (j q) -> p j q", j=4),
                                   ACT.Exp, scale=scale).then_inc(r_exp.sem, 1)

            def attn_out(g, c):
                unit = g * GS + c
                r_av.wait_done(act, unit)
                act.activation(ae[:, :], bankA[:, :], ACT.Copy).then_inc(s_ae, 1)

            def aT_out(g, c):
                unit = g * GS + c
                act.wait_ge(s_back, unit + 1)
                r_o.wait_free(act, unit)
                act.activation(aT[:, c % 2, :], bankA[:, 0:P], ACT.Copy).then_inc(r_aT.sem, 1)

            for g in range(2):
                ln_evacuate(k, act, g, g, bankP1)
                evacuate("k", g)
                evacuate("q", g)
                v_out(g, g)
            for c in range(GS - 1):
                max_out(0, c)

            def body(t, par, more, chain):
                after = not isinstance(t, int)
                exps(t, 0, range(4))
                max_out(t, 3)
                exps(t, 1, (0, 1))
                attn_out(t, 0)
                exps(t, 1, (2, 3))
                if after:
                    ln_evacuate(k, act, t + 2, par, bankP1)
                    evacuate("k", t + 2)
                aT_out(t, 0)
                exps(t, 2, (0, 1))
                attn_out(t, 1)
                exps(t, 2, (2, 3))
                if after:
                    evacuate("q", t + 2)
                aT_out(t, 1)
                exps(t, 3, (0, 1))
                attn_out(t, 2)
                exps(t, 3, (2, 3))
                if more:
                    max_out(t + 1, 0)
                aT_out(t, 2)
                attn_out(t, 3)
                if more:
                    max_out(t + 1, 1)
                aT_out(t, 3)
                if after:
                    v_out(t + 2, par)
                if more:
                    max_out(t + 1, 2)

            groups(act, body)

        @block.gpsimd
        def _(pool):
            for r in (r_full["k"], r_full["q"], r_mp):
                r.grant(pool)
            pool.memset(v1[:, :, :, :, :], 1.0).then_inc(s_fill, 1)

            def split(g, par, chain):
                for n in "kq":
                    if rope:
                        pool.wait_ge(r_out[n].sem, g + 2)
                        chain(pool.tensor_tensor(full[n][:, :], turned[n][0][:, :], turned[n][1][:, :], ALU.add))
                    else:
                        r_out[n].wait_done(pool, g)
                    if not isinstance(g, int) or g > 0:
                        pool.wait_ge(s_parts_out[n], (16 * NPART if n == "k" else 16) * g)
                    p = [parts[n][:, a, :] for a in range(NPART)]
                    chain(pool.tensor_tensor(p[0], full[n][:, :], bcast(k.ones[:, 0:1], [P, T]), ALU.mult))
                    chain(pool.tensor_tensor(rest[:, :], full[n][:, :], p[0], ALU.subtract))
                    chain(pool.tensor_tensor(p[1], rest[:, :], bcast(k.ones[:, 0:1], [P, T]), ALU.mult))
                    pool.tensor_tensor(p[2], rest[:, :], p[1], ALU.subtract).then_inc(r_full[n].sem, 1)
                    r_full[n].wait_done(pool, g)

            def split_max(g, c, chain):
                unit = g * GS + c
                pool.wait_ge(s_nm, unit + 1)
                r_mT.wait_free(pool, unit)
                part = lambda a: mp[:, c, a * HEADS:(a + 1) * HEADS]
                chain(pool.tensor_tensor(part(0), nm[:, c, :], k.ones[:, 0:HEADS], ALU.mult))
                chain(pool.tensor_tensor(nm_rest[:, :], nm[:, c, :], part(0), ALU.subtract))
                chain(pool.tensor_tensor(part(1), nm_rest[:, :], k.ones[:, 0:HEADS], ALU.mult))
                pool.tensor_tensor(part(2), nm_rest[:, :], part(1), ALU.subtract).then_inc(r_mp.sem, 1)
                r_mp.wait_done(pool, unit)

            head = Chain(pool, s_head, 0, 0)
            for g in range(2):
                ln_rstd(k, pool, g)
                split(g, g, head)
            for c in range(GS):
                split_max(0, c, head)

            def body(t, par, more, chain):
                if not isinstance(t, int):
                    ln_rstd(k, pool, t + 2)
                    split(t + 2, par, chain)
                if more:
                    for c in range(GS):
                        split_max(t + 1, c, chain)

            groups(pool, body, s_split, (36 + 4 * rope, 12))

        @block.vector
        def _(dve):
            r_red.grant(dve)
            r_x.grant(dve)
            if rope:
                r_out["k"].grant(dve)
                r_out["q"].grant(dve)
            dve.memset(stack["k"][64:AROWS, :, :, :], 1.0).then_inc(s_fill, 1)
            dve.memset(bankA[:, :], 0.0).then_inc(s_fill, 1)
            k.wait_weights(dve, name)
            dve.wait_ge(s_bp, 1)
            dve.tensor_tensor(bias[:, :], bankM[:, 0:P], w["bo"][:, :], ALU.add).then_inc(s_bias, 1)
            dve.wait_ge(s_bias, 1)
            for c in range(GS):
                ins = dve.tensor_scalar(gb[:, c, :], bias[:, :], k.tanh_g[:, gain:gain + 1], None, ALU.mult)
            ins.then_inc(s_bias, 1)
            dve.wait_ge(s_bias, 2)

            def norm(g):
                ln_stats(k, dve, g)
                ln_apply(k, dve, g)
                dve.wait_ge(k.s_xn, g + 1)
                xs = k.x_sb[:, bass.ds(g * T, T)]
                dve.tensor_tensor(xs, xs, gb[:, :, :].rearrange("p c d -> p (c d)"), ALU.add)

            def rotate(n, g):
                if rope:
                    dve.wait_ge(s_proj[n], g + 1)
                    r_full[n].wait_free(dve, g)
                    dve.scalar_tensor_tensor(turned[n][0][:, :], bankP0[:, :], w["b" + n][:, :], w["cos"][:, :],
                                             ALU.add, ALU.mult)
                    dve.scalar_tensor_tensor(turned[n][1][:, :], bankP1[:, :], w["b" + n + "s"][:, :],
                                             w["sin"][:, :], ALU.add, ALU.mult).then_inc(r_out[n].sem, 1)

            def maxima(g, c, units):
                if units[0] == 0:
                    r_mp.wait_free(dve, g * GS + c)
                for u in units:
                    unit = (g * GS + c) * 4 + u
                    dve.wait_ge(s_s, unit + 1)
                    dve.tensor_reduce(nm[:, c, 4 * u:4 * u + 4], bankS[u % 2].rearrange("p (j t) -> p j t", j=4), AX,
                                      ALU.max, negate=True).then_inc(r_red.sem, 1)
                if units[-1] == 3:
                    r_red.wait_done(dve, (g * GS + c) * 4 + 3)
                    dve.sem_inc(s_nm, 1)

            def normalise(g, c, chain):
                dve.wait_ge(s_turned, g * GS + c + 1)
                both = bankM.rearrange("p (h n) -> p h n", n=32)
                chain(dve.reciprocal(rz[:, :], both[:, :, HD]))
                dve.tensor_tensor(an[:, :].rearrange("p (h d) -> p h d", d=HD), both[:, :, 0:HD],
                                  bcast(rz[:, :].unsqueeze(2), [P, HEADS, HD]), ALU.mult).then_inc(s_an, 1)

            def update(g, c):
                unit = g * GS + c
                r_o.wait_done(dve, unit)
                xc = k.x_sb[:, bass.ds(unit * P, P)]
                dve.scalar_tensor_tensor(xc, bankM[:, 0:P], k.tanh_g[:, gain:gain + 1], xc, ALU.mult, ALU.add)\
                   .then_inc(r_x.sem, 1)

            for g in range(2):
                norm(g)
                rotate("k", g)
                rotate("q", g)
            for c in range(GS):
                maxima(0, c, range(4))

            def body(t, par, more, chain):
                after = not isinstance(t, int)

                def between(c, first, second):
                    if more:
                        maxima(t + 1, c, first)
                    update(t, c)
                    if more:
                        maxima(t + 1, c, second)

                if after:
                    norm(t + 2)
                normalise(t, 0, chain)
                if after:
                    rotate("k", t + 2)
                between(0, (0, 1), (2, 3))
                normalise(t, 1, chain)
                if after:
                    rotate("q", t + 2)
                between(1, (0, 1), (2, 3))
                normalise(t, 2, chain)
                between(2, (0, 1), (2, 3))
                normalise(t, 3, chain)
                between(3, (0, 1, 2), (3,))

            groups(dve, body, s_chain, (2 * GS, 2 * GS))


def layer0_attention(nc, k):
    heads_attention(nc, k, "l0x", True, 0)


def layer1_attention(nc, k):
    heads_attention(nc, k, "l1x", False, 1)


def layer0_ffn(nc, k):
    with ExitStack() as ctx:
        sb, sem = k.local(ctx, "l0f")
        ln_tensors(k, sb, sem)
        w = k.w
        wsum = sb("abs_sums", [P, 2], F32)
        wmean = sb("abs_mean", [P, 2], F32)
        winv = sb("abs_rmean", [P, 2], F32)
        wr = sb("w_steps", [P, 2, HID], F32)
        w1q = sb("w1q", [P, HID], BF16)
        w2q = sb("w2q", [P, NHB, P], BF16)
        amax = sb("amax", [P, GS], F32)
        qs = sb("q_scale", [P, GS], F32)
        dq = sb("q_step", [P, GS], F32)
        xr = sb("xn_steps", [P, GS, P], F32)
        xq = sb("xq", [P, GS, P], BF16)
        xqT = sb("xqT", [P, T], BF16)
        srow = sb("q_step_rows", [P, GS, P], F32)
        hs = sb("h_scaled", [P, 2, GS, P], F32)
        cv = sb("convolved", [P, 2, GS, P], F32)
        hT = sb("hT", [P, NHB, T], F32)
        hm = sb("h_absmax", [P, T], F32)
        qr = sb("q2_steps", [P, NHB, T], F32)
        q2 = sb("q2", [P, NHB, T], BF16)
        top = sb("row_scales", [P, 6, GS], F32)
        gw = sb("tanh_g_w2_step", [P, 1], F32)
        bankX, bankR, bankH0, bankH1, bankM, bankS, bankY, bankT = (k.bank(i) for i in range(8))
        bankH = [bankH0, bankH1]

        s_prep = sem("prep_step")
        s_wsum = sem("abs_sums_spread")
        s_chain = sem("dve_step")
        s_first = sem("first_quant_step")
        s_quant = sem("xq_ready")
        r_qT = Ring(sem("xqT_in_psum"), 1)
        s_qT = sem("xqT_ready")
        s_srow = sem("q_step_spread")
        s_srs = sem("q_step_rows_ready")
        s_h = sem("h_in_psum")
        r_hs = Ring(sem("h_scaled_ready"), 2)
        s_cv = sem("convolved_ready")
        r_act = Ring(sem("hT_ready"), 2)
        s_hm = sem("h_absmax_ready")
        s_hmT = sem("h_absmaxT_in_psum")
        s_sc = sem("row_scales_ready")
        s_scr = sem("row_scales_spread")
        s_q2 = sem("q2_ready")
        r_y = Ring(sem("y_in_psum"), 1)
        r_out = Ring(sem("x_updated"), 1)

        block = ctx.enter_context(nc.Block())

        @block.tensor
        def _(pe):
            for r in (r_qT, k.r_xnT_used, r_y):
                r.grant(pe)
            k.wait_weights(pe, "l0f")
            pe.wait_ge(s_prep, 1)
            pe.matmul(bankM[:, 0:2], k.ones[:, :], wsum[:, :], start=True, stop=True).then_inc(s_wsum, 1)
            pe.wait_ge(s_prep, 6)

            def turn_q(g):
                pe.wait_ge(s_quant, g + 1)
                for c in range(GS):
                    pe.matmul(bankS[:, seq(c)], bcast(dq[:, c:c + 1], [P, P]), k.ident[:, :], start=True, stop=True)
                for c in range(GS):
                    ins = pe.transpose(bankX.bitcast(BF16)[:, seq(c)], xq[:, c, :], k.ident_bf[:, :])
                ins.then_inc(r_qT.sem, 1)

            turn_q(0)

            def body(g, par, more, chain):
                pe.wait_ge(s_qT, g + 1)
                for n in range(NHB):
                    r_hs.wait_free(pe, g * NHB + n)
                    pe.matmul(bankH[n % 2][:, :], w1q[:, seq(n)], xqT[:, :], start=True, stop=True).then_inc(s_h, 1)
                pe.wait_ge(s_hm, g + 1)
                for c in range(GS):
                    ins = pe.transpose(bankT[:, seq(c)], hm[:, seq(c)], k.ident[:, :])
                ins.then_inc(s_hmT, 1)
                pe.wait_ge(s_sc, g + 1)
                for c in range(GS):
                    ins = pe.matmul(bankR[:, seq(c)], bcast(top[:, 3, c:c + 1], [P, P]), k.ident[:, :],
                                    start=True, stop=True)
                ins.then_inc(s_scr, 1)
                if more:
                    turn_q(g + 1)
                pe.wait_ge(s_q2, g + 1)
                r_out.wait_free(pe, g)
                for c in range(GS):
                    for n in range(NHB):
                        ins = pe.matmul(bankY[:, seq(c)], q2[:, n, seq(c)], w2q[:, n, :], start=(n == 0),
                                        stop=(n == NHB - 1))
                ins.then_inc(r_y.sem, 1)

            groups(pe, body)

        @block.scalar
        def _(act):
            r_act.grant(act)

            def body(g, par, more, chain):
                r_qT.wait_done(act, g)
                act.activation(xqT[:, :], bankX.bitcast(BF16)[:, 0:T], ACT.Copy).then_inc(s_qT, 1)
                act.activation(srow[:, :, :], bankS.rearrange("p (c t) -> p c t", c=GS), ACT.Copy)\
                   .then_inc(s_srs, 1)
                for n in range(NHB):
                    act.wait_ge(s_cv, g * NHB + n + 1)
                    act.activation(hT[:, n, :], cv[:, n % 2, :, :].rearrange("p c t -> p (c t)"), ACT.Silu,
                                   bias=w["l0f_cb"][:, n:n + 1]).then_inc(r_act.sem, 1)

            groups(act, body)

        @block.gpsimd
        def _(pool):
            ln_rstd(k, pool, 0)
            groups(pool, lambda g, par, more, chain: ln_rstd(k, pool, g + 1) if more else None)

        @block.vector
        def _(dve):
            r_hs.grant(dve)
            r_out.grant(dve)
            k.wait_weights(dve, "l0f")
            prep = Chain(dve, s_prep, 0, 0)
            dve.tensor_reduce(wsum[:, 0:1], w["l0f_w1"][:, :], AX, ALU.add, apply_absolute_value=True)
            prep(dve.tensor_reduce(wsum[:, 1:2], w["l0f_w2"][:, :, :].rearrange("p n d -> p (n d)"), AX, ALU.add,
                                   apply_absolute_value=True))
            dve.wait_ge(s_wsum, 1)
            prep(dve.tensor_scalar(wmean[:, :], bankM[:, 0:2], 1.0 / (P * HID), 1e-5, ALU.mult, ALU.max))
            prep(dve.reciprocal(winv[:, :], wmean[:, :]))
            dve.tensor_scalar(wr[:, 0, :], w["l0f_w1"][:, :], winv[:, 0:1], MAGIC, ALU.mult, ALU.add)
            prep(dve.tensor_scalar(wr[:, 1, :], w["l0f_w2"][:, :, :].rearrange("p n d -> p (n d)"), winv[:, 1:2],
                                   MAGIC, ALU.mult, ALU.add))
            prep(dve.tensor_scalar(wr[:, :, :], wr[:, :, :], -MAGIC, 1.0, ALU.add, ALU.min))
            dve.tensor_scalar(w1q[:, :], wr[:, 0, :], -1.0, None, ALU.max)
            dve.tensor_scalar(gw[:, :], k.tanh_g[:, 4:5], wmean[:, 1:2], 1.0 / 127.0, ALU.mult, ALU.mult)
            prep(dve.tensor_scalar(w2q[:, :, :].rearrange("p n d -> p (n d)"), wr[:, 1, :], -1.0, None, ALU.max))

            def quantise(g, chain):
                dve.wait_ge(s_done_xn, g + 1)
                chain(dve.tensor_reduce(amax[:, :], k.xn[:, :, :], AX, ALU.max, apply_absolute_value=True))
                chain(dve.tensor_scalar(amax[:, :], amax[:, :], 1e-5, None, ALU.max))
                chain(dve.reciprocal(qs[:, :], amax[:, :]))
                chain(dve.tensor_scalar(qs[:, :], qs[:, :], 127.0, None, ALU.mult))
                r_qT.wait_free(dve, g)
                dve.tensor_scalar(dq[:, :], amax[:, :], 1.0 / 127.0, wmean[:, 0:1], ALU.mult, ALU.mult)
                for c in range(GS):
                    ins = dve.tensor_scalar(xr[:, c, :], k.xn[:, c, :], qs[:, c:c + 1], MAGIC, ALU.mult, ALU.add)
                chain(ins)
                dve.tensor_scalar(xq[:, :, :], xr[:, :, :], -MAGIC, None, ALU.add).then_inc(s_quant, 1)

            s_done_xn = k.s_xn
            k.r_xnT_psum = r_qT
            ln_stats(k, dve, 0)
            ln_apply(k, dve, 0)
            quantise(0, Chain(dve, s_first, 0, 0))

            def body(g, par, more, chain):
                dve.wait_ge(s_srs, g + 1)
                for n in range(NHB):
                    h, y = hs[:, n % 2, :, :], cv[:, n % 2, :, :]
                    tap = lambda i: w["l0f_cw"][:, 3 * n + i:3 * n + i + 1]
                    dve.wait_ge(s_h, g * NHB + n + 1)
                    ins = dve.tensor_tensor(h, bankH[n % 2].rearrange("p (c t) -> p c t", c=GS), srow[:, :, :],
                                            ALU.mult)
                    ins.then_inc(r_hs.sem, 1)
                    r_hs.wait_done(dve, g * NHB + n)
                    r_act.wait_free(dve, g * NHB + n)
                    chain(dve.tensor_scalar(y, h, tap(1), None, ALU.mult))
                    chain(dve.scalar_tensor_tensor(y[:, :, 1:P], h[:, :, 0:P - 1], tap(0), y[:, :, 1:P],
                                                   ALU.mult, ALU.add))
                    dve.scalar_tensor_tensor(y[:, :, 0:P - 1], h[:, :, 1:P], tap(2), y[:, :, 0:P - 1],
                                             ALU.mult, ALU.add).then_inc(s_cv, 1)
                if more:
                    ln_stats(k, dve, g + 1)
                r_act.wait_done(dve, g * NHB + 3)
                dve.tensor_reduce(hm[:, :], hT[:, :, :].rearrange("p n t -> p t n"), AX, ALU.max,
                                  apply_absolute_value=True).then_inc(s_hm, 1)
                if more:
                    ln_apply(k, dve, g + 1)
                dve.wait_ge(s_hmT, g + 1)
                chain(dve.tensor_reduce(top[:, 0, :], bankT.rearrange("p (c t) -> p c t", c=GS), AX, ALU.max,
                                        apply_absolute_value=True))
                chain(dve.tensor_scalar(top[:, 1, :], top[:, 0, :], 1e-5, None, ALU.max))
                chain(dve.reciprocal(top[:, 2, :], top[:, 1, :]))
                dve.tensor_scalar(top[:, 3, :], top[:, 2, :], 127.0, None, ALU.mult).then_inc(s_sc, 1)
                chain(dve.tensor_scalar(top[:, 4, :], top[:, 1, :], gw[:, 0:1], None, ALU.mult))
                if more:
                    quantise(g + 1, chain)
                dve.wait_ge(s_scr, g + 1)
                rows = bcast(bankR.unsqueeze(1), [P, NHB, T])
                chain(dve.tensor_tensor(qr[:, :, :], hT[:, :, :], rows, ALU.mult))
                chain(dve.tensor_scalar(qr[:, :, :], qr[:, :, :], MAGIC, None, ALU.add))
                r_y.wait_free(dve, g)
                dve.tensor_scalar(q2[:, :, :], qr[:, :, :], -MAGIC, None, ALU.add).then_inc(s_q2, 1)
                r_y.wait_done(dve, g)
                for c in range(GS):
                    xc = k.x_sb[:, bass.ds((g * GS + c) * P, P)]
                    ins = dve.scalar_tensor_tensor(xc, bankY[:, seq(c)], top[:, 4, c:c + 1], xc, ALU.mult, ALU.add)
                ins.then_inc(r_out.sem, 1)

            groups(dve, body, s_chain, (38, 33))


NE1, RANK = 3, 8
NZ = NE1 * RANK
NZL = NZ + NE1
ZW = 32


def layer1_ffn(nc, k):
    with ExitStack() as ctx:
        sb, sem = k.local(ctx, "l1f")
        ln_tensors(k, sb, sem)
        shifted = sb("shifted", [P, GS, NE1], F32)
        expd = sb("expd", [P, GS, NE1], F32)
        small = sb("small", [P, 4, GS], F32)
        gate = sb("gate", [P, GS, NE1], F32)
        zg = sb("zg", [P, GS, ZW], F32)
        zgT = sb("zgT", [P, T], F32)
        hT = sb("hT", [P, NHB, T], F32)
        bankX, bankZ, bankZT, bankH, bankY, bankR = (
            k.bank(0), k.bank(1), k.bank(2), [k.bank(3), k.bank(4)], k.banks(5, 2), k.bank(7))
        zview = bankZ.rearrange("p (c w) -> p c w", c=GS)[:, :, 0:NZL]
        WY = P + NZL
        yview = bankY.rearrange("p (a w) -> p a w", a=2)[:, :, 0:2 * WY].rearrange("p a (b w) -> p a b w", b=2)

        s_const = sem("zg_const_ready")
        s_chain = sem("dve_step")
        s_z = sem("z_in_psum")
        s_shift = sem("logits_shifted")
        s_exp = sem("gates_exp")
        s_zg = sem("zg_ready")
        r_zT = Ring(sem("zgT_in_psum"), 1)
        r_zTs = Ring(sem("zgT_ready"), 1)
        r_lora = Ring(sem("lora_done"), 1)
        s_h = sem("h_in_psum")
        r_h = Ring(sem("h_ready"), 2)
        r_y = Ring(sem("y_in_psum"), 1)
        r_out = Ring(sem("x_updated"), 1)

        block = ctx.enter_context(nc.Block())

        @block.tensor
        def _(pe):
            r_zT.grant(pe)
            r_lora.grant(pe)
            r_y.grant(pe)
            k.r_xnT_psum.grant(pe)
            k.r_xnT_used.grant(pe)
            k.wait_weights(pe, "l1f")
            ln_transpose(k, pe, 0, bankX)

            def turn_zg(unit):
                pe.wait_ge(s_zg, unit + 1)
                r_zTs.wait_free(pe, unit)
                for c in range(GS):
                    ins = pe.transpose(bankZT[0:ZW, seq(c)], zg[:, c, :], k.ident[:, :])
                ins.then_inc(r_zT.sem, 1)

            def body(g, par, more, chain):
                xnT = k.xnT[:, par, :]
                k.r_xnT.wait_done(pe, g)
                for c in range(GS):
                    ins = pe.matmul(zview[:, c, :], xnT[:, seq(c)], k.w["l1f_ar1"][:, :], start=True, stop=True)
                ins.then_inc(s_z, 1)

                def base(n):
                    r_h.wait_free(pe, g * NHB + n)
                    return pe.matmul(bankH[n % 2][:, :], k.w["l1f_w1"][:, seq(n)], xnT, start=True, stop=False)

                def lora(n):
                    return pe.matmul(bankH[n % 2][:, :], k.w["l1f_b1"][:, seq(n)], zgT[:, :],
                                     start=False, stop=True)

                base(0)
                base(1)
                turn_zg(2 * g)
                r_zTs.wait_done(pe, 2 * g)
                lora(0).then_inc(s_h, 1)
                lora(1).then_inc(s_h, 1)
                base(2)
                lora(2).then_inc(s_h, 1)
                base(3).then_inc(k.r_xnT_used.sem, 1)
                ins = lora(3)
                ins.then_inc(s_h, 1)
                if more:
                    ln_transpose(k, pe, g + 1, bankX)
                r_out.wait_free(pe, g)
                r_h.wait_done(pe, g * NHB + NHB - 1)
                for c in range(GS):
                    for n in range(NHB):
                        ins = pe.matmul(yview[:, c // 2, c % 2, :], hT[:, n, seq(c)], k.w["l1f_w2ar"][:, n, :],
                                        start=(n == 0), stop=(n == NHB - 1))
                ins.then_inc(r_y.sem, 1)
                turn_zg(2 * g + 1)
                r_zTs.wait_done(pe, 2 * g + 1)
                for c in range(GS):
                    ins = pe.matmul(bankR[:, seq(c)], zgT[:, seq(c)], k.w["l1f_b2"][:, :], start=True, stop=True)
                ins.then_inc(r_lora.sem, 1)

            groups(pe, body)

        @block.scalar
        def _(act):
            r_zTs.grant(act)
            r_h.grant(act)
            k.r_xnT.grant(act)
            act.wait_ge(s_const, 2)
            ln_evacuate(k, act, 0, 0, bankX)

            def gates(unit):
                act.wait_ge(s_shift, unit + 1)
                act.activation(expd[:, :, :], shifted[:, :, :], ACT.Exp).then_inc(s_exp, 1)
                r_zT.wait_done(act, unit)

            def body(g, par, more, chain):
                gates(2 * g)
                r_lora.wait_free(act, g)
                act.activation(zgT[0:ZW, :], bankZT[0:ZW, :], ACT.Copy).then_inc(r_zTs.sem, 1)
                r_y.wait_free(act, g)
                for n in range(NHB):
                    act.wait_ge(s_h, g * NHB + n + 1)
                    act.activation(hT[:, n, :], bankH[n % 2][:, :], ACT.Relu).then_inc(r_h.sem, 1)
                if more:
                    ln_evacuate(k, act, g + 1, 1 - par, bankX)
                gates(2 * g + 1)
                act.activation(zgT[0:ZW, :], bankZT[0:ZW, :], ACT.Copy).then_inc(r_zTs.sem, 1)

            groups(act, body)

        @block.gpsimd
        def _(pool):
            pool.memset(zgT[:, :], 0.0).then_inc(s_const, 1)
            ln_rstd(k, pool, 0)
            groups(pool, lambda g, par, more, chain: ln_rstd(k, pool, g + 1) if more else None)

        @block.vector
        def _(dve):
            r_out.grant(dve)
            dve.memset(zg[:, :, NZ + 1:ZW], 0.0)
            dve.memset(zg[:, :, NZ:NZ + 1], 1.0).then_inc(s_const, 1)
            ln_stats(k, dve, 0)
            ln_apply(k, dve, 0)

            def gates(unit, chain, logits, zs):
                chain(dve.tensor_reduce(small[:, 0, :], logits, AX, ALU.max))
                mx = small[:, 0, :].rearrange("p (a b) -> p a b", a=logits.shape[1]) if len(logits.shape) == 4 \
                    else small[:, 0, :]
                sh = shifted[:, :, :]
                if len(logits.shape) == 4:
                    sh = shifted[:, :, :].rearrange("p (a b) e -> p a b e", a=2)
                dve.tensor_tensor(sh, logits, bcast(mx.unsqueeze(len(mx.shape)), logits.shape),
                                  ALU.subtract).then_inc(s_shift, 1)
                dve.wait_ge(s_exp, unit + 1)
                chain(dve.tensor_reduce(small[:, 1, :], expd[:, :, :], AX, ALU.add))
                chain(dve.tensor_scalar(small[:, 2, :], small[:, 1, :], float(RANK), None, ALU.mult))
                chain(dve.reciprocal(small[:, 3, :], small[:, 2, :]))
                chain(dve.tensor_tensor(gate[:, :, :], expd[:, :, :],
                                        bcast(small[:, 3, :].unsqueeze(2), [P, GS, NE1]), ALU.mult))
                r_zT.wait_free(dve, unit)
                n = GS // len(zs)
                for a, z in enumerate(zs):
                    part = slice(a * n, a * n + n)
                    ins = dve.tensor_tensor(zg[:, part, 0:NZ].rearrange("p c (e r) -> p c e r", e=NE1), z,
                                            bcast(gate[:, part, :].unsqueeze(3), [P, n, NE1, RANK]), ALU.mult)
                ins.then_inc(s_zg, 1)

            def body(g, par, more, chain):
                dve.wait_ge(s_z, g + 1)
                gates(2 * g, chain, zview[:, :, NZ:NZL],
                      [zview[:, :, 0:NZ].rearrange("p c (e r) -> p c e r", e=NE1)])
                if more:
                    ln_stats(k, dve, g + 1)
                    ln_apply(k, dve, g + 1)
                r_y.wait_done(dve, g)
                gates(2 * g + 1, chain, yview[:, :, :, P + NZ:WY],
                      [yview[:, a, :, P:P + NZ].rearrange("p c (e r) -> p c e r", e=NE1) for a in range(2)])
                for a in range(2):
                    xs = k.x_sb[:, bass.ds((g * GS + 2 * a) * P, 2 * P)].rearrange("p (c d) -> p c d", c=2)
                    ins = dve.scalar_tensor_tensor(xs, yview[:, a, :, 0:P], k.tanh_g[:, 5:6], xs, ALU.mult, ALU.add)
                chain(ins)
                r_lora.wait_done(dve, g)
                xs = k.x_sb[:, bass.ds(g * T, T)]
                dve.scalar_tensor_tensor(xs, bankR[:, :], k.tanh_g[:, 5:6], xs, ALU.mult, ALU.add)\
                   .then_inc(r_out.sem, 1)

            groups(dve, body, s_chain, 22)


def layer2_attention(nc, k):
    with ExitStack() as ctx:
        sb, sem = k.local(ctx, "l2x")
        ln_tensors(k, sb, sem)
        ctxT = sb("ctxT", [P, 2, T], F32)
        ctok = sb("ctx_tok", [P, 2, T], F32)
        hwT = sb("h_w3_plus_w2_T", [P, T], F32)
        nmax = sb("minus_max", [P, GS], F32)
        total = sb("total", [P, GS], F32)
        rtot = sb("rtot", [P, GS], F32)
        probs = sb("probs", [P, GS, P], F32)
        attn = sb("attn", [P, GS, P], F32)
        attnT = sb("attnT", [P, T], F32)
        pool_max = sb("row_max", [P, GS], F32)
        pool_nmax = sb("pool_minus_max", [P, GS], F32)
        pool_exp = sb("pool_exp", [P, GS, P], F32)
        pool_tot = sb("pool_total", [P, GS], F32)
        pool_rtot = sb("pool_rtot", [P, GS], F32)
        weighed = sb("weighed", [P, GS, P], F32)
        hsum = sb("h_sum", [P, GS], F32)
        hbar = sb("h_bar", [P, GS], F32)
        aT = sb("aT", [P, T], F32)
        haT = sb("h_times_aT", [P, T], F32)
        hhT = sb("h_times_hbarT", [P, GS, P], F32)
        gb = sb("tanh_g_b", [P, GS, P], F32)
        bankX, bankS, bankE, bankAT, bankA, bankR, bankO = (k.bank(i) for i in range(7))
        w = k.w

        s_chain = sem("dve_step")
        s_gb = sem("bias_ready")
        r_ctx = Ring(sem("ctx_used"), 2)
        s_ctx = [sem(f"ctx_in_{p}") for p in range(2)]
        r_hw = Ring(sem("hwT_ready"), 1)
        r_s = Ring(sem("sim_in_psum"), 1)
        s_nmax = sem("minus_max_ready")
        s_p = sem("probs_ready")
        s_attn = sem("attn_ready")
        r_at = Ring(sem("attnT_in_psum"), 1)
        s_at = sem("attnT_ready")
        s_rmax = sem("row_max_ready")
        s_r = sem("row_max_spread")
        s_pn = sem("pool_minus_max_ready")
        s_pe = sem("pool_exp_ready")
        s_a = sem("aT_in_psum")
        s_aT = sem("aT_ready")
        s_haT = sem("haT_ready")
        s_feat = sem("feats_ready")
        r_o = Ring(sem("out_in_psum"), 1)
        r_out = Ring(sem("x_updated"), 1)

        block = ctx.enter_context(nc.Block())

        @block.sync
        def _(sp):
            with sp.Fori(0, NG // 2) as it:
                for par in range(2):
                    g = 2 * it + par
                    r_ctx.wait_free(sp, g)
                    for buf, src in ((ctxT, "ctxT"), (ctok, "ctx_tok")):
                        sp.dma_start(buf[:, par, :], k.dram[src][:, bass.ds(g * T, T)]).then_inc(s_ctx[par], 16)

        @block.tensor
        def _(pe):
            for r in (k.r_xnT_psum, k.r_xnT_used, r_ctx, r_s, r_at, r_o):
                r.grant(pe)
            k.wait_weights(pe, "l2x")
            ln_transpose(k, pe, 0, bankX)

            def body(g, par, more, chain):
                xnT, cT = k.xnT[:, par, :], ctxT[:, par, :]
                pe.wait_ge(s_ctx[par], (g - par) * 16 + 32)
                r_hw.wait_done(pe, g)
                r_out.wait_free(pe, g)
                for c in range(GS):
                    pe.matmul(bankE[:, c:c + 1], xnT[:, seq(c)], w["l2x_w1"][:, :], start=True, stop=True)
                for c in range(GS):
                    ins = pe.matmul(bankS[:, seq(c)], hwT[:, seq(c)], cT[:, seq(c)], start=True, stop=True)
                ins.then_inc(r_s.sem, 1)
                pe.wait_ge(s_rmax, g + 1)
                for c in range(GS):
                    ins = pe.matmul(bankR[:, seq(c)], bcast(pool_max[:, c:c + 1], [P, P]), k.ident[:, :],
                                    start=True, stop=True)
                ins.then_inc(s_r, 1)
                if more:
                    ln_transpose(k, pe, g + 1, bankX)
                pe.wait_ge(s_attn, g + 1)
                for c in range(GS):
                    ins = pe.transpose(bankAT[:, seq(c)], attn[:, c, :], k.ident[:, :])
                ins.then_inc(r_at.sem, 1)
                pe.wait_ge(s_at, g + 1)
                for c in range(GS):
                    ins = pe.matmul(bankA[:, seq(c)], ctok[:, par, seq(c)], attnT[:, seq(c)], start=True, stop=True)
                ins.then_inc(s_a, 1)
                pe.wait_ge(s_aT, g + 1)
                pe.wait_ge(s_feat, g + 1)
                for c in range(GS):
                    for n, f in enumerate((xnT[:, seq(c)], aT[:, seq(c)], haT[:, seq(c)], hhT[:, c, :])):
                        ins = pe.matmul(bankO[:, seq(c)], f, w["l2x_wqv"][:, n, :], start=(n == 0), stop=(n == 3))
                ins.then_inc(r_o.sem, 1)
                r_o.wait_done(pe, g)
                pe.sem_inc(r_ctx.sem, 1)
                pe.sem_inc(k.r_xnT_used.sem, 1)

            groups(pe, body)

        @block.scalar
        def _(act):
            for r in (k.r_xnT,):
                r.grant(act)
            ln_evacuate(k, act, 0, 0, bankX)

            def body(g, par, more, chain):
                act.wait_ge(s_nmax, g + 1)
                for c in range(GS):
                    ins = act.activation(probs[:, c, :], bankS[:, seq(c)], ACT.Exp, bias=nmax[:, c:c + 1],
                                         accum_out=total[:, c:c + 1])
                ins.then_inc(s_p, 1)
                act.wait_ge(s_pn, g + 1)
                for c in range(GS):
                    ins = act.activation(pool_exp[:, c, :], bankR[:, seq(c)], ACT.Exp,
                                         bias=pool_nmax[:, c:c + 1], accum_out=pool_tot[:, c:c + 1])
                ins.then_inc(s_pe, 1)
                if more:
                    ln_evacuate(k, act, g + 1, 1 - par, bankX)
                r_at.wait_done(act, g)
                act.activation(attnT[:, :], bankAT[:, :], ACT.Copy).then_inc(s_at, 1)
                act.wait_ge(s_haT, g + 1)
                r_o.wait_free(act, g)
                act.activation(aT[:, :], bankA[:, :], ACT.Copy).then_inc(s_aT, 1)

            groups(act, body)

        @block.gpsimd
        def _(pool):
            ln_rstd(k, pool, 0)
            groups(pool, lambda g, par, more, chain: ln_rstd(k, pool, g + 1) if more else None)

        @block.vector
        def _(dve):
            r_hw.grant(dve)
            r_out.grant(dve)
            k.wait_weights(dve, "l2x")
            for c in range(GS):
                ins = dve.tensor_scalar(gb[:, c, :], w["l2x_bqv"][:, :], k.tanh_g[:, 2:3], None, ALU.mult)
            ins.then_inc(s_gb, 1)
            dve.wait_ge(s_gb, 1)
            ln_stats(k, dve, 0)
            ln_apply(k, dve, 0)

            def body(g, par, more, chain):
                xnT = k.xnT[:, par, :]
                xnT3 = xnT.rearrange("p (c t) -> p c t", c=GS)
                k.r_xnT.wait_done(dve, g)
                r_s.wait_free(dve, g)
                dve.tensor_scalar(hwT[:, :], xnT, w["l2x_w3"][:, :], w["l2x_w2"][:, :], ALU.mult, ALU.add)\
                   .then_inc(r_hw.sem, 1)
                r_s.wait_done(dve, g)
                dve.tensor_reduce(nmax[:, :], bankS.rearrange("p (c t) -> p c t", c=GS), AX, ALU.max,
                                  negate=True).then_inc(s_nmax, 1)
                dve.wait_ge(s_nmax, g + 1)
                dve.scalar_tensor_tensor(pool_max[:, :], bankE[:, 0:GS], w["l2x_bsim"][:, 0:1], nmax[:, :],
                                         ALU.add, ALU.subtract).then_inc(s_rmax, 1)
                if more:
                    ln_stats(k, dve, g + 1)
                dve.wait_ge(s_p, g + 1)
                chain(dve.reciprocal(rtot[:, :], total[:, :]))
                dve.tensor_tensor(attn[:, :, :], probs[:, :, :], bcast(rtot[:, :].unsqueeze(2), [P, GS, P]),
                                  ALU.mult).then_inc(s_attn, 1)
                dve.wait_ge(s_r, g + 1)
                dve.tensor_reduce(pool_nmax[:, :], bankR.rearrange("p (c t) -> p c t", c=GS), AX, ALU.max,
                                  negate=True).then_inc(s_pn, 1)
                if more:
                    ln_apply(k, dve, g + 1)
                xs = k.x_sb[:, bass.ds(g * T, T)]
                dve.tensor_tensor(xs, xs, gb[:, :, :].rearrange("p c d -> p (c d)"), ALU.add)
                dve.wait_ge(s_pe, g + 1)
                chain(dve.tensor_tensor(weighed[:, :, :], xnT3, pool_exp[:, :, :], ALU.mult))
                dve.tensor_reduce(hsum[:, :], weighed[:, :, :], AX, ALU.add)
                chain(dve.reciprocal(pool_rtot[:, :], pool_tot[:, :]))
                chain(dve.tensor_tensor(hbar[:, :], hsum[:, :], pool_rtot[:, :], ALU.mult))
                r_o.wait_free(dve, g)
                dve.tensor_tensor(hhT[:, :, :], xnT3, bcast(hbar[:, :].unsqueeze(2), [P, GS, P]), ALU.mult)\
                   .then_inc(s_feat, 1)
                dve.wait_ge(s_a, g + 1)
                dve.tensor_tensor(haT[:, :], bankA[:, :], xnT, ALU.mult).then_inc(s_haT, 1)
                r_o.wait_done(dve, g)
                dve.scalar_tensor_tensor(xs, bankO[:, :], k.tanh_g[:, 2:3], xs, ALU.mult, ALU.add)\
                   .then_inc(r_out.sem, 1)

            groups(dve, body, s_chain, 8)


NE2 = 8
NTILE = NSEQ + NE2
MARGIN = 63.5


def tiles(eng, body):
    with eng.Fori(0, NTILE // 2 - 2) as it:
        for par in range(2):
            body(2 * it + par, par)
    for u in range(NTILE - 4, NTILE):
        body(u, u % 2)


def exists(u):
    return not isinstance(u, int) or u < NTILE


def layer2_ffn(nc, k):
    with ExitStack() as ctx:
        sb, sem = k.local(ctx, "l2f")
        ln_tensors(k, sb, sem)
        w = k.w
        all_tokens = [P, NSEQ, NE2]
        zeros = sb("zeros", [P, P], F32)
        h_all = sb("h_all", [P, NSEQ * P], F32)
        lg = sb("logits", all_tokens, F32)
        sh = sb("logits_shifted", all_tokens, F32)
        ex = sb("gate_exp", all_tokens, F32)
        ta = sb("select", all_tokens, F32)
        hot = sb("chosen", all_tokens, F32)
        top = sb("tops", [P, 5, NSEQ], F32)
        gate = sb("tanh_g_gates", [P, NSEQ], F32)
        upto = [sb(f"tokens_up_to_{i}", all_tokens, F32) for i in range(2)]
        tot = sb("tokens_of_sequence", all_tokens, F32)
        cnt = sb("expert_tiles", [P, NE2], F32)
        ends = [sb(f"tiles_up_to_{i}", [P, NE2], F32) for i in range(2)]
        base = sb("expert_base", [P, NE2], F32)
        pos_f = sb("pos_f32", [P, NSEQ], F32)
        pos = sb("pos", [P, NSEQ], I32)
        le = sb("tile_past_expert", [P, NTILE, NE2], F32)
        te_f = sb("tile_expert_f32", [P, NTILE], F32)
        te = sb("tile_expert", [P, NTILE], I32)
        xt = sb("x_tile", [P, 2, P], F32)
        xT = sb("xT_tile", [P, 2, P], F32)
        hp = sb("h_tile", [P, 2, HID], F32)
        hT = sb("hT_tile", [P, 2, HID], F32)
        yt = sb("y_tile", [P, 2, P], F32)
        back = sb("y_of_token", [P, NSEQ, P], F32)
        sorted_x = nc.dram_tensor("l2f_sorted_x", (NTILE * P, P), F32).ap()
        sorted_y = nc.dram_tensor("l2f_sorted_y", (NTILE * P, P), F32).ap()
        bankX, bankM = k.bank(0), k.bank(7)
        bankU, bankH, bankY = [k.bank(1), k.bank(2)], [k.bank(3), k.bank(4)], [k.bank(5), k.bank(6)]

        s_zeros = sem("zeros_ready")
        s_zeroed = sem("sorted_x_zeroed")
        s_step = sem("dve_step")
        s_logits = sem("logits_in_psum")
        r_logits = Ring(sem("logits_ready"), 1)
        s_all = sem("all_logits_ready")
        s_shift = sem("logits_shifted_ready")
        s_ex = sem("gate_exp_ready")
        s_hot = sem("chosen_ready")
        s_count = sem("counts_in_psum")
        s_pos = sem("pos_ready")
        s_te = sem("tile_expert_ready")
        s_scatter = sem("rows_scattered")
        s_x = [sem(f"x_tile_in_{p}") for p in range(2)]
        r_turn = Ring(sem("x_tile_turned"), 2)
        r_xT = Ring(sem("xT_tile_ready"), 1)
        r_up = Ring(sem("h_in_psum"), 2)
        r_hp = Ring(sem("h_tile_ready"), 2)
        r_turnh = Ring(sem("h_tile_turned"), 2)
        r_hT = Ring(sem("hT_tile_ready"), 2)
        r_y = Ring(sem("y_in_psum"), 2)
        r_yt = Ring(sem("y_tile_ready"), 2)
        s_out = [sem(f"y_tile_out_{p}") for p in range(2)]
        s_back = [sem(f"rows_gathered_{i}") for i in range(NG)]

        block = ctx.enter_context(nc.Block())

        @block.sync
        def _(sp):
            sp.wait_ge(s_zeros, 1)
            sp.dma_start(sorted_x.rearrange("(u p) d -> p u d", p=P), bcast(zeros[:, :].unsqueeze(1), [P, NTILE, P]))\
              .then_inc(s_zeroed, 16)
            sp.wait_ge(s_scatter, 16 * NSEQ)

            def load(u, par):
                r_turn.wait_free(sp, u)
                sp.dma_start(xt[:, par, :], sorted_x[bass.ds(u * P, P), :]).then_inc(s_x[par], 16)

            tiles(sp, load)

        @block.tensor
        def _(pe):
            for r in (k.r_xnT_psum, k.r_xnT_used, r_turn, r_up, r_turnh, r_y):
                r.grant(pe)
            k.wait_weights(pe, "l2f")
            ln_transpose(k, pe, 0, bankX)

            def route(g, par, more, chain):
                k.r_xnT.wait_done(pe, g)
                r_logits.wait_free(pe, g)
                for c in range(GS):
                    ins = pe.matmul(bankM[:, c * NE2:(c + 1) * NE2], k.xnT[:, par, seq(c)], w["l2f_router"][:, :],
                                    start=True, stop=True)
                ins.then_inc(s_logits, 1)
                if more:
                    ln_transpose(k, pe, g + 1, bankX)
                r_logits.wait_done(pe, g)
                pe.sem_inc(k.r_xnT_used.sem, 1)

            groups(pe, route)

            pe.wait_ge(s_hot, 1)
            flat = hot[:, :, :].rearrange("p c e -> p (c e)")
            pe.matmul(bankY[0][:, 0:NSEQ * NE2], k.before[:, :], flat, start=True, stop=True)
            pe.matmul(bankY[1][:, 0:NSEQ * NE2], k.ones[:, :], flat, start=True, stop=True).then_inc(s_count, 1)
            pe.wait_ge(s_te, 1)

            def expert(u):
                return pe.value_load(te[0:1, bass.ds(u, 1)], min_val=0, max_val=NE2 - 1)

            def turn_x(u, par):
                pe.wait_ge(s_x[par], (u - par) * 8 + 16)
                r_xT.wait_free(pe, u)
                pe.transpose(bankX[:, 0:P], xt[:, par, :], k.ident[:, :]).then_inc(r_turn.sem, 1)

            def up(u, par):
                e = expert(u)
                r_xT.wait_done(pe, u)
                r_hp.wait_free(pe, u)
                pe.matmul(bankU[par][:, :], xT[:, par, :], w["l2f_w1"][:, bass.ds(e * HID, HID)], start=True,
                          stop=True).then_inc(r_up.sem, 1)

            def turn_h(u, par):
                r_hp.wait_done(pe, u)
                r_hT.wait_free(pe, u)
                for n in range(NHB):
                    ins = pe.transpose(bankH[par][:, seq(n)], hp[:, par, seq(n)], k.ident[:, :])
                ins.then_inc(r_turnh.sem, 1)

            def down(u, par):
                e = expert(u)
                r_hT.wait_done(pe, u)
                r_yt.wait_free(pe, u)
                for n in range(NHB):
                    ins = pe.matmul(bankY[par][:, 0:P], hT[:, par, seq(n)], w["l2f_w2"][:, bass.ds(e * HID + n * P, P)],
                                    start=(n == 0), stop=(n == NHB - 1))
                ins.then_inc(r_y.sem, 1)

            turn_x(0, 0)
            up(0, 0)
            turn_x(1, 1)
            up(1, 1)
            turn_x(2, 0)
            turn_h(0, 0)

            def body(u, par):
                if exists(u + 3):
                    turn_x(u + 3, 1 - par)
                if exists(u + 2):
                    up(u + 2, par)
                if exists(u + 1):
                    turn_h(u + 1, 1 - par)
                down(u, par)

            tiles(pe, body)

        @block.scalar
        def _(act):
            for r in (k.r_xnT, r_xT, r_hT):
                r.grant(act)
            ln_evacuate(k, act, 0, 0, bankX)
            groups(act, lambda g, par, more, chain: ln_evacuate(k, act, g + 1, 1 - par, bankX) if more else None)
            act.wait_ge(s_shift, 1)
            act.activation(ex[:, :, :], sh[:, :, :], ACT.Exp).then_inc(s_ex, 1)

            def evacuate(u, par):
                r_turn.wait_done(act, u)
                r_up.wait_free(act, u)
                act.activation(xT[:, par, :], bankX[:, 0:P], ACT.Copy).then_inc(r_xT.sem, 1)

            for u in range(3):
                evacuate(u, u % 2)

            def body(u, par):
                r_turnh.wait_done(act, u)
                r_y.wait_free(act, u)
                act.activation(hT[:, par, :], bankH[par][:, :], ACT.Relu).then_inc(r_hT.sem, 1)
                if exists(u + 3):
                    evacuate(u + 3, 1 - par)

            tiles(act, body)

        @block.gpsimd
        def _(pool):
            ln_rstd(k, pool, 0)
            groups(pool, lambda g, par, more, chain: ln_rstd(k, pool, g + 1) if more else None)
            pool.wait_ge(s_zeroed, 16)
            pool.wait_ge(s_pos, 1)
            for c in range(NSEQ):
                pool.indirect_dma_start(sorted_x[:, :], bass.IndirectOffsetOnAxis(pos[:, c:c + 1], 0),
                                        h_all[:, seq(c)], None).then_inc(s_scatter, 16)
            def store(u, par):
                r_yt.wait_done(pool, u)
                pool.dma_start(sorted_y[bass.ds(u * P, P), :], yt[:, par, :]).then_inc(s_out[par], 16)

            tiles(pool, store)
            for par in range(2):
                pool.wait_ge(s_out[par], 16 * NTILE // 2)
            for c in range(NSEQ):
                pool.indirect_dma_start(back[:, c, :], None, sorted_y[:, :],
                                        bass.IndirectOffsetOnAxis(pos[:, c:c + 1], 0)).then_inc(s_back[c // GS], 16)

        @block.vector
        def _(dve):
            for r in (r_logits, r_hp, r_yt):
                r.grant(dve)
            dve.memset(zeros[:, :], 0.0).then_inc(s_zeros, 1)
            k.wait_weights(dve, "l2f")

            def norm(g):
                ln_stats(k, dve, g)
                ln_apply(k, dve, g)
                dve.wait_ge(k.s_xn, g + 1)
                dve.tensor_copy(h_all[:, bass.ds(g * T, T)], k.xn[:, :, :].rearrange("p c d -> p (c d)"))

            norm(0)

            def route(g, par, more, chain):
                if more:
                    norm(g + 1)
                dve.wait_ge(s_logits, g + 1)
                n = GS * NE2
                dve.tensor_tensor(lg[:, :, :].rearrange("p c e -> p (c e)")[:, bass.ds(g * n, n)],
                                  bankM[:, 0:n], w["l2f_router_b"][:, :], ALU.add).then_inc(r_logits.sem, 1)

            groups(dve, route)
            r_logits.wait_done(dve, NG - 1)

            def per_token(ap):
                return bcast(ap.unsqueeze(2), all_tokens)

            def per_expert(ap, n=NSEQ):
                return bcast(ap.unsqueeze(1), [P, n, NE2])

            step = Chain(dve, s_step, 0, 0)
            step(dve.tensor_reduce(top[:, 0, :], lg[:, :, :], AX, ALU.max))
            dve.tensor_tensor(sh[:, :, :], lg[:, :, :], per_token(top[:, 0, :]), ALU.subtract).then_inc(s_shift, 1)
            dve.wait_ge(s_ex, 1)
            dve.tensor_reduce(top[:, 1, :], ex[:, :, :], AX, ALU.add)
            step(dve.tensor_reduce(top[:, 2, :], ex[:, :, :], AX, ALU.max))
            dve.reciprocal(top[:, 3, :], top[:, 1, :])
            step(dve.tensor_tensor(ta[:, :, :], ex[:, :, :], per_token(top[:, 2, :]), ALU.is_equal))
            dve.scalar_tensor_tensor(gate[:, :], top[:, 2, :], k.tanh_g[:, 6:7], top[:, 3, :], ALU.mult, ALU.mult)
            step(dve.tensor_tensor(ta[:, :, :], ta[:, :, :], per_expert(k.descending[:, 0, NE3 - NE2:NE3]), ALU.mult))
            step(dve.tensor_reduce(top[:, 4, :], ta[:, :, :], AX, ALU.max))
            dve.tensor_tensor(hot[:, :, :], ta[:, :, :], per_token(top[:, 4, :]), ALU.is_equal).then_inc(s_hot, 1)

            dve.wait_ge(s_count, 1)
            counts = lambda bank: bank[:, 0:NSEQ * NE2].rearrange("p (c e) -> p c e", c=NSEQ)
            step(dve.tensor_copy(tot[:, :, :], counts(bankY[1])))

            def scan(src, buffers, n):
                stride, flip = 1, 0
                while stride < n:
                    dst = buffers[flip]
                    dve.tensor_copy(dst[:, 0:stride], src[:, 0:stride])
                    step(dve.tensor_tensor(dst[:, stride:n], src[:, stride:n], src[:, 0:n - stride], ALU.add))
                    src, flip, stride = dst, 1 - flip, 2 * stride
                return src

            inclusive = scan(tot, upto, NSEQ)
            step(dve.tensor_scalar(cnt[:, :], inclusive[:, NSEQ - 1, :], MARGIN, 1.0 / P, ALU.add, ALU.mult))
            step(dve.tensor_scalar(cnt[:, :], cnt[:, :], MAGIC, MAGIC, ALU.add, ALU.subtract))
            end = scan(cnt, ends, NE2)
            dve.tensor_tensor(base[:, :], end[:, :], cnt[:, :], ALU.subtract)
            step(dve.tensor_tensor(le[:, :, :], per_expert(end[:, :], NTILE),
                                   bcast(k.tile_index[:, :].unsqueeze(2), [P, NTILE, NE2]), ALU.is_le))
            dve.tensor_scalar(base[:, :], base[:, :], float(P), None, ALU.mult)
            step(dve.tensor_reduce(te_f[:, :], le[:, :, :], AX, ALU.add))
            step(dve.tensor_scalar(te_f[:, :], te_f[:, :], float(NE2 - 1), None, ALU.min))
            dve.tensor_copy(te[:, :], te_f[:, :]).then_inc(s_te, 1)
            other = upto[1] if inclusive is upto[0] else upto[0]
            step(dve.tensor_tensor(other[:, :, :], inclusive[:, :, :], tot[:, :, :], ALU.subtract))
            step(dve.tensor_tensor(other[:, :, :], other[:, :, :], per_expert(base[:, :]), ALU.add))
            step(dve.tensor_tensor(other[:, :, :], other[:, :, :], counts(bankY[0]), ALU.add))
            step(dve.tensor_tensor(other[:, :, :], other[:, :, :], hot[:, :, :], ALU.mult))
            step(dve.tensor_reduce(pos_f[:, :], other[:, :, :], AX, ALU.add))
            dve.tensor_copy(pos[:, :], pos_f[:, :]).then_inc(s_pos, 1)
            dve.wait_ge(s_te, 1)

            def expert(u):
                return dve.value_load(te[0:1, bass.ds(u, 1)], min_val=0, max_val=NE2 - 1)

            def add_b1(u, par):
                e = expert(u)
                r_up.wait_done(dve, u)
                r_turnh.wait_free(dve, u)
                dve.tensor_tensor(hp[:, par, :], bankU[par][:, :], w["l2f_b1"][:, bass.ds(e * HID, HID)], ALU.add)\
                   .then_inc(r_hp.sem, 1)

            def add_b2(u, par):
                e = expert(u)
                r_y.wait_done(dve, u)
                if not isinstance(u, int) or u >= 2:
                    dve.wait_ge(s_out[par], (u - par) * 8)
                dve.tensor_tensor(yt[:, par, :], bankY[par][:, 0:P], w["l2f_b2"][:, bass.ds(e * P, P)], ALU.add)\
                   .then_inc(r_yt.sem, 1)

            add_b1(0, 0)
            add_b1(1, 1)

            def body(u, par):
                if exists(u + 2):
                    add_b1(u + 2, par)
                add_b2(u, par)

            tiles(dve, body)

            for c in range(NSEQ):
                if c % GS == 0:
                    dve.wait_ge(s_back[c // GS], 16 * GS)
                dve.scalar_tensor_tensor(k.x_sb[:, seq(c)], back[:, c, :], gate[:, c:c + 1], k.x_sb[:, seq(c)],
                                         ALU.mult, ALU.add)


def layer3_attention(nc, k):
    with ExitStack() as ctx:
        sb, sem = k.local(ctx, "l3x")
        ln_tensors(k, sb, sem)
        amax = sb("amax", [P, 3], F32)
        amax_all = sb("amax_all", [P, 3], F32)
        step = sb("step", [P, 3], F32)
        inv = sb("inv", [P, 3], F32)
        wr = sb("w_rounded", [P, 3, P], F32)
        wi = sb("w_steps", [P, 3, P], F32)
        gbv = sb("tanh_g_bv", [P, GS, P], F32)
        ctxT = sb("ctxT", [P, 2, T], F32)
        qT = sb("qT", [P, T], F32)
        kT = sb("kT", [P, T], F32)
        v = sb("v", [P, GS, P], F32)
        nmax = sb("nmax", [P, GS], F32)
        nmax_s = sb("nmax_scaled", [P, GS], F32)
        probs = sb("probs", [P, GS, P], F32)
        probsT = sb("probsT", [P, T], F32)
        total = sb("total", [P, GS], F32)
        rtot = sb("rtot", [P, GS], F32)
        rg = sb("rtot_tanh_g", [P, GS], F32)
        bankX, bankQ, bankK, bankV, bankS, bankPT, bankO, bankM = (k.bank(i) for i in range(8))
        scale = float(P) ** -0.5

        s_prep = sem("weights_step")
        s_all = sem("absmax_everywhere")
        s_amT = sem("absmax_turned")
        s_wr = sem("w_rounded_ready")
        s_chain = sem("dve_step")
        r_ctx = Ring(sem("ctxT_used"), 2)
        s_ctx = [sem(f"ctxT_in_{p}") for p in range(2)]
        s_q, s_kk, s_v = sem("q_in_psum"), sem("k_in_psum"), sem("v_in_psum")
        r_proj = Ring(sem("qkv_ready"), 1)
        r_s = Ring(sem("scores_in_psum"), 1)
        s_nmax = sem("minus_max_ready")
        r_p = Ring(sem("probs_ready"), 1)
        r_pt = Ring(sem("probsT_in_psum"), 1)
        r_pts = Ring(sem("probsT_ready"), 1)
        r_o = Ring(sem("out_in_psum"), 1)
        r_out = Ring(sem("x_updated"), 1)
        r_xb = Ring(sem("x_plus_bias"), 1)

        block = ctx.enter_context(nc.Block())

        @block.sync
        def _(sp):
            with sp.Fori(0, NG // 2) as it:
                for par in range(2):
                    g = 2 * it + par
                    r_ctx.wait_free(sp, g)
                    sp.dma_start(ctxT[:, par, :], k.dram["ctxT"][:, bass.ds(g * T, T)]).then_inc(s_ctx[par], 16)

        @block.tensor
        def _(pe):
            for r in (k.r_xnT_psum, k.r_xnT_used, r_ctx, r_s, r_pt, r_o):
                r.grant(pe)
            k.wait_weights(pe, "l3x")
            pe.wait_ge(s_prep, 1)
            pe.transpose(bankM[0:3, 0:P], amax[:, :], k.ident[:, :]).then_inc(s_amT, 1)
            pe.wait_ge(s_prep, 3)
            pe.matmul(bankM[:, P:P + 3], k.ones[0:3, :], wr[0:3, 0, 0:3], start=True, stop=True).then_inc(s_all, 1)
            ln_transpose(k, pe, 0, bankX)
            pe.wait_ge(s_wr, 1)

            def body(g, par, more, chain):
                xnT, cT = k.xnT[:, par, :], ctxT[:, par, :]
                pe.wait_ge(s_ctx[par], (g - par) * 8 + 16)
                r_proj.wait_free(pe, g)
                pe.matmul(bankK[:, :], wr[:, 1, :], cT, start=True, stop=True).then_inc(s_kk, 1)
                k.r_xnT.wait_done(pe, g)
                pe.matmul(bankQ[:, :], wr[:, 0, :], xnT, start=True, stop=True).then_inc(s_q, 1)
                for c in range(GS):
                    ins = pe.matmul(bankV[:, seq(c)], cT[:, seq(c)], wr[:, 2, :], start=True, stop=True)
                ins.then_inc(s_v, 1)
                pe.wait_ge(s_v, g + 1)
                pe.sem_inc(r_ctx.sem, 1)
                pe.sem_inc(k.r_xnT_used.sem, 1)
                r_proj.wait_done(pe, g)
                r_p.wait_free(pe, g)
                for c in range(GS):
                    ins = pe.matmul(bankS[:, seq(c)], qT[:, seq(c)], kT[:, seq(c)], start=True, stop=True)
                ins.then_inc(r_s.sem, 1)
                if more:
                    ln_transpose(k, pe, g + 1, bankX)
                r_p.wait_done(pe, g)
                r_pts.wait_free(pe, g)
                for c in range(GS):
                    ins = pe.transpose(bankPT[:, seq(c)], probs[:, c, :], k.ident[:, :])
                ins.then_inc(r_pt.sem, 1)
                r_pts.wait_done(pe, g)
                r_out.wait_free(pe, g)
                for c in range(GS):
                    ins = pe.matmul(bankO[:, seq(c)], probsT[:, seq(c)], v[:, c, :], start=True, stop=True)
                ins.then_inc(r_o.sem, 1)

            groups(pe, body)

        @block.scalar
        def _(act):
            for r in (k.r_xnT, r_proj, r_p, r_pts):
                r.grant(act)
            ln_evacuate(k, act, 0, 0, bankX)

            def body(g, par, more, chain):
                r_s.wait_free(act, g)
                act.wait_ge(s_kk, g + 1)
                act.activation(kT[:, :], bankK[:, :], ACT.Identity, bias=k.w["l3x_bk"][:, :])
                act.wait_ge(s_q, g + 1)
                act.activation(qT[:, :], bankQ[:, :], ACT.Identity, bias=k.w["l3x_bq"][:, :])
                act.wait_ge(s_v, g + 1)
                r_o.wait_free(act, g)
                act.activation(v[:, :, :], bankV.rearrange("p (c d) -> p c d", c=GS), ACT.Copy)\
                   .then_inc(r_proj.sem, 1)
                if more:
                    ln_evacuate(k, act, g + 1, 1 - par, bankX)
                act.wait_ge(s_nmax, g + 1)
                r_pt.wait_free(act, g)
                for c in range(GS):
                    ins = act.activation(probs[:, c, :], bankS[:, seq(c)], ACT.Exp, bias=nmax_s[:, c:c + 1],
                                         scale=scale, accum_out=total[:, c:c + 1])
                ins.then_inc(r_p.sem, 1)
                r_pt.wait_done(act, g)
                r_o.wait_free(act, g)
                act.activation(probsT[:, :], bankPT[:, :], ACT.Copy).then_inc(r_pts.sem, 1)

            groups(act, body)

        @block.gpsimd
        def _(pool):
            ln_rstd(k, pool, 0)
            groups(pool, lambda g, par, more, chain: ln_rstd(k, pool, g + 1) if more else None)

        @block.vector
        def _(dve):
            r_out.grant(dve)
            k.wait_weights(dve, "l3x")
            prep = Chain(dve, s_prep, 0, 0)
            for i, n in enumerate(("l3x_wq", "l3x_wk", "l3x_wv")):
                ins = dve.tensor_reduce(amax[:, i:i + 1], k.w[n][:, :], AX, ALU.max, apply_absolute_value=True)
            prep(ins)
            ln_stats(k, dve, 0)
            dve.wait_ge(s_amT, 1)
            prep(dve.tensor_reduce(amax_all[0:3, 0:1], bankM[0:3, 0:P], AX, ALU.max))
            prep(dve.tensor_scalar(wr[0:3, 0, 0:3], k.ident[0:3, 0:3], amax_all[0:3, 0:1], None, ALU.mult))
            dve.wait_ge(s_all, 1)
            prep(dve.tensor_scalar(step[:, :], bankM[:, P:P + 3], 2.0 / 256.0, None, ALU.mult))
            prep(dve.reciprocal(inv[:, :], step[:, :]))
            for i, n in enumerate(("l3x_wq", "l3x_wk", "l3x_wv")):
                prep(dve.tensor_scalar(wi[:, i, :], k.w[n][:, :], inv[:, i:i + 1], MAGIC, ALU.mult, ALU.add))
                ins = dve.tensor_scalar(wr[:, i, :], wi[:, i, :], -MAGIC, step[:, i:i + 1], ALU.add, ALU.mult)
            ins.then_inc(s_wr, 1)
            for c in range(GS):
                ins = dve.tensor_scalar(gbv[:, c, :], k.w["l3x_bv"][:, :], k.tanh_g[:, 3:4], None, ALU.mult)
            prep(ins)
            ln_apply(k, dve, 0)

            def body(g, par, more, chain):
                if more:
                    ln_stats(k, dve, g + 1)
                r_s.wait_done(dve, g)
                chain(dve.tensor_reduce(nmax[:, :], bankS.rearrange("p (c w) -> p c w", c=GS), AX, ALU.max,
                                        negate=True))
                dve.tensor_scalar(nmax_s[:, :], nmax[:, :], scale, None, ALU.mult).then_inc(s_nmax, 1)
                if more:
                    ln_apply(k, dve, g + 1)
                xs = k.x_sb[:, bass.ds(g * T, T)]
                dve.tensor_tensor(xs, xs, gbv[:, :, :].rearrange("p c d -> p (c d)"), ALU.add)
                r_p.wait_done(dve, g)
                chain(dve.reciprocal(rtot[:, :], total[:, :]))
                chain(dve.tensor_scalar(rg[:, :], rtot[:, :], k.tanh_g[:, 3:4], None, ALU.mult))
                r_o.wait_done(dve, g)
                for c in range(GS):
                    xc = k.x_sb[:, bass.ds((g * GS + c) * P, P)]
                    ins = dve.scalar_tensor_tensor(xc, bankO[:, seq(c)], rg[:, c:c + 1], xc, ALU.mult, ALU.add)
                ins.then_inc(r_out.sem, 1)

            groups(dve, body, s_chain, 6)


NE3 = 16


def layer3_ffn(nc, k):
    with ExitStack() as ctx:
        sb, sem = k.local(ctx, "l3f")
        ln_tensors(k, sb, sem)
        w = k.w
        sq = sb("sim_squared", [P, NE3], F32)
        cnorm = sb("column_norm", [P, NE3], F32)
        cinv = sb("column_rnorm", [P, NE3], F32)
        sn = sb("sim_normed", [P, NE3], F32)
        sig = sb("sigmoid_gates", [P, NE3], F32)
        sig_e = sb("exp_minus_gates", [P, NE3], F32)
        xsq = sb("xn_squared", [P, GS, P], F32)
        ssum = sb("xn_sum_squares", [P, GS], F32)
        rnorm = sb("xn_rnorm", [P, GS], F32)
        lg = sb("logits", [P, GS, NE3], F32)
        gated = sb("gated", [P, GS, NE3], F32)
        hard = sb("hard", [P, GS, NE3], F32)
        ta = sb("select_a", [P, GS, NE3], F32)
        tb = sb("select_b", [P, GS, NE3], F32)
        tc = sb("select_c", [P, GS, NE3], F32)
        top = sb("tops", [P, 8, GS], F32)
        ex = sb("gate_exp", [P, GS, NE3], F32)
        w3 = sb("w_parts", [P, GS, P], BF16)
        wr1 = sb("w_rest1", [P, GS, NE3], F32)
        wT = sb("w_partsT", [P, 2, T], BF16)
        wO = sb("w_partsT_out", [P, T], BF16)
        xe = sb("weighted_T", [P, 2, T], F32)
        qT, kT, vT, oT = (sb(n, [P, T], F32) for n in ("qT", "kT", "vT", "oT"))
        v = sb("v", [P, GS, P], F32)
        nmax = sb("minus_max", [P, GS], F32)
        probs = sb("probs", [P, GS, P], F32)
        probsT = sb("probsT", [P, T], F32)
        attn = sb("attn", [P, GS, P], F32)
        total = sb("total", [P, GS], F32)
        rtot = sb("rtot", [P, GS], F32)
        yT = sb("yT", [P, T], F32)
        bankW = [k.bank(0), k.bank(1)]
        bankQ, bankK, bankV, bankX, bankS, bankM = (k.bank(i) for i in range(2, 8))
        scale = float(P) ** -0.5

        s_prep = sem("prep_step")
        s_csum = sem("column_sums")
        s_cpow = sem("column_rnorm_ready")
        s_sige = sem("exp_minus_gates_ready")
        s_chain = sem("dve_step")
        s_gates = sem("logits_in_psum")
        s_ss = sem("sum_squares_ready")
        s_rn0 = sem("sum_squares_clamped")
        s_rn = sem("xn_rnorm_ready")
        s_gx = sem("gated_shifted")
        s_ex = sem("gate_exp_ready")
        s_w3 = sem("w_parts_ready")
        s_wTp = sem("w_partsT_in_psum")
        r_wT = Ring(sem("w_partsT_ready"), 1)
        r_wTu = Ring(sem("w_partsT_used"), 2)
        s_we = sem("w_e_spread")
        r_xe = Ring(sem("weighted_ready"), 2)
        r_xu = Ring(sem("weighted_used"), 2)
        s_wO = sem("w_partsT_out_ready")
        r_qkv = Ring(sem("qkv_ready"), 1)
        s_vt = sem("v_turned")
        r_v = Ring(sem("v_ready"), 1)
        s_s = sem("scores_in_psum")
        s_nmax = sem("minus_max_ready")
        s_p = sem("probs_ready")
        s_attn = sem("attn_ready")
        s_pt = sem("probsT_in_psum")
        s_pts = sem("probsT_ready")
        s_o = sem("oT_in_psum")
        s_oT = sem("oT_ready")
        s_y = sem("yT_in_psum")
        s_yT = sem("yT_ready")
        s_yt = sem("y_in_psum")
        r_out = Ring(sem("x_updated"), 1)

        block = ctx.enter_context(nc.Block())

        @block.tensor
        def _(pe):
            for r in (k.r_xnT_psum, k.r_xnT_used, r_wTu, r_xu):
                r.grant(pe)
            k.wait_weights(pe, "l3f")
            pe.wait_ge(s_prep, 1)
            pe.matmul(bankM[:, 0:NE3], k.ones[:, :], sq[:, :], start=True, stop=True).then_inc(s_csum, 1)
            ln_transpose(k, pe, 0, bankX)
            pe.wait_ge(s_prep, 3)

            def route(g, par):
                k.r_xnT.wait_done(pe, g)
                for c in range(GS):
                    ins = pe.matmul(bankM[:, c * NE3:(c + 1) * NE3], k.xnT[:, par, seq(c)], sn[:, :],
                                    start=True, stop=True)
                ins.then_inc(s_gates, 1)

            def turn_weights(g):
                pe.wait_ge(s_w3, g + 1)
                for c in range(GS):
                    ins = pe.transpose(bankM[:, 256:512].bitcast(BF16)[:, seq(c)], w3[:, c, :], k.ident_bf[:, :])
                ins.then_inc(s_wTp, 1)

            def mixture(first, weights, operands, banks, between=lambda e: None):
                def spread(e):
                    r_xe.wait_free(pe, first + e)
                    pe.matmul(bankW[e % 2][:, :], k.select[:, e, :], weights, start=True, stop=True)\
                      .then_inc(s_we, 1)

                spread(0)
                for e in range(NE3):
                    if e + 1 < NE3:
                        spread(e + 1)
                    r_xe.wait_done(pe, first + e)
                    for name, bank in zip(operands, banks):
                        ins = pe.matmul(bank[:, :], w[name][:, e, :], xe[:, e % 2, :],
                                        start=(e == 0), stop=(e == NE3 - 1))
                    ins.then_inc(r_xu.sem, 1)
                    between(e)

            def mix_qkv(g, par, first, between):
                r_wT.wait_done(pe, g)
                r_qkv.wait_free(pe, g)
                mixture(first, wT[:, par, :], ("l3f_q", "l3f_k", "l3f_v"), (bankQ, bankK, bankV), between)

            def qkv_mixed(first):
                r_xu.wait_done(pe, first + NE3 - 1)
                pe.sem_inc(k.r_xnT_used.sem, 1)
                pe.sem_inc(r_wTu.sem, 1)

            def router_between(g, par, e):
                if e == 2:
                    ln_transpose(k, pe, g, bankX)
                if e == 4:
                    route(g, par)
                if e == NE3 - 2:
                    turn_weights(g)

            def attention_between(t, e):
                if e == 1:
                    r_qkv.wait_done(pe, t)
                    r_out.wait_free(pe, t)
                    for c in range(GS):
                        ins = pe.transpose(bankX[:, seq(c)], vT[:, seq(c)], k.ident[:, :])
                    ins.then_inc(s_vt, 1)
                    for c in range(GS):
                        ins = pe.matmul(bankS[:, seq(c)], qT[:, seq(c)], kT[:, seq(c)], start=True, stop=True)
                    ins.then_inc(s_s, 1)
                    r_v.wait_done(pe, t)
                if e == 5:
                    pe.wait_ge(s_attn, t + 1)
                    for c in range(GS):
                        ins = pe.transpose(bankS[:, seq(c)], attn[:, c, :], k.ident[:, :])
                    ins.then_inc(s_pt, 1)
                if e == 7:
                    pe.wait_ge(s_pts, t + 1)
                    for c in range(GS):
                        ins = pe.matmul(bankX[:, seq(c)], v[:, c, :], probsT[:, seq(c)], start=True, stop=True)
                    ins.then_inc(s_o, 1)

            route(0, 0)
            turn_weights(0)
            mix_qkv(0, 0, 0, lambda e: router_between(1, 1, e))
            qkv_mixed(0)

            def body(t, par, more, chain):
                after = not isinstance(t, int)
                first = (2 * t + 1) * NE3

                def between(e):
                    attention_between(t, e)
                    if after:
                        router_between(t + 2, par, e)

                if more:
                    mix_qkv(t + 1, 1 - par, first, between)
                    out_first = first + NE3
                else:
                    for e in range(NE3):
                        between(e)
                    out_first = first
                pe.wait_ge(s_wO, t + 1)
                pe.wait_ge(s_oT, t + 1)
                mixture(out_first, wO[:, :], ("l3f_o",), (bankS,))
                if more:
                    qkv_mixed(first)
                pe.wait_ge(s_yT, t + 1)
                for c in range(GS):
                    ins = pe.transpose(bankX[:, seq(c)], yT[:, seq(c)], k.ident[:, :])
                ins.then_inc(s_yt, 1)

            groups(pe, body)

        @block.scalar
        def _(act):
            for r in (k.r_xnT, r_wT, r_qkv, r_v):
                r.grant(act)
            k.wait_weights(act, "l3f")
            act.activation(sig_e[:, :], w["l3f_gates"][:, :], ACT.Exp, scale=-1.0).then_inc(s_sige, 1)
            ln_evacuate(k, act, 0, 0, bankX)

            def gates_exp(g):
                act.wait_ge(s_gx, g + 1)
                act.activation(ex[:, :, :], tb[:, :, :], ACT.Exp).then_inc(s_ex, 1)

            def weights_out(g, par):
                act.wait_ge(s_wTp, g + 1)
                r_wTu.wait_free(act, g)
                act.activation(wT[:, par, :], bankM[:, 256:512].bitcast(BF16), ACT.Copy).then_inc(r_wT.sem, 1)

            def qkv_out(first):
                r_xu.wait_done(act, first + NE3 - 1)
                act.activation(vT[:, :], bankV[:, :], ACT.Copy)
                act.activation(qT[:, :], bankQ[:, :], ACT.Copy)
                act.activation(kT[:, :], bankK[:, :], ACT.Copy).then_inc(r_qkv.sem, 1)

            gates_exp(0)
            weights_out(0, 0)
            ln_evacuate(k, act, 1, 1, bankX)
            gates_exp(1)
            weights_out(1, 1)
            qkv_out(0)

            def body(t, par, more, chain):
                after = not isinstance(t, int)
                first = (2 * t + 1) * NE3
                r_wT.wait_done(act, t)
                act.activation(wO[:, :], wT[:, par, :], ACT.Copy).then_inc(s_wO, 1)
                act.wait_ge(s_vt, t + 1)
                act.activation(v[:, :, :], bankX.rearrange("p (c d) -> p c d", c=GS), ACT.Copy)\
                   .then_inc(r_v.sem, 1)
                if after:
                    ln_evacuate(k, act, t + 2, par, bankX)
                act.wait_ge(s_nmax, t + 1)
                for c in range(GS):
                    ins = act.activation(probs[:, c, :], bankS[:, seq(c)], ACT.Exp, bias=nmax[:, c:c + 1],
                                         scale=scale, accum_out=total[:, c:c + 1])
                ins.then_inc(s_p, 1)
                act.wait_ge(s_pt, t + 1)
                act.activation(probsT[:, :], bankS[:, :], ACT.Copy).then_inc(s_pts, 1)
                if after:
                    gates_exp(t + 2)
                act.wait_ge(s_o, t + 1)
                act.activation(oT[:, :], bankX[:, :], ACT.Copy).then_inc(s_oT, 1)
                if after:
                    weights_out(t + 2, par)
                if more:
                    qkv_out(first)
                r_xu.wait_done(act, first + (2 if more else 1) * NE3 - 1)
                act.activation(yT[:, :], bankS[:, :], ACT.Copy).then_inc(s_yT, 1)

            groups(act, body)

        @block.gpsimd
        def _(pool):
            pool.wait_ge(s_prep, 2)
            pool.tensor_tensor(cinv[:, :], cnorm[:, :], k.minus_half[:, 0:NE3], ALU.pow).then_inc(s_cpow, 1)
            ln_rstd(k, pool, 0)

            def norms(g):
                pool.wait_ge(s_ss, g + 1)
                pool.tensor_tensor(rnorm[:, :], ssum[:, :], k.minus_half[:, 0:GS], ALU.pow).then_inc(s_rn, 1)

            norms(0)
            ln_rstd(k, pool, 1)
            norms(1)

            def body(t, par, more, chain):
                if not isinstance(t, int):
                    ln_rstd(k, pool, t + 2)
                    norms(t + 2)

            groups(pool, body)

        @block.vector
        def _(dve):
            r_xe.grant(dve)
            r_out.grant(dve)
            k.wait_weights(dve, "l3f")
            prep = Chain(dve, s_prep, 0, 0)
            prep(dve.tensor_tensor(sq[:, :], w["l3f_sim"][:, :], w["l3f_sim"][:, :], ALU.mult))
            dve.memset(w3[:, :, :], 0.0)
            dve.wait_ge(s_csum, 1)
            prep(dve.tensor_scalar(cnorm[:, :], bankM[:, 0:NE3], 1e-24, None, ALU.max))
            dve.wait_ge(s_cpow, 1)
            prep(dve.tensor_tensor(sn[:, :], w["l3f_sim"][:, :], cinv[:, :], ALU.mult))
            dve.wait_ge(s_sige, 1)
            prep(dve.tensor_scalar(sig_e[:, :], sig_e[:, :], 1.0, None, ALU.add))
            prep(dve.reciprocal(sig[:, :], sig_e[:, :]))
            ln_stats(k, dve, 0)
            ln_apply(k, dve, 0)

            first = Chain(dve, sem("first_gates_step"), 0, 0)

            def both(ap):
                return bcast(ap.unsqueeze(2), [P, GS, NE3])

            def norms(g, chain):
                dve.wait_ge(k.s_xn, g + 1)
                chain(dve.tensor_tensor(xsq[:, :, :], k.xn[:, :, :], k.xn[:, :, :], ALU.mult))
                chain(dve.tensor_reduce(top[:, 0, :], xsq[:, :, :], AX, ALU.add))
                dve.tensor_scalar(ssum[:, :], top[:, 0, :], 1e-24, None, ALU.max).then_inc(s_ss, 1)

            def logits(g, chain):
                raw = bankM[:, 0:GS * NE3].rearrange("p (c e) -> p c e", c=GS)
                dve.wait_ge(s_gates, g + 1)
                dve.wait_ge(s_rn, g + 1)
                chain(dve.tensor_tensor(ta[:, :, :], raw, both(rnorm[:, :]), ALU.mult))
                chain(dve.tensor_tensor(lg[:, :, :], ta[:, :, :], bcast(sig[:, :].unsqueeze(1), [P, GS, NE3]),
                                        ALU.subtract))
                dve.tensor_scalar(hard[:, :, :], lg[:, :, :], 0.0, None, ALU.is_gt)
                chain(dve.tensor_scalar(gated[:, :, :], lg[:, :, :], 0.0, None, ALU.max))
                chain(dve.tensor_reduce(top[:, 1, :], gated[:, :, :], AX, ALU.max))
                dve.tensor_tensor(tb[:, :, :], gated[:, :, :], both(top[:, 1, :]), ALU.subtract).then_inc(s_gx, 1)
                chain(dve.tensor_scalar(top[:, 2, :], top[:, 1, :], 0.0, None, ALU.is_le))

            def find_largest(chain):
                chain(dve.tensor_reduce(top[:, 3, :], lg[:, :, :], AX, ALU.max))
                chain(dve.tensor_tensor(ta[:, :, :], lg[:, :, :], both(top[:, 3, :]), ALU.is_equal))
                chain(dve.tensor_tensor(ta[:, :, :], ta[:, :, :], k.descending[:, :, :], ALU.mult))
                chain(dve.tensor_reduce(top[:, 4, :], ta[:, :, :], AX, ALU.max))
                chain(dve.tensor_tensor(tc[:, :, :], ta[:, :, :], both(top[:, 4, :]), ALU.is_equal))

            def take_largest(chain):
                chain(dve.scalar_tensor_tensor(lg[:, :, :], tc[:, :, :], -1e30, lg[:, :, :], ALU.mult, ALU.add))
                chain(dve.tensor_tensor(ta[:, :, :], tc[:, :, :], both(top[:, 2, :]), ALU.mult))
                chain(dve.tensor_tensor(hard[:, :, :], hard[:, :, :], ta[:, :, :], ALU.add))

            def token_weights(g, chain):
                dve.wait_ge(s_ex, g + 1)
                chain(dve.tensor_tensor(ta[:, :, :], ex[:, :, :], hard[:, :, :], ALU.mult))
                chain(dve.tensor_reduce(top[:, 5, :], ta[:, :, :], AX, ALU.add))
                chain(dve.reciprocal(top[:, 6, :], top[:, 5, :]))
                chain(dve.tensor_tensor(ta[:, :, :], ta[:, :, :], both(top[:, 6, :]), ALU.mult))

            def weight_parts(chain):
                chain(dve.tensor_copy(w3[:, :, 0:NE3], ta[:, :, :]))
                chain(dve.tensor_tensor(wr1[:, :, :], ta[:, :, :], w3[:, :, 0:NE3], ALU.subtract))
                chain(dve.tensor_copy(w3[:, :, NE3:2 * NE3], wr1[:, :, :]))
                dve.tensor_tensor(w3[:, :, 2 * NE3:3 * NE3], wr1[:, :, :], w3[:, :, NE3:2 * NE3], ALU.subtract)\
                   .then_inc(s_w3, 1)

            def router_between(g, e, chain):
                if e == 0:
                    ln_stats(k, dve, g)
                if e == 1:
                    ln_apply(k, dve, g)
                if e == 2:
                    norms(g, chain)
                if e == 5:
                    logits(g, chain)
                if e in (6, 8):
                    find_largest(chain)
                if e in (7, 9):
                    take_largest(chain)
                if e == 10:
                    token_weights(g, chain)
                if e == 11:
                    weight_parts(chain)

            def attention_between(t, e, chain):
                if e == 2:
                    dve.wait_ge(s_s, t + 1)
                    chain(dve.tensor_reduce(top[:, 7, :], bankS.rearrange("p (c t) -> p c t", c=GS), AX, ALU.max,
                                            negate=True))
                    dve.tensor_scalar(nmax[:, :], top[:, 7, :], scale, None, ALU.mult).then_inc(s_nmax, 1)
                if e == 4:
                    dve.wait_ge(s_p, t + 1)
                    chain(dve.reciprocal(rtot[:, :], total[:, :]))
                    dve.tensor_tensor(attn[:, :, :], probs[:, :, :], bcast(rtot[:, :].unsqueeze(2), [P, GS, P]),
                                      ALU.mult).then_inc(s_attn, 1)

            def weigh(first, src, between=lambda e: None):
                for e in range(NE3):
                    dve.wait_ge(s_we, first + e + 1)
                    r_xu.wait_free(dve, first + e)
                    dve.tensor_tensor(xe[:, e % 2, :], bankW[e % 2][:, :], src, ALU.mult).then_inc(r_xe.sem, 1)
                    between(e)

            for e in range(2, NE3):
                router_between(0, e, first)
            weigh(0, k.xnT[:, 0, :], lambda e: router_between(1, e, first))

            def body(t, par, more, chain):
                after = not isinstance(t, int)
                first = (2 * t + 1) * NE3

                def between(e):
                    attention_between(t, e, chain)
                    if after:
                        router_between(t + 2, e, chain)

                if more:
                    weigh(first, k.xnT[:, 1 - par, :], between)
                    out_first = first + NE3
                else:
                    for e in range(NE3):
                        between(e)
                    out_first = first
                dve.wait_ge(s_oT, t + 1)
                weigh(out_first, oT[:, :])
                dve.wait_ge(s_yt, t + 1)
                xs = k.x_sb[:, bass.ds(t * T, T)]
                dve.scalar_tensor_tensor(xs, bankX[:, :], k.tanh_g[:, 7:8], xs, ALU.mult, ALU.add)\
                   .then_inc(r_out.sem, 1)

            groups(dve, body, s_chain, (LINKS3, LINKS3_LAST))


LINKS3, LINKS3_LAST = 64, 4


def launch_constants():
    freq = (np.float32(1) / np.float32(10000) ** (np.arange(0, HD, 2, dtype=np.float32) / np.float32(HD)))
    angle = np.repeat(np.repeat(freq.astype(np.float32), 2), HEADS)[:, None] * np.arange(P, dtype=np.float32)[None]
    sign = np.tile(np.repeat(np.array([-1, 1], np.float32), HEADS), HD // 2)[:, None]
    part_of = np.zeros((P, NE3), np.float32)
    for e in range(NE3):
        part_of[e:3 * NE3:NE3, e] = 1
    return {
        "l0x_cos": np.tile(np.cos(angle), (1, GS)),
        "l0x_sin": np.tile(np.sin(angle) * sign, (1, GS)),
        "c_ident": np.eye(P, dtype=np.float32),
        "c_part_of": part_of,
        "c_before": np.triu(np.ones((P, P), np.float32), 1),
        "c_tile_index": np.tile(np.arange(NTILE, dtype=np.float32), (P, 1)),
        "c_descending": np.tile(np.arange(NE3, 0, -1, dtype=np.float32), (P, GS, 1)),
    }


class Global(Core):
    def __init__(self, nc, ctx, dram):
        self.nc, self.ctx, self.dram, self.w, self.due = nc, ctx, dram, {}, {}
        sb = lambda name, shape, dt: ctx.enter_context(nc.sbuf_tensor(name, shape, dt))
        self.psum = ctx.enter_context(nc.psum_tensor("psum", [P, 8 * 512], F32))
        self.x_sb = sb("x_sb", [P, NSEQ * P], F32)
        self.ident = sb("ident", [P, P], F32)
        self.ident_bf = sb("ident_bf", [P, P], BF16)
        self.part_of = sb("part_of", [P, NE3], F32)
        self.select = sb("select", [P, NE3, P], BF16)
        self.descending = sb("descending", [P, GS, NE3], F32)
        self.before = sb("before", [P, P], F32)
        self.tile_index = sb("tile_index", [P, NTILE], F32)
        self.minus_half = sb("minus_half", [P, 16], F32)
        self.ones = sb("ones", [P, P], F32)
        self.one_cell = sb("one_cell", [P, 1], F32)
        self.eps = sb("eps", [P, GS], F32)
        self.g_in = sb("g_in", [P, 8], F32)
        self.tanh_g = sb("tanh_g", [P, 8], F32)

    def bank(self, i):
        return self.psum[:, i * 512:(i + 1) * 512]

    def banks(self, i, n):
        return self.psum[:, i * 512:(i + n) * 512]

    def local(self, ctx, prefix):
        sb = lambda name, shape, dt: ctx.enter_context(self.nc.sbuf_tensor(f"{prefix}_{name}", shape, dt))
        used = []
        ctx.callback(self.nc.all_engine_barrier)
        ctx.callback(lambda: self.nc.clear_and_free_semaphores(used))

        def sem(name):
            used.append(self.nc.alloc_semaphore(f"{prefix}_{name}"))
            return used[-1]

        return sb, sem

    def weight(self, layer, name, shape, dt=F32):
        self.w[name] = self.ctx.enter_context(self.nc.sbuf_tensor("w_" + name, shape, dt))
        self.due.setdefault(layer, []).append(name)

    def wait_weights(self, eng, layer):
        eng.wait_ge(self.s_weights[layer], 16 * len(self.due[layer]))


ATTN = {"wq": [P, P], "wk": [P, P], "wv": [P, P], "wo": [P, P], "bq": [P, 1], "bk": [P, 1], "bv": [P, 1],
        "bo": [P, P]}
WEIGHTS = {
    "l0x": {"l0x_" + n: s for n, s in (ATTN | {"wqs": [P, P], "wks": [P, P], "bqs": [P, 1], "bks": [P, 1],
                                               "cos": [P, T], "sin": [P, T]}).items()},
    "l1x": {"l1x_" + n: s for n, s in ATTN.items()},
    "l0f": {"l0f_w1": [P, HID], "l0f_w2": [P, NHB, P], "l0f_cw": [P, 3 * NHB], "l0f_cb": [P, NHB]},
    "l2f": {"l2f_router": [P, NE2], "l2f_router_b": [P, GS * NE2], "l2f_w1": [P, NE2 * HID],
            "l2f_b1": [P, NE2 * HID], "l2f_w2": [P, NE2 * HID], "l2f_b2": [P, NE2 * P]},
    "l2x": {"l2x_w1": [P, 1], "l2x_w2": [P, 1], "l2x_w3": [P, 1], "l2x_bsim": [P, 1], "l2x_wqv": [P, 4, P],
            "l2x_bqv": [P, P]},
    "l3f": {"l3f_sim": [P, NE3], "l3f_gates": [P, NE3], "l3f_q": [P, NE3, P], "l3f_k": [P, NE3, P],
            "l3f_v": [P, NE3, P], "l3f_o": [P, NE3, P]},
    "l3x": {"l3x_wq": [P, P], "l3x_wk": [P, P], "l3x_wv": [P, P], "l3x_bq": [P, 1], "l3x_bk": [P, 1],
            "l3x_bv": [P, P]},
    "l1f": {"l1f_ar1": [P, NZL], "l1f_w1": [P, HID], "l1f_b1": [P, HID], "l1f_w2ar": [P, NHB, P + NZL],
            "l1f_b2": [P, P]},
}
LAYERS = {"l0x": layer0_attention, "l0f": layer0_ffn, "l1x": layer1_attention, "l1f": layer1_ffn, "l2x": layer2_attention, "l2f": layer2_ffn, "l3x": layer3_attention, "l3f": layer3_ffn}


LATE = ("l2f", "l3f")


def load_weights(k, sp, layers):
    for layer in layers:
        for name in k.due[layer]:
            w, src = k.w[name], k.dram[name]
            if tuple(src.shape) != tuple(w.shape):
                src = bcast(src, w.shape)
            sp.dma_start(w[:], src).then_inc(k.s_weights[layer], 16)


def program(nc, dram, out, layers):
    with ExitStack() as ctx:
        k = Global(nc, ctx, dram)
        k.s_weights = {}
        for layer in layers:
            k.s_weights[layer] = ctx.enter_context(nc.semaphore(f"weights_{layer}_in"))
            if layer not in LATE:
                for name, shape in WEIGHTS[layer].items():
                    k.weight(layer, name, shape)
        s_x = ctx.enter_context(nc.semaphore("x_in"))
        s_const = ctx.enter_context(nc.semaphore("constants_in"))
        k.s_filled = ctx.enter_context(nc.semaphore("fills_ready"))
        s_tanh = ctx.enter_context(nc.semaphore("tanh_g_ready"))
        s_out = ctx.enter_context(nc.semaphore("x_out"))

        with nc.Block() as block:
            @block.sync
            def _(sp):
                for name, t in (("ident", k.ident), ("part_of", k.part_of), ("descending", k.descending),
                                ("before", k.before), ("tile_index", k.tile_index)):
                    sp.dma_start(t[:], dram["c_" + name]).then_inc(s_const, 16)
                sp.dma_start(k.g_in[:, :], bcast(dram["gains"], [P, 8])).then_inc(s_const, 16)
                sp.dma_start(k.x_sb[:, :], dram["x"]).then_inc(s_x, 16)
                load_weights(k, sp, [layer for layer in layers if layer not in LATE])

            @block.vector
            def _(dve):
                dve.memset(k.minus_half[:, :], -0.5).then_inc(k.s_filled, 1)
                dve.memset(k.ones[:, :], 1.0).then_inc(k.s_filled, 1)
                dve.memset(k.eps[:, :], LN_EPS).then_inc(k.s_filled, 1)
                dve.wait_ge(s_const, 96)
                dve.tensor_copy(k.ident_bf[:, :], k.ident[:, :]).then_inc(k.s_filled, 1)
                dve.tensor_copy(k.select[:, :, :], bcast(k.part_of[:, :].unsqueeze(2), [P, NE3, P]))\
                   .then_inc(k.s_filled, 1)
                dve.wait_ge(k.s_filled, 5)
                dve.wait_ge(s_x, 16)

            @block.scalar
            def _(act):
                act.wait_ge(s_const, 96)
                act.activation(k.tanh_g[:, :], k.g_in[:, :], ACT.Tanh).then_inc(s_tanh, 1)
                act.wait_ge(s_tanh, 1)

        early = [layer for layer in layers if layer in ("l0x", "l0f", "l1x")]
        late = [layer for layer in layers if layer in LATE]
        for layer in early:
            LAYERS[layer](nc, k)
        for layer in late:
            for name, shape in WEIGHTS[layer].items():
                k.weight(layer, name, shape)
        with nc.Block() as block:
            @block.sync
            def _(sp):
                load_weights(k, sp, late)

        for layer in layers[len(early):]:
            LAYERS[layer](nc, k)

        with nc.Block() as block:
            @block.sync
            def _(sp):
                sp.dma_start(out, k.x_sb[:, :]).then_inc(s_out, 16)
                sp.wait_ge(s_out, 16)


def layouts(i):
    f = lambda a: np.ascontiguousarray(a, dtype=np.float32)
    pad = lambda a, rows: np.concatenate([a, np.zeros((rows - a.shape[0],) + a.shape[1:], np.float32)])
    tok = lambda a: f(np.transpose(a, (1, 0, 2)).reshape(P, NSEQ * P))
    d = launch_constants()
    d["x"] = tok(i["x"])
    d["ctx_tok"] = tok(i["ctx_1024"])
    d["ctxT"] = f(np.transpose(i["ctx_1024"], (2, 0, 1)).reshape(P, NSEQ * P))
    d["gains"] = f(np.concatenate([i["g_xattn"], i["g_ffn"]]).reshape(1, 8))
    swap = np.arange(P) ^ 1
    by_d = np.arange(P).reshape(HEADS, HD).T.ravel()
    for n in (0, 1):
        for m in "qk":
            wm, bm = i[f"L{n}_xattn_W{m}"], i[f"L{n}_xattn_b{m}"]
            d[f"l{n}x_w{m}"], d[f"l{n}x_b{m}"] = f(wm[by_d].T), f(bm[by_d].reshape(P, 1))
            if n == 0:
                d[f"l0x_w{m}s"], d[f"l0x_b{m}s"] = f(wm[swap][by_d].T), f(bm[swap][by_d].reshape(P, 1))
        d[f"l{n}x_wv"], d[f"l{n}x_wo"] = f(i[f"L{n}_xattn_Wv"].T), f(i[f"L{n}_xattn_Wo"].T)
        d[f"l{n}x_bv"], d[f"l{n}x_bo"] = f(i[f"L{n}_xattn_bv"].reshape(P, 1)), f(i[f"L{n}_xattn_bo"].reshape(1, P))
    d["l0f_w1"] = f(i["L0_ffn_w1"].T)
    d["l0f_w2"] = f(np.transpose(i["L0_ffn_w2"].T.reshape(NHB, P, P), (1, 0, 2)))
    d["l0f_cw"] = f(np.transpose(i["L0_ffn_conv_w"].reshape(NHB, P, 3), (1, 0, 2)).reshape(P, 3 * NHB))
    d["l0f_cb"] = f(i["L0_ffn_conv_b"].reshape(NHB, P).T)
    d["l2f_router"] = f(i["L2_ffn_router_W"])
    d["l2f_router_b"] = f(np.tile(i["L2_ffn_router_b"].reshape(1, NE2), (1, GS)))
    d["l2f_w1"] = f(np.transpose(i["L2_ffn_W1"], (1, 0, 2)).reshape(P, NE2 * HID))
    d["l2f_b1"] = f(i["L2_ffn_b1"].reshape(1, NE2 * HID))
    d["l2f_w2"] = f(np.transpose(i["L2_ffn_W2"].reshape(NE2, NHB, P, P), (2, 0, 1, 3)).reshape(P, NE2 * HID))
    d["l2f_b2"] = f(i["L2_ffn_b2"].reshape(1, NE2 * P))
    for n in range(3):
        d[f"l2x_w{n + 1}"] = f(i["L2_xattn_w_sim"][n * P:(n + 1) * P].reshape(P, 1))
    d["l2x_bsim"] = f(i["L2_xattn_b_sim"].reshape(1, 1))
    d["l2x_wqv"] = f(np.transpose(i["L2_xattn_W_qv"].reshape(4, P, P), (1, 0, 2)))
    d["l2x_bqv"] = f(i["L2_xattn_b_qv"].reshape(1, P))
    for n in "qkvo":
        d[f"l3f_{n}"] = f(np.transpose(i[f"L3_ffn_{n}_proj"], (1, 0, 2)))
    d["l3f_sim"] = f(i["L3_ffn_sim_matrix"])
    d["l3f_gates"] = f(i["L3_ffn_gates"].reshape(1, NE3))
    d["l3x_wq"], d["l3x_wk"], d["l3x_wv"] = (f(i[f"L3_xattn_W{n}"]) for n in "qkv")
    d["l3x_bq"], d["l3x_bk"] = (f(i[f"L3_xattn_b{n}"].reshape(P, 1)) for n in "qk")
    d["l3x_bv"] = f(i["L3_xattn_bv"].reshape(1, P))
    flat_a = lambda a: np.transpose(a, (1, 0, 2)).reshape(a.shape[1], NZ)
    d["l1f_ar1"] = f(np.concatenate([flat_a(i["L1_ffn_A1"]), i["L1_ffn_R1"]], 1))
    d["l1f_w1"] = f(i["L1_ffn_W1"])
    d["l1f_b1"] = f(pad(np.concatenate([i["L1_ffn_B1"].reshape(NZ, HID), i["L1_ffn_b1"][None]]), P))
    w2ar = np.concatenate([i["L1_ffn_W2"], flat_a(i["L1_ffn_A2"]), i["L1_ffn_R2"]], 1)
    d["l1f_w2ar"] = f(np.transpose(w2ar.reshape(NHB, P, P + NZL), (1, 0, 2)))
    d["l1f_b2"] = f(pad(np.concatenate([i["L1_ffn_B2"].reshape(NZ, P), i["L1_ffn_b2"][None]]), P))
    return d


def kernel(**inputs):
    import concourse.bacc as bacc
    from concourse.bass_utils import run_bass_kernel_spmd

    arrays = layouts({n: np.asarray(a) for n, a in inputs.items()})
    nc = bacc.Bacc("TRN2", target_bir_lowering=False, num_devices=1)
    dram = {n: nc.dram_tensor(f"in_{n}", a.shape, mybir.dt.from_np(a.dtype), kind="ExternalInput").ap()
            for n, a in arrays.items()}
    out = nc.dram_tensor("out_x", (P, NSEQ * P), F32, kind="ExternalOutput").ap()
    program(nc, dram, out, list(LAYERS))
    r = run_bass_kernel_spmd(nc, [{f"in_{n}": a for n, a in arrays.items()}], core_ids=[0])
    x = r.results[0]["out_x"]
    return np.ascontiguousarray(x.reshape(P, NSEQ, P).transpose(1, 0, 2))
```

```python
from contextlib import ExitStack

import numpy as np
import concourse.bass as bass
from concourse import mybir

F32 = mybir.dt.float32
BF16 = mybir.dt.bfloat16
I32 = mybir.dt.int32
ALU = mybir.AluOpType
ACT = mybir.ActivationFunctionType
AX = mybir.AxisListType.X

P = 128
NSEQ = 32
GS = 4
NG = NSEQ // GS
T = GS * P
HEADS, HD = 16, 8
HID = 512
NHB = HID // P
LN_EPS = 1e-5
MAGIC = 12582912.0


class Ring:

    def __init__(self, sem, depth):
        self.sem, self.depth = sem, depth

    def grant(self, eng):
        eng.sem_inc(self.sem, self.depth)

    def wait_free(self, eng, unit):
        eng.wait_ge(self.sem, unit + 1)

    def wait_done(self, eng, unit):
        eng.wait_ge(self.sem, unit + 1 + self.depth)


class Chain:

    def __init__(self, eng, sem, links, it):
        self.eng, self.sem, self.links, self.it, self.n = eng, sem, links, it, 0

    def __call__(self, ins):
        self.n += 1
        ins.then_inc(self.sem, 1)
        self.eng.wait_ge(self.sem, self.it * self.links + self.n)


class Core:
    pass


def seq(c):
    return slice(c * P, (c + 1) * P)


def bcast(ap, shape):
    return ap.broadcast_to(shape)


def ln_tensors(k, sb, sem):
    k.stats = sb("ln_stats", [P, GS, 6], F32)
    k.mv = sb("ln_mean_var", [P, GS, 2], F32)
    k.rstd = sb("ln_rstd", [P, GS], F32)
    k.xn = sb("xn", [P, GS, P], F32)
    k.xnT = sb("xnT", [P, 2, T], F32)
    k.s_rows = sem("ln_rows_counted")
    k.s_stats = sem("ln_stats_ready")
    k.s_vare = sem("ln_var_plus_eps")
    k.s_rstd = sem("ln_rstd_ready")
    k.s_xn = sem("xn_ready")
    k.r_xnT_psum = Ring(sem("xnT_in_psum"), 1)
    k.r_xnT = Ring(sem("xnT_ready"), 1)
    k.r_xnT_used = Ring(sem("xnT_used"), 2)


def ln_stats(k, dve, g):
    for c in range(GS):
        ins = dve.bn_stats(k.stats[:, c, :], k.x_sb[:, bass.ds((g * GS + c) * P, P)])
    ins.then_inc(k.s_rows, 1)
    dve.wait_ge(k.s_rows, g + 1)
    dve.tensor_copy(k.one_cell[:, :], k.eps[:, 0:1])
    for c in range(GS):
        ins = dve.bn_aggr(k.mv[:, c, :], k.stats[:, c, :])
    ins.then_inc(k.s_stats, 1)


def ln_rstd(k, pool, g):
    pool.wait_ge(k.s_stats, g + 1)
    pool.tensor_tensor(k.rstd[:, :], k.mv[:, :, 1], k.eps[:, :], ALU.add).then_inc(k.s_vare, 1)
    pool.wait_ge(k.s_vare, g + 1)
    pool.tensor_tensor(k.rstd[:, :], k.rstd[:, :], k.minus_half[:, 0:GS], ALU.pow).then_inc(k.s_rstd, 1)


def ln_apply(k, dve, g):
    dve.wait_ge(k.s_rstd, g + 1)
    k.r_xnT_psum.wait_free(dve, g)
    for c in range(GS):
        ins = dve.tensor_scalar(k.xn[:, c, :], k.x_sb[:, bass.ds((g * GS + c) * P, P)],
                                k.mv[:, c, 0:1], k.rstd[:, c:c + 1], ALU.subtract, ALU.mult)
    ins.then_inc(k.s_xn, 1)


def ln_transpose(k, pe, g, bank):
    pe.wait_ge(k.s_xn, g + 1)
    k.r_xnT.wait_free(pe, g)
    for c in range(GS):
        ins = pe.transpose(bank[:, seq(c)], k.xn[:, c, :], k.ident[:, :])
    ins.then_inc(k.r_xnT_psum.sem, 1)


def ln_evacuate(k, act, g, par, bank):
    k.r_xnT_psum.wait_done(act, g)
    k.r_xnT_used.wait_free(act, g)
    act.activation(k.xnT[:, par, :], bank[:, :], ACT.Copy).then_inc(k.r_xnT.sem, 1)


def groups(eng, body, chain_sem=None, links=0):
    links = links if isinstance(links, tuple) else (links, links)
    per_pair = links[0]

    def two(it, last):
        chain = Chain(eng, chain_sem, per_pair, it)
        for par in range(2):
            body(2 * it + par, par, not (last and par), chain)
        assert chain.n == links[last], f"{chain.n} links, not {links[last]}"

    with eng.Fori(0, NG // 2 - 1) as it:
        two(it, False)
    two(NG // 2 - 1, True)


NPART = 3
SROWS = NPART * NPART * HD


def heads_attention(nc, k, name, rope, gain):
    with ExitStack() as ctx:
        sb, sem = k.local(ctx, name)
        ln_tensors(k, sb, sem)
        w = {n[len(name) + 1:]: t for n, t in k.w.items() if n.startswith(name + "_")}
        ctxT = sb("ctxT", [P, 2, T], F32)
        gb = sb("tanh_g_bias", [P, GS, P], F32)
        bias = sb("out_bias", [P, P], F32)
        turned = {n: [sb(f"{n}_turned{i}", [P, T], F32) for i in range(2)] for n in "kq"} if rope else None
        full = {n: sb(f"{n}_full", [P, T], F32) for n in "kq"}
        rest = sb("rest", [P, T], F32)
        parts = {n: sb(f"{n}_parts", [P, NPART, T], BF16) for n in "kq"}
        stack = {n: sb(f"{n}_stack", [SROWS, 2, HEADS, T], BF16) for n in "kq"}
        v1 = sb("v_and_one", [P, 2, GS, HEADS, HD + 1], F32)
        nm = sb("minus_max", [P, GS, HEADS], F32)
        nm_rest = sb("minus_max_rest", [P, HEADS], F32)
        mp = sb("minus_max_parts", [P, GS, P], BF16)
        mT = sb("minus_max_T", [P, T], BF16)
        pT = sb("probsT", [P, 2, HEADS, P], F32)
        ae = sb("attn_sums_T", [P, T], F32)
        rz = sb("rsum", [P, HEADS], F32)
        an = sb("attn", [P, P], F32)
        aT = sb("aT", [P, 2, P], F32)
        bankS, bankT = [k.bank(0), k.bank(1)], [k.bank(2), k.bank(3)]
        bankA, bankP0, bankP1 = (k.bank(i) for i in range(4, 7))
        bankM = k.bank(7)
        scale = float(HD) ** -0.5
        scratch = {"k": nc.dram_tensor(f"{name}_k_scratch", (2, SROWS * HEADS, T), BF16).ap(),
                   "q": nc.dram_tensor(f"{name}_q_scratch", (2, NPART, P, T), BF16).ap()}

        s_fill = sem("fills_done")
        s_bias = sem("bias_step")
        s_bp = sem("v_bias_in_psum")
        s_chain = sem("dve_step")
        s_split = sem("pool_step")
        s_ctx = [sem(f"ctxT_in_{p}") for p in range(2)]
        s_proj = {n: sem(f"{n}_in_psum") for n in "kqv"}
        r_out = {n: Ring(sem(f"{n}_emptied"), 1) for n in "kq"}
        r_v = Ring(sem("v_ready"), 1)
        r_full = {n: Ring(sem(f"{n}_split"), 1) for n in "kq"}
        s_slot = sem("stack_slot_free")
        s_stack = [sem(f"stack_in_{p}") for p in range(2)]
        s_head = sem("pool_head_step")
        s_nm = sem("minus_max_ready")
        s_s = sem("scores_in_psum")
        r_red = Ring(sem("maxima_taken"), 2)
        r_mp = Ring(sem("minus_max_split"), GS)
        r_mT = Ring(sem("minus_maxT_in_psum"), GS)
        r_mTs = Ring(sem("minus_maxT_ready"), 1)
        s_parts_out = {n: sem(f"{n}_parts_in_dram") for n in "kq"}
        s_t = sem("scoresT_in_psum")
        r_exp = Ring(sem("exp_done"), 2)
        r_av = Ring(sem("attn_in_psum"), 2)
        s_ae = sem("attn_sums_T_ready")
        s_turned = sem("attn_sums_in_psum")
        s_an = sem("attn_ready")
        s_back = sem("aT_in_psum")
        r_aT = Ring(sem("aT_ready"), 1)
        r_o = Ring(sem("out_in_psum"), 2)
        r_x = Ring(sem("x_updated"), 1)

        def landed(eng, sems, g, par, dmas):
            eng.wait_ge(sems[par], (g - par) * 8 * dmas + 16 * dmas)

        block = ctx.enter_context(nc.Block())

        @block.sync
        def _(sp):
            def load_ctx(g, par):
                if not isinstance(g, int):
                    sp.wait_ge(s_proj["v"], g - 1)
                sp.dma_start(ctxT[:, par, :], k.dram["ctxT"][:, bass.ds(g * T, T)]).then_inc(s_ctx[par], 16)

            def k_parts_out(g, par):
                r_full["k"].wait_done(sp, g)
                copies = scratch["k"][par, 0:SROWS * HEADS, :].rearrange("(x y p) t -> y p x t", y=NPART, p=P)
                for y in range(NPART):
                    sp.dma_start(copies[y], parts["k"][:, :, :])\
                      .then_inc(s_parts_out["k"], 16)

            def q_parts_out(g, par):
                r_full["q"].wait_done(sp, g)
                sp.dma_start(scratch["q"][par].rearrange("y p t -> p y t"), parts["q"][:, :, :])\
                  .then_inc(s_parts_out["q"], 16)

            def build_k(g, par):
                sp.wait_ge(s_parts_out["k"], 16 * NPART * (g + 1))
                sp.dma_start(stack["k"][:, par, :, :],
                             scratch["k"][par].rearrange("(r h) t -> r h t", h=HEADS)).then_inc(s_stack[par], 16)

            def build_q(g, par):
                sp.wait_ge(s_parts_out["q"], 16 * (g + 1))
                for x in range(NPART):
                    sp.dma_start(stack["q"][x * NPART * HD:(x + 1) * NPART * HD, par, :, :],
                                 scratch["q"][par].rearrange("y (d h) t -> (y d) h t", d=HD)).then_inc(s_stack[par], 16)

            load_ctx(0, 0)
            load_ctx(1, 1)
            k.load_rest_of_x(sp)
            for g in range(2):
                k_parts_out(g, g)
                build_k(g, g)
                q_parts_out(g, g)
                build_q(g, g)

            def body(t, par, more, chain):
                if not isinstance(t, int):
                    load_ctx(t + 2, par)
                    k_parts_out(t + 2, par)
                    q_parts_out(t + 2, par)
                    sp.wait_ge(s_t, (t + 1) * GS * 4)
                    sp.sem_inc(s_slot, 1)
                    build_k(t + 2, par)
                    build_q(t + 2, par)

            groups(sp, body)
            k.load_other_weights(sp)

        @block.tensor
        def _(pe):
            for r in (k.r_xnT_psum, k.r_xnT_used, r_mT, r_av, r_o):
                r.grant(pe)
            k.wait_weights(pe, name)
            pe.matmul(bankM[:, 0:P], bcast(w["bv"][:, 0:1], [P, P]), w["wo"][:, :], start=True, stop=True)\
              .then_inc(s_bp, 1)
            pe.wait_ge(s_bias, 1)
            pe.wait_ge(s_fill, 3)

            def project(n, g, par, src):
                last = None
                for bank, kind in ((bankP0, ""), (bankP1, "s"))[:2 if rope else 1]:
                    last = pe.matmul(bank[:, :], w[f"w{n}{kind}"][:, :], src, start=True, stop=True)
                last.then_inc(s_proj[n], 1)

            def turn_xn(g):
                r_out["q"].wait_free(pe, g)
                if rope:
                    r_out["k"].wait_done(pe, g)
                ln_transpose(k, pe, g, bankP1)

            def project_k(g, par):
                r_v.wait_free(pe, g)
                landed(pe, s_ctx, g, par, 1)
                if not isinstance(g, int):
                    r_mTs.wait_done(pe, (g - 2) * GS + 3)
                project("k", g, par, ctxT[:, par, :])

            def project_q(g, par):
                r_out["k"].wait_done(pe, g)
                k.r_xnT.wait_done(pe, g)
                project("q", g, par, k.xnT[:, par, :])

            def project_v(g, par):
                r_out["q"].wait_done(pe, g)
                pe.sem_inc(k.r_xnT_used.sem, 1)
                for c in range(GS):
                    ins = pe.matmul(bankP0[:, seq(c)], ctxT[:, par, seq(c)], w["wv"][:, :], start=True, stop=True)
                ins.then_inc(s_proj["v"], 1)

            def scores(g, par, c, u):
                if c == 0 and u == 0:
                    landed(pe, s_stack, g, par, 1 + NPART)
                unit = (g * GS + c) * 4 + u
                r_red.wait_free(pe, unit)
                for j in range(4):
                    h = 4 * u + j
                    ins = pe.matmul(bankS[u % 2][:, seq(j)], stack["q"][0:SROWS, par, h, seq(c)],
                                    stack["k"][0:SROWS, par, h, seq(c)], start=True, stop=True)
                ins.then_inc(s_s, 1)

            def turn_max(g, c, queries_due=None):
                if c == 0 and queries_due is not None:
                    r_out["q"].wait_done(pe, queries_due)
                r_mp.wait_done(pe, g * GS + c)
                r_mTs.wait_free(pe, g * GS + c)
                pe.matmul(bankP1[:, seq(c)], mp[:, c, :], k.ident_bf[:, :], start=True, stop=True)\
                  .then_inc(r_mT.sem, 1)

            def scoresT(g, par, c, u):
                if u == 0:
                    r_mTs.wait_done(pe, g * GS + c)
                r_exp.wait_free(pe, (g * GS + c) * 4 + u)
                for j in range(4):
                    h = 4 * u + j
                    pe.matmul(bankT[u % 2][:, seq(j)], stack["k"][:, par, h, seq(c)],
                              stack["q"][:, par, h, seq(c)], start=True, stop=False)
                    ins = pe.matmul(bankT[u % 2][:, seq(j)], k.select[:, h, :], mT[:, seq(c)], start=False, stop=True)
                ins.then_inc(s_t, 1)

            def attend(g, par, c):
                unit = g * GS + c
                r_exp.wait_done(pe, unit * 4 + 3)
                r_aT.wait_free(pe, unit)
                for h in range(HEADS):
                    row = 32 * (h % 4)
                    ins = pe.matmul(bankA[row:row + HD + 1, seq(h // 4)], v1[:, par, c, h, :], pT[:, c % 2, h, :],
                                    start=True, stop=True)
                ins.then_inc(r_av.sem, 1)

            def turn(g, c):
                unit = g * GS + c
                pe.wait_ge(s_ae, unit + 1)
                r_x.wait_free(pe, unit)
                for u in range(4):
                    ins = pe.transpose(bankM[:, seq(u)], ae[:, seq(u)], k.ident[:, :])
                ins.then_inc(s_turned, 1)

            def back(g, c):
                pe.wait_ge(s_an, g * GS + c + 1)
                pe.transpose(bankA[:, 0:P], an[:, :], k.ident[:, :]).then_inc(s_back, 1)

            def out(g, c):
                unit = g * GS + c
                r_aT.wait_done(pe, unit)
                pe.matmul(bankM[:, 0:P], aT[:, c % 2, :], w["wo"][:, :], start=True, stop=True).then_inc(r_o.sem, 1)

            for g in range(2):
                project_k(g, g)
                turn_xn(g)
                project_q(g, g)
                project_v(g, g)
            for c in range(GS):
                for u in range(4):
                    scores(0, 0, c, u)
                if c > 0:
                    turn_max(0, c - 1, 1)

            def body(t, par, more, chain):
                after = not isinstance(t, int)

                def step(ct, cs, *between):
                    for u in range(4):
                        if ct is not None:
                            scoresT(t, par, ct, u)
                        if cs is not None and more:
                            scores(t + 1, 1 - par, cs, u)
                        for at, what in between:
                            if at == u:
                                what()

                att = lambda c: (1, lambda: attend(t, par, c))
                put = lambda c, at=0: (at, lambda: out(t, c))
                step(0, None)
                turn_max(t, 3)
                if after:
                    project_k(t + 2, par)
                step(1, None, att(0))
                turn(t, 0)
                if after:
                    turn_xn(t + 2)
                back(t, 0)
                if after:
                    project_q(t + 2, par)
                step(2, 0, put(0), att(1))
                turn(t, 1)
                back(t, 1)
                step(3, 1, put(1), att(2))
                turn(t, 2)
                if more:
                    turn_max(t + 1, 0, t + 2 if after else None)
                back(t, 2)
                step(None, 2, put(2), att(3))
                turn(t, 3)
                if more:
                    turn_max(t + 1, 1)
                step(None, 3, (0, lambda: back(t, 3)), put(3, 2))
                if after:
                    project_v(t + 2, par)
                if more:
                    turn_max(t + 1, 2)

            groups(pe, body)

        @block.scalar
        def _(act):
            for r in (k.r_xnT, r_v, r_mTs, r_exp, r_aT) + (() if rope else (r_out["k"], r_out["q"])):
                r.grant(act)
            k.wait_weights(act, name)
            act.wait_ge(s_fill, 3)

            def evacuate(n, g):
                if not rope:
                    act.wait_ge(s_proj[n], g + 1)
                    r_full[n].wait_free(act, g)
                    act.activation(full[n][:, :], bankP0[:, :], ACT.Identity, bias=w["b" + n][:, :])\
                       .then_inc(r_out[n].sem, 1)

            def v_out(g, par):
                act.wait_ge(s_proj["v"], g + 1)
                act.activation(v1[:, par, :, :, 0:HD], bankP0.rearrange("p (c h d) -> p c h d", c=GS, h=HEADS), ACT.Copy)\
                   .then_inc(r_v.sem, 1)

            def max_out(g, c):
                r_mT.wait_done(act, g * GS + c)
                act.activation(mT[:, seq(c)], bankP1[:, seq(c)], ACT.Copy).then_inc(r_mTs.sem, 1)

            def exps(g, c, units):
                unit = g * GS + c
                if units[0] == 0:
                    r_av.wait_free(act, unit)
                for u in units:
                    act.wait_ge(s_t, unit * 4 + u + 1)
                    act.activation(pT[:, c % 2, 4 * u:4 * u + 4, :], bankT[u % 2].rearrange("p (j q) -> p j q", j=4),
                                   ACT.Exp, scale=scale).then_inc(r_exp.sem, 1)

            def attn_out(g, c):
                unit = g * GS + c
                r_av.wait_done(act, unit)
                act.activation(ae[:, :], bankA[:, :], ACT.Copy).then_inc(s_ae, 1)

            def aT_out(g, c):
                unit = g * GS + c
                act.wait_ge(s_back, unit + 1)
                r_o.wait_free(act, unit)
                act.activation(aT[:, c % 2, :], bankA[:, 0:P], ACT.Copy).then_inc(r_aT.sem, 1)

            for g in range(2):
                evacuate("k", g)
                ln_evacuate(k, act, g, g, bankP1)
                evacuate("q", g)
                v_out(g, g)
            for c in range(GS - 1):
                max_out(0, c)

            def body(t, par, more, chain):
                after = not isinstance(t, int)
                exps(t, 0, range(4))
                max_out(t, 3)
                if after:
                    evacuate("k", t + 2)
                exps(t, 1, (0, 1))
                attn_out(t, 0)
                exps(t, 1, (2, 3))
                if after:
                    ln_evacuate(k, act, t + 2, par, bankP1)
                aT_out(t, 0)
                if after:
                    evacuate("q", t + 2)
                exps(t, 2, (0, 1))
                attn_out(t, 1)
                exps(t, 2, (2, 3))
                aT_out(t, 1)
                exps(t, 3, (0, 1))
                attn_out(t, 2)
                exps(t, 3, (2, 3))
                if more:
                    max_out(t + 1, 0)
                aT_out(t, 2)
                attn_out(t, 3)
                if more:
                    max_out(t + 1, 1)
                aT_out(t, 3)
                if after:
                    v_out(t + 2, par)
                if more:
                    max_out(t + 1, 2)

            groups(act, body)

        @block.gpsimd
        def _(pool):
            for r in (r_full["k"], r_full["q"], r_mp):
                r.grant(pool)
            pool.memset(v1[:, :, :, :, :], 1.0).then_inc(s_fill, 1)

            def split(n, g, chain):
                if rope:
                    pool.wait_ge(r_out[n].sem, g + 2)
                    chain(pool.tensor_tensor(full[n][:, :], turned[n][0][:, :], turned[n][1][:, :], ALU.add))
                else:
                    r_out[n].wait_done(pool, g)
                if not isinstance(g, int) or g > 0:
                    pool.wait_ge(s_parts_out[n], (16 * NPART if n == "k" else 16) * g)
                p = [parts[n][:, a, :] for a in range(NPART)]
                chain(pool.tensor_tensor(p[0], full[n][:, :], bcast(k.ones[:, 0:1], [P, T]), ALU.mult))
                chain(pool.tensor_tensor(rest[:, :], full[n][:, :], p[0], ALU.subtract))
                chain(pool.tensor_tensor(p[1], rest[:, :], bcast(k.ones[:, 0:1], [P, T]), ALU.mult))
                pool.tensor_tensor(p[2], rest[:, :], p[1], ALU.subtract).then_inc(r_full[n].sem, 1)
                r_full[n].wait_done(pool, g)

            def split_max(g, c, chain):
                unit = g * GS + c
                pool.wait_ge(s_nm, unit + 1)
                r_mT.wait_free(pool, unit)
                part = lambda a: mp[:, c, a * HEADS:(a + 1) * HEADS]
                chain(pool.tensor_tensor(part(0), nm[:, c, :], k.ones[:, 0:HEADS], ALU.mult))
                chain(pool.tensor_tensor(nm_rest[:, :], nm[:, c, :], part(0), ALU.subtract))
                chain(pool.tensor_tensor(part(1), nm_rest[:, :], k.ones[:, 0:HEADS], ALU.mult))
                pool.tensor_tensor(part(2), nm_rest[:, :], part(1), ALU.subtract).then_inc(r_mp.sem, 1)
                r_mp.wait_done(pool, unit)

            head = Chain(pool, s_head, 0, 0)
            ln_rstd(k, pool, 0)
            ln_rstd(k, pool, 1)
            for g in range(2):
                split("k", g, head)
                split("q", g, head)
            for c in range(GS):
                split_max(0, c, head)

            def body(t, par, more, chain):
                after = not isinstance(t, int)
                if after:
                    ln_rstd(k, pool, t + 2)
                    split("k", t + 2, chain)
                    split("q", t + 2, chain)
                if more:
                    for c in range(GS):
                        split_max(t + 1, c, chain)

            groups(pool, body, s_split, (36 + 4 * rope, 12))

        @block.vector
        def _(dve):
            r_red.grant(dve)
            r_x.grant(dve)
            if rope:
                r_out["k"].grant(dve)
                r_out["q"].grant(dve)
            dve.memset(mp[:, :, NPART * HEADS:], 0.0).then_inc(s_fill, 1)
            dve.memset(bankA[:, :], 0.0).then_inc(s_fill, 1)
            k.wait_weights(dve, name)
            dve.wait_ge(s_bp, 1)
            dve.tensor_tensor(bias[:, :], bankM[:, 0:P], w["bo"][:, :], ALU.add).then_inc(s_bias, 1)
            dve.wait_ge(s_bias, 1)
            for c in range(GS):
                ins = dve.tensor_scalar(gb[:, c, :], bias[:, :], k.tanh_g[:, gain:gain + 1], None, ALU.mult)
            ins.then_inc(s_bias, 1)
            dve.wait_ge(s_bias, 2)

            def norm(g):
                ln_apply(k, dve, g)
                dve.wait_ge(k.s_xn, g + 1)
                xs = k.x_sb[:, bass.ds(g * T, T)]
                dve.tensor_tensor(xs, xs, gb[:, :, :].rearrange("p c d -> p (c d)"), ALU.add)

            def rotate(n, g):
                if rope:
                    dve.wait_ge(s_proj[n], g + 1)
                    r_full[n].wait_free(dve, g)
                    dve.scalar_tensor_tensor(turned[n][0][:, :], bankP0[:, :], w["b" + n][:, :], w["cos"][:, :],
                                             ALU.add, ALU.mult)
                    dve.scalar_tensor_tensor(turned[n][1][:, :], bankP1[:, :], w["b" + n + "s"][:, :],
                                             w["sin"][:, :], ALU.add, ALU.mult).then_inc(r_out[n].sem, 1)

            def maxima(g, c, units):
                if units[0] == 0:
                    r_mp.wait_free(dve, g * GS + c)
                for u in units:
                    unit = (g * GS + c) * 4 + u
                    dve.wait_ge(s_s, unit + 1)
                    dve.tensor_reduce(nm[:, c, 4 * u:4 * u + 4], bankS[u % 2].rearrange("p (j t) -> p j t", j=4), AX,
                                      ALU.max, negate=True).then_inc(r_red.sem, 1)
                if units[-1] == 3:
                    r_red.wait_done(dve, (g * GS + c) * 4 + 3)
                    dve.sem_inc(s_nm, 1)

            def normalise(g, c, chain):
                dve.wait_ge(s_turned, g * GS + c + 1)
                both = bankM.rearrange("p (h n) -> p h n", n=32)
                chain(dve.reciprocal(rz[:, :], both[:, :, HD]))
                dve.tensor_tensor(an[:, :].rearrange("p (h d) -> p h d", d=HD), both[:, :, 0:HD],
                                  bcast(rz[:, :].unsqueeze(2), [P, HEADS, HD]), ALU.mult).then_inc(s_an, 1)

            def update(g, c):
                unit = g * GS + c
                r_o.wait_done(dve, unit)
                xc = k.x_sb[:, bass.ds(unit * P, P)]
                dve.scalar_tensor_tensor(xc, bankM[:, 0:P], k.tanh_g[:, gain:gain + 1], xc, ALU.mult, ALU.add)\
                   .then_inc(r_x.sem, 1)

            ln_stats(k, dve, 0)
            rotate("k", 0)
            norm(0)
            ln_stats(k, dve, 1)
            rotate("q", 0)
            rotate("k", 1)
            norm(1)
            rotate("q", 1)
            for c in range(GS):
                maxima(0, c, range(4))
            dve.wait_ge(k.s_x, 16)

            def body(t, par, more, chain):
                after = not isinstance(t, int)

                def between(c, first, second):
                    if more:
                        maxima(t + 1, c, first)
                    update(t, c)
                    if more:
                        maxima(t + 1, c, second)

                if after:
                    ln_stats(k, dve, t + 2)
                    norm(t + 2)
                    rotate("k", t + 2)
                normalise(t, 0, chain)
                if after:
                    rotate("q", t + 2)
                between(0, (0, 1), (2, 3))
                normalise(t, 1, chain)
                between(1, (0, 1), (2, 3))
                normalise(t, 2, chain)
                between(2, (0, 1), (2, 3))
                normalise(t, 3, chain)
                between(3, (0, 1, 2), (3,))

            groups(dve, body, s_chain, (2 * GS, 2 * GS))


def layer0_attention(nc, k):
    heads_attention(nc, k, "l0x", True, 0)


def layer1_attention(nc, k):
    heads_attention(nc, k, "l1x", False, 1)


def layer0_ffn(nc, k):
    with ExitStack() as ctx:
        sb, sem = k.local(ctx, "l0f")
        ln_tensors(k, sb, sem)
        w = k.w
        wsum = sb("abs_sums", [P, 2], F32)
        wmean = sb("abs_mean", [P, 2], F32)
        winv = sb("abs_rmean", [P, 2], F32)
        wr = sb("w_steps", [P, 2, HID], F32)
        w1c = sb("w1_by_tap", [P, 3, HID], F32)
        w2q = sb("w2q", [P, NHB, P], BF16)
        amax = sb("amax", [P, GS], F32)
        qs = sb("q_scale", [P, GS], F32)
        dq = sb("q_step", [P, GS], F32)
        xr = sb("xn_steps", [P, GS, P], F32)
        xq = sb("xq", [P, GS, P], F32)
        xqT = sb("xqT", [P, 2, GS, P], F32)
        hT = sb("hT", [P, 2, NHB, T], F32)
        hm = sb("h_absmax", [P, T], F32)
        qr = sb("q2_steps", [P, NHB, T], F32)
        q2 = sb("q2", [P, NHB, T], BF16)
        top = sb("row_scales", [P, 6, GS], F32)
        gw = sb("tanh_g_w2_step", [P, 1], F32)
        bankX, bankR, bankM, bankY, bankT = (k.bank(i) for i in range(5))
        bankH = [k.bank(5), k.bank(6)]

        s_prep = sem("prep_step")
        s_wsum = sem("abs_sums_spread")
        s_chain = sem("dve_step")
        s_first = sem("first_quant_step")
        s_quant = sem("xq_ready")
        r_qT = Ring(sem("xqT_in_psum"), 1)
        r_qTs = Ring(sem("xqT_ready"), 1)
        r_conv = Ring(sem("convolved_in_psum"), 2 * NHB)
        r_act = Ring(sem("hT_ready"), 2)
        s_hm = sem("h_absmax_ready")
        r_hmT = Ring(sem("h_absmaxT_in_psum"), 1)
        s_sc = sem("row_scales_ready")
        s_scr = sem("row_scales_spread")
        r_q2 = Ring(sem("q2_ready"), 2)
        r_y = Ring(sem("y_in_psum"), 1)
        r_out = Ring(sem("x_updated"), 1)

        block = ctx.enter_context(nc.Block())

        @block.tensor
        def _(pe):
            for r in (r_qT, r_conv, r_hmT, r_y):
                r.grant(pe)
            k.wait_weights(pe, "l0f")
            pe.wait_ge(s_prep, 1)
            pe.matmul(bankM[:, 0:2], k.ones[:, :], wsum[:, :], start=True, stop=True).then_inc(s_wsum, 1)

            def turn_q(g):
                pe.wait_ge(s_quant, g + 1)
                r_qTs.wait_free(pe, g)
                for c in range(GS):
                    ins = pe.transpose(bankX[:, seq(c)], xq[:, c, :], k.ident[:, :])
                ins.then_inc(r_qT.sem, 1)

            def convolve(g, par, n):
                if n == 0:
                    r_qTs.wait_done(pe, g)
                r_act.wait_free(pe, g * NHB + n)
                out = bankH[n % 2].rearrange("p (c t) -> p c t", c=GS)
                pe.matmul(out, w1c[:, 1, seq(n)], xqT[:, par, :, :], start=True, stop=False)
                pe.matmul(out[:, :, 1:P], w1c[:, 0, seq(n)], xqT[:, par, :, 0:P - 1], start=False, stop=False)
                pe.matmul(out[:, :, 0:P - 1], w1c[:, 2, seq(n)], xqT[:, par, :, 1:P], start=False, stop=True)\
                  .then_inc(r_conv.sem, 1)

            turn_q(0)
            pe.wait_ge(s_prep, 7)
            for n in range(NHB):
                convolve(0, 0, n)

            def body(t, par, more, chain):
                if more:
                    turn_q(t + 1)
                    convolve(t + 1, 1 - par, 0)
                pe.wait_ge(s_hm, t + 1)
                for c in range(GS):
                    ins = pe.transpose(bankT[:, seq(c)], hm[:, seq(c)], k.ident[:, :])
                ins.then_inc(r_hmT.sem, 1)
                if more:
                    convolve(t + 1, 1 - par, 1)
                pe.wait_ge(s_sc, t + 1)
                for c in range(GS):
                    ins = pe.matmul(bankR[:, seq(c)], bcast(top[:, 3, c:c + 1], [P, P]), k.ident[:, :],
                                    start=True, stop=True)
                ins.then_inc(s_scr, 1)
                if more:
                    convolve(t + 1, 1 - par, 2)
                    convolve(t + 1, 1 - par, 3)
                r_q2.wait_done(pe, t)
                r_out.wait_free(pe, t)
                for c in range(GS):
                    for n in range(NHB):
                        ins = pe.matmul(bankY[:, seq(c)], q2[:, n, seq(c)], w2q[:, n, :], start=(n == 0),
                                        stop=(n == NHB - 1))
                ins.then_inc(r_y.sem, 1)

            groups(pe, body)

        @block.scalar
        def _(act):
            r_qTs.grant(act)
            r_act.grant(act)
            k.wait_weights(act, "l0f")

            def front(g, par):
                r_qT.wait_done(act, g)
                r_conv.wait_free(act, (g + 1) * NHB - 1)
                act.activation(xqT[:, par, :, :], bankX.rearrange("p (c t) -> p c t", c=GS), ACT.Copy)\
                   .then_inc(r_qTs.sem, 1)
                for n in range(NHB):
                    r_conv.wait_done(act, g * NHB + n)
                    if n == 0:
                        r_q2.wait_free(act, g)
                    act.activation(hT[:, par, n, :], bankH[n % 2][:, :], ACT.Silu,
                                   bias=w["l0f_cb"][:, n:n + 1]).then_inc(r_act.sem, 1)

            front(0, 0)
            groups(act, lambda t, par, more, chain: front(t + 1, 1 - par) if more else None)

        @block.gpsimd
        def _(pool):
            ln_rstd(k, pool, 0)
            ln_rstd(k, pool, 1)

            def body(t, par, more, chain):
                if not isinstance(t, int):
                    ln_rstd(k, pool, t + 2)

            groups(pool, body)

        @block.vector
        def _(dve):
            r_q2.grant(dve)
            r_out.grant(dve)
            k.wait_weights(dve, "l0f")
            prep = Chain(dve, s_prep, 0, 0)
            dve.tensor_reduce(wsum[:, 0:1], w["l0f_w1"][:, :], AX, ALU.add, apply_absolute_value=True)
            prep(dve.tensor_reduce(wsum[:, 1:2], w["l0f_w2"][:, :, :].rearrange("p n d -> p (n d)"), AX, ALU.add,
                                   apply_absolute_value=True))
            ln_stats(k, dve, 0)
            dve.wait_ge(s_wsum, 1)
            prep(dve.tensor_scalar(wmean[:, :], bankM[:, 0:2], 1.0 / (P * HID), 1e-5, ALU.mult, ALU.max))
            prep(dve.reciprocal(winv[:, :], wmean[:, :]))

            def round_weights():
                dve.tensor_scalar(wr[:, 0, :], w["l0f_w1"][:, :], winv[:, 0:1], MAGIC, ALU.mult, ALU.add)
                prep(dve.tensor_scalar(wr[:, 1, :], w["l0f_w2"][:, :, :].rearrange("p n d -> p (n d)"), winv[:, 1:2],
                                       MAGIC, ALU.mult, ALU.add))
                prep(dve.tensor_scalar(wr[:, :, :], wr[:, :, :], -MAGIC, 1.0, ALU.add, ALU.min))
                prep(dve.tensor_scalar(wr[:, 0, :], wr[:, 0, :], -1.0, None, ALU.max))
                for i in range(3):
                    dve.tensor_tensor(w1c[:, i, :], wr[:, 0, :], w["l0f_cw"][:, i * HID:(i + 1) * HID], ALU.mult)
                dve.tensor_scalar(gw[:, :], k.tanh_g[:, 4:5], wmean[:, 1:2], 1.0 / 127.0, ALU.mult, ALU.mult)
                prep(dve.tensor_scalar(w2q[:, :, :].rearrange("p n d -> p (n d)"), wr[:, 1, :], -1.0, None, ALU.max))

            def quantise(g, chain):
                dve.wait_ge(s_done_xn, g + 1)
                chain(dve.tensor_reduce(amax[:, :], k.xn[:, :, :], AX, ALU.max, apply_absolute_value=True))
                chain(dve.tensor_scalar(amax[:, :], amax[:, :], 1e-5, None, ALU.max))
                chain(dve.reciprocal(qs[:, :], amax[:, :]))
                chain(dve.tensor_scalar(qs[:, :], qs[:, :], 127.0, None, ALU.mult))
                r_qT.wait_free(dve, g)
                dve.tensor_scalar(dq[:, :], amax[:, :], 1.0 / 127.0, wmean[:, 0:1], ALU.mult, ALU.mult)
                for c in range(GS):
                    ins = dve.tensor_scalar(xr[:, c, :], k.xn[:, c, :], qs[:, c:c + 1], MAGIC, ALU.mult, ALU.add)
                chain(ins)
                for c in range(GS):
                    ins = dve.tensor_scalar(xq[:, c, :], xr[:, c, :], -MAGIC, dq[:, c:c + 1], ALU.add, ALU.mult)
                ins.then_inc(s_quant, 1)

            s_done_xn = k.s_xn
            k.r_xnT_psum = r_qT
            first = Chain(dve, s_first, 0, 0)
            ln_apply(k, dve, 0)
            quantise(0, first)
            round_weights()
            ln_stats(k, dve, 1)
            ln_apply(k, dve, 1)
            quantise(1, first)

            def body(t, par, more, chain):
                after = not isinstance(t, int)
                hidden = hT[:, par, :, :]
                if after:
                    ln_stats(k, dve, t + 2)
                r_act.wait_done(dve, t * NHB + 3)
                dve.tensor_reduce(hm[:, :], hidden.rearrange("p n t -> p t n"), AX, ALU.max,
                                  apply_absolute_value=True).then_inc(s_hm, 1)
                if after:
                    ln_apply(k, dve, t + 2)
                r_hmT.wait_done(dve, t)
                chain(dve.tensor_reduce(top[:, 0, :], bankT.rearrange("p (c t) -> p c t", c=GS), AX, ALU.max,
                                        apply_absolute_value=True))
                chain(dve.tensor_scalar(top[:, 1, :], top[:, 0, :], 1e-5, None, ALU.max))
                chain(dve.reciprocal(top[:, 2, :], top[:, 1, :]))
                dve.tensor_scalar(top[:, 3, :], top[:, 2, :], 127.0, None, ALU.mult).then_inc(s_sc, 1)
                dve.tensor_scalar(top[:, 4, :], top[:, 1, :], gw[:, 0:1], None, ALU.mult)
                if after:
                    quantise(t + 2, chain)
                dve.wait_ge(s_scr, t + 1)
                rows = bcast(bankR.unsqueeze(1), [P, NHB, T])
                chain(dve.tensor_tensor(qr[:, :, :], hidden, rows, ALU.mult))
                dve.tensor_scalar(q2[:, :, :], qr[:, :, :], MAGIC, MAGIC, ALU.add, ALU.subtract).then_inc(r_q2.sem, 1)
                r_y.wait_done(dve, t)
                for c in range(GS):
                    xc = k.x_sb[:, bass.ds((t * GS + c) * P, P)]
                    ins = dve.scalar_tensor_tensor(xc, bankY[:, seq(c)], top[:, 4, c:c + 1], xc, ALU.mult, ALU.add)
                ins.then_inc(r_out.sem, 1)

            groups(dve, body, s_chain, (18, 8))


NE1, RANK = 3, 8
NZ = NE1 * RANK
NZL = NZ + NE1
ZW = 32


def layer1_ffn(nc, k):
    with ExitStack() as ctx:
        sb, sem = k.local(ctx, "l1f")
        ln_tensors(k, sb, sem)
        shifted = sb("shifted", [P, GS, NE1], F32)
        expd = sb("expd", [P, GS, NE1], F32)
        small = sb("small", [P, 4, GS], F32)
        gate = sb("gate", [P, GS, NE1], F32)
        zg = sb("zg", [P, GS, ZW], F32)
        zgT = [sb(f"zgT_{n}", [P, T], F32) for n in ("first", "second")]
        hT = sb("hT", [P, NHB, T], F32)
        bankX, bankZ, bankZT, bankH, bankY, bankR = (
            k.bank(0), k.bank(1), k.bank(2), [k.bank(3), k.bank(4)], k.banks(5, 2), k.bank(7))
        zview = bankZ.rearrange("p (c w) -> p c w", c=GS)[:, :, 0:NZL]
        WY = P + NZL
        yview = bankY.rearrange("p (a w) -> p a w", a=2)[:, :, 0:2 * WY].rearrange("p a (b w) -> p a b w", b=2)

        s_const = sem("zg_const_ready")
        s_chain = sem("dve_step")
        s_first = sem("first_dve_step")
        s_z = sem("z_in_psum")
        s_shift = sem("logits_shifted")
        s_exp = sem("gates_exp")
        s_zg = sem("zg_ready")
        r_zT = Ring(sem("zgT_in_psum"), 1)
        r_zTs = Ring(sem("zgT_ready"), 1)
        r_lora = Ring(sem("lora_done"), 1)
        s_h = sem("h_in_psum")
        r_h = Ring(sem("h_ready"), 2)
        r_y = Ring(sem("y_in_psum"), 1)
        r_out = Ring(sem("x_updated"), 1)

        block = ctx.enter_context(nc.Block())

        @block.tensor
        def _(pe):
            r_zT.grant(pe)
            r_lora.grant(pe)
            r_y.grant(pe)
            k.r_xnT_psum.grant(pe)
            k.r_xnT_used.grant(pe)
            k.wait_weights(pe, "l1f")
            ln_transpose(k, pe, 0, bankX)

            def turn_zg(unit):
                pe.wait_ge(s_zg, unit + 1)
                r_zTs.wait_free(pe, unit)
                for c in range(GS):
                    ins = pe.transpose(bankZT[0:ZW, seq(c)], zg[:, c, :], k.ident[:, :])
                ins.then_inc(r_zT.sem, 1)

            def first_z(g, par):
                k.r_xnT.wait_done(pe, g)
                for c in range(GS):
                    ins = pe.matmul(zview[:, c, :], k.xnT[:, par, seq(c)], k.w["l1f_ar1"][:, :], start=True, stop=True)
                ins.then_inc(s_z, 1)

            def base(g, par, n):
                r_h.wait_free(pe, g * NHB + n)
                return pe.matmul(bankH[n % 2][:, :], k.w["l1f_w1"][:, seq(n)], k.xnT[:, par, :], start=True, stop=False)

            def lora(n):
                pe.matmul(bankH[n % 2][:, :], k.w["l1f_b1"][:, seq(n)], zgT[0][:, :], start=False, stop=True)\
                  .then_inc(s_h, 1)

            first_z(0, 0)
            ln_transpose(k, pe, 1, bankX)
            turn_zg(0)
            base(0, 0, 0)
            base(0, 0, 1)

            def body(t, par, more, chain):
                r_zTs.wait_done(pe, 2 * t)
                lora(0)
                lora(1)
                base(t, par, 2)
                lora(2)
                base(t, par, 3).then_inc(k.r_xnT_used.sem, 1)
                lora(3)
                if more:
                    first_z(t + 1, 1 - par)
                r_out.wait_free(pe, t)
                r_h.wait_done(pe, t * NHB + NHB - 1)
                for c in range(GS):
                    for n in range(NHB):
                        ins = pe.matmul(yview[:, c // 2, c % 2, :], hT[:, n, seq(c)], k.w["l1f_w2ar"][:, n, :],
                                        start=(n == 0), stop=(n == NHB - 1))
                ins.then_inc(r_y.sem, 1)
                if more:
                    turn_zg(2 * t + 1)
                    if not isinstance(t, int):
                        ln_transpose(k, pe, t + 2, bankX)
                    base(t + 1, 1 - par, 0)
                    base(t + 1, 1 - par, 1)
                second = 2 * t + 1 + more
                turn_zg(second)
                r_zTs.wait_done(pe, second)
                for c in range(GS):
                    ins = pe.matmul(bankR[:, seq(c)], zgT[1][:, seq(c)], k.w["l1f_b2"][:, :], start=True, stop=True)
                ins.then_inc(r_lora.sem, 1)

            groups(pe, body)

        @block.scalar
        def _(act):
            r_zTs.grant(act)
            r_h.grant(act)
            k.r_xnT.grant(act)
            act.wait_ge(s_const, 3)
            ln_evacuate(k, act, 0, 0, bankX)

            def gates(unit, which):
                act.wait_ge(s_shift, unit + 1)
                act.activation(expd[:, :, :], shifted[:, :, :], ACT.Exp).then_inc(s_exp, 1)
                r_zT.wait_done(act, unit)
                act.activation(zgT[which][0:ZW, :], bankZT[0:ZW, :], ACT.Copy).then_inc(r_zTs.sem, 1)

            gates(0, 0)
            ln_evacuate(k, act, 1, 1, bankX)

            def body(t, par, more, chain):
                r_y.wait_free(act, t)
                for n in range(NHB):
                    act.wait_ge(s_h, t * NHB + n + 1)
                    act.activation(hT[:, n, :], bankH[n % 2][:, :], ACT.Relu).then_inc(r_h.sem, 1)
                if more:
                    gates(2 * t + 1, 0)
                if not isinstance(t, int):
                    ln_evacuate(k, act, t + 2, par, bankX)
                r_lora.wait_free(act, t)
                gates(2 * t + 1 + more, 1)

            groups(act, body)

        @block.gpsimd
        def _(pool):
            pool.memset(zgT[0][:, :], 0.0).then_inc(s_const, 1)
            pool.memset(zgT[1][:, :], 0.0).then_inc(s_const, 1)
            ln_rstd(k, pool, 0)
            ln_rstd(k, pool, 1)
            groups(pool, lambda t, par, more, chain: ln_rstd(k, pool, t + 2) if not isinstance(t, int) else None)

        @block.vector
        def _(dve):
            r_out.grant(dve)
            dve.memset(zg[:, :, NZ + 1:ZW], 0.0)
            dve.memset(zg[:, :, NZ:NZ + 1], 1.0).then_inc(s_const, 1)
            ln_stats(k, dve, 0)
            ln_apply(k, dve, 0)

            def gates(unit, chain, logits, zs):
                chain(dve.tensor_reduce(small[:, 0, :], logits, AX, ALU.max))
                mx = small[:, 0, :].rearrange("p (a b) -> p a b", a=logits.shape[1]) if len(logits.shape) == 4 \
                    else small[:, 0, :]
                sh = shifted[:, :, :]
                if len(logits.shape) == 4:
                    sh = shifted[:, :, :].rearrange("p (a b) e -> p a b e", a=2)
                dve.tensor_tensor(sh, logits, bcast(mx.unsqueeze(len(mx.shape)), logits.shape),
                                  ALU.subtract).then_inc(s_shift, 1)
                dve.wait_ge(s_exp, unit + 1)
                chain(dve.tensor_reduce(small[:, 1, :], expd[:, :, :], AX, ALU.add))
                chain(dve.tensor_scalar(small[:, 2, :], small[:, 1, :], float(RANK), None, ALU.mult))
                chain(dve.reciprocal(small[:, 3, :], small[:, 2, :]))
                chain(dve.tensor_tensor(gate[:, :, :], expd[:, :, :],
                                        bcast(small[:, 3, :].unsqueeze(2), [P, GS, NE1]), ALU.mult))
                r_zT.wait_free(dve, unit)
                n = GS // len(zs)
                for a, z in enumerate(zs):
                    part = slice(a * n, a * n + n)
                    ins = dve.tensor_tensor(zg[:, part, 0:NZ].rearrange("p c (e r) -> p c e r", e=NE1), z,
                                            bcast(gate[:, part, :].unsqueeze(3), [P, n, NE1, RANK]), ALU.mult)
                ins.then_inc(s_zg, 1)

            def first_gates(g, unit, chain):
                dve.wait_ge(s_z, g + 1)
                gates(unit, chain, zview[:, :, NZ:NZL],
                      [zview[:, :, 0:NZ].rearrange("p c (e r) -> p c e r", e=NE1)])

            first_gates(0, 0, Chain(dve, s_first, 0, 0))
            ln_stats(k, dve, 1)
            ln_apply(k, dve, 1)

            def body(t, par, more, chain):
                if more:
                    first_gates(t + 1, 2 * t + 1, chain)
                if not isinstance(t, int):
                    ln_stats(k, dve, t + 2)
                    ln_apply(k, dve, t + 2)
                r_y.wait_done(dve, t)
                gates(2 * t + 1 + more, chain, yview[:, :, :, P + NZ:WY],
                      [yview[:, a, :, P:P + NZ].rearrange("p c (e r) -> p c e r", e=NE1) for a in range(2)])
                for a in range(2):
                    xs = k.x_sb[:, bass.ds((t * GS + 2 * a) * P, 2 * P)].rearrange("p (c d) -> p c d", c=2)
                    ins = dve.scalar_tensor_tensor(xs, yview[:, a, :, 0:P], k.tanh_g[:, 5:6], xs, ALU.mult, ALU.add)
                chain(ins)
                r_lora.wait_done(dve, t)
                xs = k.x_sb[:, bass.ds(t * T, T)]
                dve.scalar_tensor_tensor(xs, bankR[:, :], k.tanh_g[:, 5:6], xs, ALU.mult, ALU.add)\
                   .then_inc(r_out.sem, 1)

            groups(dve, body, s_chain, (22, 17))


def layer2_attention(nc, k):
    with ExitStack() as ctx:
        sb, sem = k.local(ctx, "l2x")
        ln_tensors(k, sb, sem)
        ctxT = sb("ctxT", [P, 2, T], F32)
        ctok = sb("ctx_tok", [P, 2, T], F32)
        hwT = sb("h_w3_plus_w2_T", [P, T], F32)
        nmax = sb("minus_max", [P, GS], F32)
        total = sb("total", [P, GS], F32)
        rtot = sb("rtot", [P, GS], F32)
        probs = sb("probs", [P, GS, P], F32)
        attn = sb("attn", [P, GS, P], F32)
        attnT = sb("attnT", [P, T], F32)
        pool_max = sb("row_max", [P, GS], F32)
        pool_nmax = sb("pool_minus_max", [P, GS], F32)
        pool_exp = sb("pool_exp", [P, GS, P], F32)
        pool_tot = sb("pool_total", [P, GS], F32)
        pool_rtot = sb("pool_rtot", [P, GS], F32)
        weighed = sb("weighed", [P, GS, P], F32)
        hsum = sb("h_sum", [P, GS], F32)
        hbar = sb("h_bar", [P, GS], F32)
        aT = sb("aT", [P, T], F32)
        haT = sb("h_times_aT", [P, T], F32)
        hhT = sb("h_times_hbarT", [P, GS, P], F32)
        gb = sb("tanh_g_b", [P, GS, P], F32)
        bankX, bankS, bankE, bankAT, bankA, bankR, bankO = (k.bank(i) for i in range(7))
        w = k.w

        s_chain = sem("dve_step")
        s_first = sem("first_dve_step")
        s_gb = sem("bias_ready")
        r_ctx = Ring(sem("ctx_used"), 2)
        s_ctx = [sem(f"ctx_in_{p}") for p in range(2)]
        r_hw = Ring(sem("hwT_ready"), 1)
        r_s = Ring(sem("sim_in_psum"), 1)
        s_nmax = sem("minus_max_ready")
        s_p = sem("probs_ready")
        s_attn = sem("attn_ready")
        r_at = Ring(sem("attnT_in_psum"), 1)
        s_at = sem("attnT_ready")
        s_rmax = sem("row_max_ready")
        s_r = sem("row_max_spread")
        s_pn = sem("pool_minus_max_ready")
        s_pe = sem("pool_exp_ready")
        s_a = sem("aT_in_psum")
        s_aT = sem("aT_ready")
        s_haT = sem("haT_ready")
        s_feat = sem("feats_ready")
        r_o = Ring(sem("out_in_psum"), 1)
        r_out = Ring(sem("x_updated"), 1)

        block = ctx.enter_context(nc.Block())

        @block.sync
        def _(sp):
            with sp.Fori(0, NG // 2) as it:
                for par in range(2):
                    g = 2 * it + par
                    r_ctx.wait_free(sp, g)
                    for buf, src in ((ctxT, "ctxT"), (ctok, "ctx_tok")):
                        sp.dma_start(buf[:, par, :], k.dram[src][:, bass.ds(g * T, T)]).then_inc(s_ctx[par], 16)

        @block.tensor
        def _(pe):
            for r in (k.r_xnT_psum, k.r_xnT_used, r_ctx, r_s, r_at, r_o):
                r.grant(pe)
            k.wait_weights(pe, "l2x")
            ln_transpose(k, pe, 0, bankX)

            def similarity(g, par):
                xnT, cT = k.xnT[:, par, :], ctxT[:, par, :]
                pe.wait_ge(s_ctx[par], (g - par) * 16 + 32)
                r_hw.wait_done(pe, g)
                for c in range(GS):
                    pe.matmul(bankE[:, c:c + 1], xnT[:, seq(c)], w["l2x_w1"][:, :], start=True, stop=True)
                for c in range(GS):
                    ins = pe.matmul(bankS[:, seq(c)], hwT[:, seq(c)], cT[:, seq(c)], start=True, stop=True)
                ins.then_inc(r_s.sem, 1)

            def attend(g, par, more):
                pe.wait_ge(s_rmax, g + 1)
                for c in range(GS):
                    ins = pe.matmul(bankR[:, seq(c)], bcast(pool_max[:, c:c + 1], [P, P]), k.ident[:, :],
                                    start=True, stop=True)
                ins.then_inc(s_r, 1)
                if more:
                    ln_transpose(k, pe, g + 1, bankX)
                pe.wait_ge(s_attn, g + 1)
                for c in range(GS):
                    ins = pe.transpose(bankAT[:, seq(c)], attn[:, c, :], k.ident[:, :])
                ins.then_inc(r_at.sem, 1)
                pe.wait_ge(s_at, g + 1)
                for c in range(GS):
                    ins = pe.matmul(bankA[:, seq(c)], ctok[:, par, seq(c)], attnT[:, seq(c)], start=True, stop=True)
                ins.then_inc(s_a, 1)

            def out(g, par):
                xnT = k.xnT[:, par, :]
                pe.wait_ge(s_aT, g + 1)
                pe.wait_ge(s_feat, g + 1)
                r_out.wait_free(pe, g)
                for c in range(GS):
                    for n, f in enumerate((xnT[:, seq(c)], aT[:, seq(c)], haT[:, seq(c)], hhT[:, c, :])):
                        ins = pe.matmul(bankO[:, seq(c)], f, w["l2x_wqv"][:, n, :], start=(n == 0), stop=(n == 3))
                ins.then_inc(r_o.sem, 1)
                r_o.wait_done(pe, g)
                pe.sem_inc(r_ctx.sem, 1)
                pe.sem_inc(k.r_xnT_used.sem, 1)

            similarity(0, 0)
            attend(0, 0, True)

            def body(t, par, more, chain):
                if more:
                    similarity(t + 1, 1 - par)
                out(t, par)
                if more:
                    attend(t + 1, 1 - par, not isinstance(t, int))

            groups(pe, body)

        @block.scalar
        def _(act):
            for r in (k.r_xnT,):
                r.grant(act)
            ln_evacuate(k, act, 0, 0, bankX)

            def attend(g, par, more):
                act.wait_ge(s_nmax, g + 1)
                for c in range(GS):
                    ins = act.activation(probs[:, c, :], bankS[:, seq(c)], ACT.Exp, bias=nmax[:, c:c + 1],
                                         accum_out=total[:, c:c + 1])
                ins.then_inc(s_p, 1)
                act.wait_ge(s_pn, g + 1)
                for c in range(GS):
                    ins = act.activation(pool_exp[:, c, :], bankR[:, seq(c)], ACT.Exp,
                                         bias=pool_nmax[:, c:c + 1], accum_out=pool_tot[:, c:c + 1])
                ins.then_inc(s_pe, 1)
                if more:
                    ln_evacuate(k, act, g + 1, 1 - par, bankX)
                r_at.wait_done(act, g)
                act.activation(attnT[:, :], bankAT[:, :], ACT.Copy).then_inc(s_at, 1)
                act.wait_ge(s_haT, g + 1)
                r_o.wait_free(act, g)
                act.activation(aT[:, :], bankA[:, :], ACT.Copy).then_inc(s_aT, 1)

            attend(0, 0, True)
            groups(act, lambda t, par, more, chain: attend(t + 1, 1 - par, not isinstance(t, int)) if more else None)

        @block.gpsimd
        def _(pool):
            ln_rstd(k, pool, 0)
            ln_rstd(k, pool, 1)
            groups(pool, lambda t, par, more, chain: ln_rstd(k, pool, t + 2) if not isinstance(t, int) else None)

        @block.vector
        def _(dve):
            r_hw.grant(dve)
            r_out.grant(dve)
            k.wait_weights(dve, "l2x")
            for c in range(GS):
                ins = dve.tensor_scalar(gb[:, c, :], w["l2x_bqv"][:, :], k.tanh_g[:, 2:3], None, ALU.mult)
            ins.then_inc(s_gb, 1)
            dve.wait_ge(s_gb, 1)
            ln_stats(k, dve, 0)
            ln_apply(k, dve, 0)

            def similarity(g, par):
                xnT = k.xnT[:, par, :]
                k.r_xnT.wait_done(dve, g)
                r_s.wait_free(dve, g)
                dve.tensor_scalar(hwT[:, :], xnT, w["l2x_w3"][:, :], w["l2x_w2"][:, :], ALU.mult, ALU.add)\
                   .then_inc(r_hw.sem, 1)
                r_s.wait_done(dve, g)
                dve.tensor_reduce(nmax[:, :], bankS.rearrange("p (c t) -> p c t", c=GS), AX, ALU.max,
                                  negate=True).then_inc(s_nmax, 1)
                dve.wait_ge(s_nmax, g + 1)
                dve.scalar_tensor_tensor(pool_max[:, :], bankE[:, 0:GS], w["l2x_bsim"][:, 0:1], nmax[:, :],
                                         ALU.add, ALU.subtract).then_inc(s_rmax, 1)

            def attend(g, par, more, chain, update_last=lambda: None):
                xnT = k.xnT[:, par, :]
                xnT3 = xnT.rearrange("p (c t) -> p c t", c=GS)
                if more:
                    ln_stats(k, dve, g + 1)
                dve.wait_ge(s_p, g + 1)
                chain(dve.reciprocal(rtot[:, :], total[:, :]))
                dve.tensor_tensor(attn[:, :, :], probs[:, :, :], bcast(rtot[:, :].unsqueeze(2), [P, GS, P]),
                                  ALU.mult).then_inc(s_attn, 1)
                dve.wait_ge(s_r, g + 1)
                dve.tensor_reduce(pool_nmax[:, :], bankR.rearrange("p (c t) -> p c t", c=GS), AX, ALU.max,
                                  negate=True).then_inc(s_pn, 1)
                if more:
                    ln_apply(k, dve, g + 1)
                xs = k.x_sb[:, bass.ds(g * T, T)]
                dve.tensor_tensor(xs, xs, gb[:, :, :].rearrange("p c d -> p (c d)"), ALU.add)
                update_last()
                dve.wait_ge(s_pe, g + 1)
                chain(dve.tensor_tensor(weighed[:, :, :], xnT3, pool_exp[:, :, :], ALU.mult))
                dve.tensor_reduce(hsum[:, :], weighed[:, :, :], AX, ALU.add)
                chain(dve.reciprocal(pool_rtot[:, :], pool_tot[:, :]))
                chain(dve.tensor_tensor(hbar[:, :], hsum[:, :], pool_rtot[:, :], ALU.mult))
                r_o.wait_free(dve, g)
                dve.tensor_tensor(hhT[:, :, :], xnT3, bcast(hbar[:, :].unsqueeze(2), [P, GS, P]), ALU.mult)\
                   .then_inc(s_feat, 1)
                dve.wait_ge(s_a, g + 1)
                dve.tensor_tensor(haT[:, :], bankA[:, :], xnT, ALU.mult).then_inc(s_haT, 1)

            def update(g):
                xs = k.x_sb[:, bass.ds(g * T, T)]
                r_o.wait_done(dve, g)
                dve.scalar_tensor_tensor(xs, bankO[:, :], k.tanh_g[:, 2:3], xs, ALU.mult, ALU.add)\
                   .then_inc(r_out.sem, 1)

            similarity(0, 0)
            attend(0, 0, True, Chain(dve, s_first, 0, 0))

            def body(t, par, more, chain):
                if more:
                    similarity(t + 1, 1 - par)
                    attend(t + 1, 1 - par, not isinstance(t, int), chain, lambda: update(t))
                else:
                    update(t)

            groups(dve, body, s_chain, (8, 4))


NE2 = 8
NTILE = NSEQ + NE2
MARGIN = 63.5


def tiles(eng, body):
    with eng.Fori(0, NTILE // 2 - 2) as it:
        for par in range(2):
            body(2 * it + par, par)
    for u in range(NTILE - 4, NTILE):
        body(u, u % 2)


def exists(u):
    return not isinstance(u, int) or u < NTILE


def layer2_ffn(nc, k):
    with ExitStack() as ctx:
        sb, sem = k.local(ctx, "l2f")
        ln_tensors(k, sb, sem)
        w = k.w
        all_tokens = [P, NSEQ, NE2]
        zeros = sb("zeros", [P, P], F32)
        h_all = sb("h_all", [P, NSEQ * P], F32)
        lg = sb("logits", all_tokens, F32)
        sh = sb("logits_shifted", all_tokens, F32)
        ex = sb("gate_exp", all_tokens, F32)
        ta = sb("select", all_tokens, F32)
        hot = sb("chosen", all_tokens, F32)
        top = sb("tops", [P, 5, NSEQ], F32)
        gate = k.routed_gate
        upto = [sb(f"tokens_up_to_{i}", all_tokens, F32) for i in range(2)]
        tot = sb("tokens_of_sequence", all_tokens, F32)
        cnt = sb("expert_tiles", [P, NE2], F32)
        ends = [sb(f"tiles_up_to_{i}", [P, NE2], F32) for i in range(2)]
        base = sb("expert_base", [P, NE2], F32)
        pos_f = sb("pos_f32", [P, NSEQ], F32)
        pos = k.routed_pos
        le = sb("tile_past_expert", [P, NTILE, NE2], F32)
        te_f = sb("tile_expert_f32", [P, NTILE], F32)
        te = sb("tile_expert", [P, NTILE], I32)
        xt = sb("x_tile", [P, 2, P], F32)
        xT = sb("xT_tile", [P, 2, P], F32)
        hp = sb("h_tile", [P, 2, HID], F32)
        hT = sb("hT_tile", [P, 2, HID], F32)
        yt = sb("y_tile", [P, 2, P], F32)
        sorted_x = nc.dram_tensor("l2f_sorted_x", (NTILE * P, P), F32).ap()
        sorted_y = k.routed_y
        bankX, bankM = k.bank(0), k.bank(7)
        bankU, bankH, bankY = [k.bank(1), k.bank(2)], [k.bank(3), k.bank(4)], [k.bank(5), k.bank(6)]

        s_zeros = sem("zeros_ready")
        s_zeroed = sem("sorted_x_zeroed")
        s_step = sem("dve_step")
        s_logits = sem("logits_in_psum")
        r_logits = Ring(sem("logits_ready"), 1)
        s_shift = sem("logits_shifted_ready")
        s_ex = sem("gate_exp_ready")
        s_hot = sem("chosen_ready")
        s_count = sem("counts_in_psum")
        s_pos = sem("pos_ready")
        s_te = sem("tile_expert_ready")
        s_scatter = sem("rows_scattered")
        s_x = [sem(f"x_tile_in_{p}") for p in range(2)]
        r_turn = Ring(sem("x_tile_turned"), 2)
        r_xT = Ring(sem("xT_tile_ready"), 1)
        r_up = Ring(sem("h_in_psum"), 2)
        r_hp = Ring(sem("h_tile_ready"), 2)
        r_turnh = Ring(sem("h_tile_turned"), 2)
        r_hT = Ring(sem("hT_tile_ready"), 2)
        r_y = Ring(sem("y_in_psum"), 2)
        r_yt = Ring(sem("y_tile_ready"), 2)
        s_out = [sem(f"y_tile_out_{p}") for p in range(2)]

        block = ctx.enter_context(nc.Block())

        @block.sync
        def _(sp):
            sp.wait_ge(s_zeros, 1)
            sp.dma_start(sorted_x.rearrange("(u p) d -> p u d", p=P), bcast(zeros[:, :].unsqueeze(1), [P, NTILE, P]))\
              .then_inc(s_zeroed, 16)
            sp.wait_ge(s_scatter, 16 * NSEQ)

            def load(u, par):
                r_turn.wait_free(sp, u)
                sp.dma_start(xt[:, par, :], sorted_x[bass.ds(u * P, P), :]).then_inc(s_x[par], 16)

            tiles(sp, load)

        @block.tensor
        def _(pe):
            for r in (k.r_xnT_psum, k.r_xnT_used, r_turn, r_up, r_turnh, r_y):
                r.grant(pe)
            k.wait_weights(pe, "l2f")
            ln_transpose(k, pe, 0, bankX)

            def route(g, par, more, chain):
                k.r_xnT.wait_done(pe, g)
                r_logits.wait_free(pe, g)
                for c in range(GS):
                    ins = pe.matmul(bankM[:, c * NE2:(c + 1) * NE2], k.xnT[:, par, seq(c)], w["l2f_router"][:, :],
                                    start=True, stop=True)
                ins.then_inc(s_logits, 1)
                if more:
                    ln_transpose(k, pe, g + 1, bankX)
                r_logits.wait_done(pe, g)
                pe.sem_inc(k.r_xnT_used.sem, 1)

            groups(pe, route)

            pe.wait_ge(s_hot, 1)
            flat = hot[:, :, :].rearrange("p c e -> p (c e)")
            pe.matmul(bankY[0][:, 0:NSEQ * NE2], k.before[:, :], flat, start=True, stop=True)
            pe.matmul(bankY[1][:, 0:NSEQ * NE2], k.ones[:, :], flat, start=True, stop=True).then_inc(s_count, 1)
            pe.wait_ge(s_te, 1)

            def expert(u):
                return pe.value_load(te[0:1, bass.ds(u, 1)], min_val=0, max_val=NE2 - 1)

            def turn_x(u, par):
                pe.wait_ge(s_x[par], (u - par) * 8 + 16)
                r_xT.wait_free(pe, u)
                pe.transpose(bankX[:, 0:P], xt[:, par, :], k.ident[:, :]).then_inc(r_turn.sem, 1)

            def up(u, par):
                e = expert(u)
                r_xT.wait_done(pe, u)
                r_hp.wait_free(pe, u)
                pe.matmul(bankU[par][:, :], xT[:, par, :], w["l2f_w1"][:, bass.ds(e * HID, HID)], start=True,
                          stop=True).then_inc(r_up.sem, 1)

            def turn_h(u, par):
                r_hp.wait_done(pe, u)
                r_hT.wait_free(pe, u)
                for n in range(NHB):
                    ins = pe.transpose(bankH[par][:, seq(n)], hp[:, par, seq(n)], k.ident[:, :])
                ins.then_inc(r_turnh.sem, 1)

            def down(u, par):
                e = expert(u)
                r_hT.wait_done(pe, u)
                r_yt.wait_free(pe, u)
                for n in range(NHB):
                    ins = pe.matmul(bankY[par][:, 0:P], hT[:, par, seq(n)], w["l2f_w2"][:, bass.ds(e * HID + n * P, P)],
                                    start=(n == 0), stop=(n == NHB - 1))
                ins.then_inc(r_y.sem, 1)

            turn_x(0, 0)
            up(0, 0)
            turn_x(1, 1)
            up(1, 1)
            turn_x(2, 0)
            turn_h(0, 0)

            def body(u, par):
                if exists(u + 3):
                    turn_x(u + 3, 1 - par)
                if exists(u + 2):
                    up(u + 2, par)
                if exists(u + 1):
                    turn_h(u + 1, 1 - par)
                down(u, par)

            tiles(pe, body)

        @block.scalar
        def _(act):
            for r in (k.r_xnT, r_xT, r_hT):
                r.grant(act)
            ln_evacuate(k, act, 0, 0, bankX)
            groups(act, lambda g, par, more, chain: ln_evacuate(k, act, g + 1, 1 - par, bankX) if more else None)
            act.wait_ge(s_shift, 1)
            act.activation(ex[:, :, :], sh[:, :, :], ACT.Exp).then_inc(s_ex, 1)

            def evacuate(u, par):
                r_turn.wait_done(act, u)
                r_up.wait_free(act, u)
                act.activation(xT[:, par, :], bankX[:, 0:P], ACT.Copy).then_inc(r_xT.sem, 1)

            for u in range(3):
                evacuate(u, u % 2)

            def body(u, par):
                r_turnh.wait_done(act, u)
                r_y.wait_free(act, u)
                act.activation(hT[:, par, :], bankH[par][:, :], ACT.Relu).then_inc(r_hT.sem, 1)
                if exists(u + 3):
                    evacuate(u + 3, 1 - par)

            tiles(act, body)

        @block.gpsimd
        def _(pool):
            ln_rstd(k, pool, 0)
            groups(pool, lambda g, par, more, chain: ln_rstd(k, pool, g + 1) if more else None)
            pool.wait_ge(s_zeroed, 16)
            pool.wait_ge(s_pos, 1)
            for c in range(NSEQ):
                pool.indirect_dma_start(sorted_x[:, :], bass.IndirectOffsetOnAxis(pos[:, c:c + 1], 0),
                                        h_all[:, seq(c)], None).then_inc(s_scatter, 16)
            def store(u, par):
                r_yt.wait_done(pool, u)
                pool.dma_start(sorted_y[bass.ds(u * P, P), :], yt[:, par, :]).then_inc(s_out[par], 16)

            tiles(pool, store)
            for par in range(2):
                pool.wait_ge(s_out[par], 16 * NTILE // 2)

        @block.vector
        def _(dve):
            for r in (r_logits, r_hp, r_yt):
                r.grant(dve)
            dve.memset(zeros[:, :], 0.0).then_inc(s_zeros, 1)
            k.wait_weights(dve, "l2f")

            def norm(g):
                ln_stats(k, dve, g)
                ln_apply(k, dve, g)
                dve.wait_ge(k.s_xn, g + 1)
                dve.tensor_copy(h_all[:, bass.ds(g * T, T)], k.xn[:, :, :].rearrange("p c d -> p (c d)"))

            norm(0)

            def route(g, par, more, chain):
                if more:
                    norm(g + 1)
                dve.wait_ge(s_logits, g + 1)
                n = GS * NE2
                dve.tensor_tensor(lg[:, :, :].rearrange("p c e -> p (c e)")[:, bass.ds(g * n, n)],
                                  bankM[:, 0:n], w["l2f_router_b"][:, :], ALU.add).then_inc(r_logits.sem, 1)

            groups(dve, route)
            r_logits.wait_done(dve, NG - 1)

            def per_token(ap):
                return bcast(ap.unsqueeze(2), all_tokens)

            def per_expert(ap, n=NSEQ):
                return bcast(ap.unsqueeze(1), [P, n, NE2])

            step = Chain(dve, s_step, 0, 0)
            step(dve.tensor_reduce(top[:, 0, :], lg[:, :, :], AX, ALU.max))
            dve.tensor_tensor(sh[:, :, :], lg[:, :, :], per_token(top[:, 0, :]), ALU.subtract).then_inc(s_shift, 1)
            dve.wait_ge(s_ex, 1)
            dve.tensor_reduce(top[:, 1, :], ex[:, :, :], AX, ALU.add)
            step(dve.tensor_reduce(top[:, 2, :], ex[:, :, :], AX, ALU.max))
            dve.reciprocal(top[:, 3, :], top[:, 1, :])
            step(dve.tensor_tensor(ta[:, :, :], ex[:, :, :], per_token(top[:, 2, :]), ALU.is_equal))
            dve.scalar_tensor_tensor(gate[:, :], top[:, 2, :], k.tanh_g[:, 6:7], top[:, 3, :], ALU.mult, ALU.mult)
            step(dve.tensor_tensor(ta[:, :, :], ta[:, :, :], per_expert(k.descending[:, 0, NE3 - NE2:NE3]), ALU.mult))
            step(dve.tensor_reduce(top[:, 4, :], ta[:, :, :], AX, ALU.max))
            dve.tensor_tensor(hot[:, :, :], ta[:, :, :], per_token(top[:, 4, :]), ALU.is_equal).then_inc(s_hot, 1)

            dve.wait_ge(s_count, 1)
            counts = lambda bank: bank[:, 0:NSEQ * NE2].rearrange("p (c e) -> p c e", c=NSEQ)
            step(dve.tensor_copy(tot[:, :, :], counts(bankY[1])))

            def scan(src, buffers, n):
                stride, flip = 1, 0
                while stride < n:
                    dst = buffers[flip]
                    dve.tensor_copy(dst[:, 0:stride], src[:, 0:stride])
                    step(dve.tensor_tensor(dst[:, stride:n], src[:, stride:n], src[:, 0:n - stride], ALU.add))
                    src, flip, stride = dst, 1 - flip, 2 * stride
                return src

            inclusive = scan(tot, upto, NSEQ)
            step(dve.tensor_scalar(cnt[:, :], inclusive[:, NSEQ - 1, :], MARGIN, 1.0 / P, ALU.add, ALU.mult))
            step(dve.tensor_scalar(cnt[:, :], cnt[:, :], MAGIC, MAGIC, ALU.add, ALU.subtract))
            end = scan(cnt, ends, NE2)
            dve.tensor_tensor(base[:, :], end[:, :], cnt[:, :], ALU.subtract)
            step(dve.tensor_tensor(le[:, :, :], per_expert(end[:, :], NTILE),
                                   bcast(k.tile_index[:, :].unsqueeze(2), [P, NTILE, NE2]), ALU.is_le))
            dve.tensor_scalar(base[:, :], base[:, :], float(P), None, ALU.mult)
            step(dve.tensor_reduce(te_f[:, :], le[:, :, :], AX, ALU.add))
            step(dve.tensor_scalar(te_f[:, :], te_f[:, :], float(NE2 - 1), None, ALU.min))
            dve.tensor_copy(te[:, :], te_f[:, :]).then_inc(s_te, 1)
            other = upto[1] if inclusive is upto[0] else upto[0]
            step(dve.tensor_tensor(other[:, :, :], inclusive[:, :, :], tot[:, :, :], ALU.subtract))
            step(dve.tensor_tensor(other[:, :, :], other[:, :, :], per_expert(base[:, :]), ALU.add))
            step(dve.tensor_tensor(other[:, :, :], other[:, :, :], counts(bankY[0]), ALU.add))
            step(dve.tensor_tensor(other[:, :, :], other[:, :, :], hot[:, :, :], ALU.mult))
            step(dve.tensor_reduce(pos_f[:, :], other[:, :, :], AX, ALU.add))
            dve.tensor_copy(pos[:, :], pos_f[:, :]).then_inc(s_pos, 1)
            dve.wait_ge(s_te, 1)

            def expert(u):
                return dve.value_load(te[0:1, bass.ds(u, 1)], min_val=0, max_val=NE2 - 1)

            def add_b1(u, par):
                e = expert(u)
                r_up.wait_done(dve, u)
                r_turnh.wait_free(dve, u)
                dve.tensor_tensor(hp[:, par, :], bankU[par][:, :], w["l2f_b1"][:, bass.ds(e * HID, HID)], ALU.add)\
                   .then_inc(r_hp.sem, 1)

            def add_b2(u, par):
                e = expert(u)
                r_y.wait_done(dve, u)
                if not isinstance(u, int) or u >= 2:
                    dve.wait_ge(s_out[par], (u - par) * 8)
                dve.tensor_tensor(yt[:, par, :], bankY[par][:, 0:P], w["l2f_b2"][:, bass.ds(e * P, P)], ALU.add)\
                   .then_inc(r_yt.sem, 1)

            add_b1(0, 0)
            add_b1(1, 1)

            def body(u, par):
                if exists(u + 2):
                    add_b1(u + 2, par)
                add_b2(u, par)

            tiles(dve, body)


def layer3_attention(nc, k):
    with ExitStack() as ctx:
        sb, sem = k.local(ctx, "l3x")
        ln_tensors(k, sb, sem)
        amax = sb("amax", [P, 3], F32)
        amax_all = sb("amax_all", [P, 3], F32)
        step = sb("step", [P, 3], F32)
        inv = sb("inv", [P, 3], F32)
        wr = sb("w_rounded", [P, 3, P], F32)
        wi = sb("w_steps", [P, 3, P], F32)
        gbv = sb("tanh_g_bv", [P, GS, P], F32)
        back = sb("routed_y_of_token", [P, 2, GS, P], F32)
        ctxT = sb("ctxT", [P, 2, T], F32)
        qT = sb("qT", [P, T], F32)
        kT = sb("kT", [P, T], F32)
        v = sb("v", [P, 2, GS, P], F32)
        nmax = sb("nmax", [P, GS], F32)
        nmax_s = sb("nmax_scaled", [P, GS], F32)
        probs = sb("probs", [P, GS, P], F32)
        probsT = sb("probsT", [P, T], F32)
        total = sb("total", [P, GS], F32)
        rtot = sb("rtot", [P, GS], F32)
        rg = sb("rtot_tanh_g", [P, GS], F32)
        bankX, bankQ, bankK, bankV, bankS, bankPT, bankO, bankM = (k.bank(i) for i in range(8))
        scale = float(P) ** -0.5

        s_back = [sem(f"rows_gathered_{p}") for p in range(2)]
        s_gated = sem("rows_gated")
        s_routed = sem("rows_added")
        s_prep = sem("weights_step")
        s_all = sem("absmax_everywhere")
        s_amT = sem("absmax_turned")
        s_wr = sem("w_rounded_ready")
        s_chain = sem("dve_step")
        r_ctx = Ring(sem("ctxT_used"), 2)
        s_ctx = [sem(f"ctxT_in_{p}") for p in range(2)]
        s_q, s_kk, s_v = sem("q_in_psum"), sem("k_in_psum"), sem("v_in_psum")
        r_proj = Ring(sem("qkv_ready"), 1)
        r_s = Ring(sem("scores_in_psum"), 1)
        s_nmax = sem("minus_max_ready")
        r_p = Ring(sem("probs_ready"), 1)
        r_pt = Ring(sem("probsT_in_psum"), 1)
        r_pts = Ring(sem("probsT_ready"), 1)
        r_o = Ring(sem("out_in_psum"), 1)
        r_out = Ring(sem("x_updated"), 1)
        r_xb = Ring(sem("x_plus_bias"), 1)

        block = ctx.enter_context(nc.Block())

        @block.sync
        def _(sp):
            with sp.Fori(0, NG // 2) as it:
                for par in range(2):
                    g = 2 * it + par
                    r_ctx.wait_free(sp, g)
                    sp.dma_start(ctxT[:, par, :], k.dram["ctxT"][:, bass.ds(g * T, T)]).then_inc(s_ctx[par], 16)

        @block.tensor
        def _(pe):
            for r in (k.r_xnT_psum, k.r_xnT_used, r_ctx, r_s, r_pt, r_o):
                r.grant(pe)
            k.wait_weights(pe, "l3x")
            pe.wait_ge(s_prep, 1)
            pe.transpose(bankM[0:3, 0:P], amax[:, :], k.ident[:, :]).then_inc(s_amT, 1)
            pe.wait_ge(s_prep, 3)
            pe.matmul(bankM[:, P:P + 3], k.ones[0:3, :], wr[0:3, 0, 0:3], start=True, stop=True).then_inc(s_all, 1)
            ln_transpose(k, pe, 0, bankX)
            pe.wait_ge(s_wr, 1)

            def project(g, par):
                xnT, cT = k.xnT[:, par, :], ctxT[:, par, :]
                pe.wait_ge(s_ctx[par], (g - par) * 8 + 16)
                r_proj.wait_free(pe, g)
                pe.matmul(bankK[:, :], wr[:, 1, :], cT, start=True, stop=True).then_inc(s_kk, 1)
                k.r_xnT.wait_done(pe, g)
                pe.matmul(bankQ[:, :], wr[:, 0, :], xnT, start=True, stop=True).then_inc(s_q, 1)
                for c in range(GS):
                    ins = pe.matmul(bankV[:, seq(c)], cT[:, seq(c)], wr[:, 2, :], start=True, stop=True)
                ins.then_inc(s_v, 1)
                pe.wait_ge(s_v, g + 1)
                pe.sem_inc(r_ctx.sem, 1)
                pe.sem_inc(k.r_xnT_used.sem, 1)

            def scores(g):
                r_proj.wait_done(pe, g)
                r_p.wait_free(pe, g)
                for c in range(GS):
                    ins = pe.matmul(bankS[:, seq(c)], qT[:, seq(c)], kT[:, seq(c)], start=True, stop=True)
                ins.then_inc(r_s.sem, 1)

            def turn_probs(g):
                r_p.wait_done(pe, g)
                r_pts.wait_free(pe, g)
                for c in range(GS):
                    ins = pe.transpose(bankPT[:, seq(c)], probs[:, c, :], k.ident[:, :])
                ins.then_inc(r_pt.sem, 1)

            def attend(g, par):
                r_pts.wait_done(pe, g)
                r_out.wait_free(pe, g)
                for c in range(GS):
                    ins = pe.matmul(bankO[:, seq(c)], probsT[:, seq(c)], v[:, par, c, :], start=True, stop=True)
                ins.then_inc(r_o.sem, 1)

            project(0, 0)
            scores(0)
            ln_transpose(k, pe, 1, bankX)

            def body(t, par, more, chain):
                if more:
                    project(t + 1, 1 - par)
                turn_probs(t)
                if more:
                    scores(t + 1)
                attend(t, par)
                if not isinstance(t, int):
                    ln_transpose(k, pe, t + 2, bankX)

            groups(pe, body)

        @block.scalar
        def _(act):
            for r in (k.r_xnT, r_proj, r_p, r_pts):
                r.grant(act)
            ln_evacuate(k, act, 0, 0, bankX)

            def projected(g, par):
                r_s.wait_free(act, g)
                act.wait_ge(s_kk, g + 1)
                act.activation(kT[:, :], bankK[:, :], ACT.Identity, bias=k.w["l3x_bk"][:, :])
                act.wait_ge(s_q, g + 1)
                act.activation(qT[:, :], bankQ[:, :], ACT.Identity, bias=k.w["l3x_bq"][:, :])
                act.wait_ge(s_v, g + 1)
                act.activation(v[:, par, :, :], bankV.rearrange("p (c d) -> p c d", c=GS), ACT.Copy)\
                   .then_inc(r_proj.sem, 1)

            projected(0, 0)
            ln_evacuate(k, act, 1, 1, bankX)

            def body(t, par, more, chain):
                act.wait_ge(s_nmax, t + 1)
                r_pt.wait_free(act, t)
                for c in range(GS):
                    ins = act.activation(probs[:, c, :], bankS[:, seq(c)], ACT.Exp, bias=nmax_s[:, c:c + 1],
                                         scale=scale, accum_out=total[:, c:c + 1])
                ins.then_inc(r_p.sem, 1)
                if more:
                    projected(t + 1, 1 - par)
                r_pt.wait_done(act, t)
                r_o.wait_free(act, t)
                act.activation(probsT[:, :], bankPT[:, :], ACT.Copy).then_inc(r_pts.sem, 1)
                if not isinstance(t, int):
                    ln_evacuate(k, act, t + 2, par, bankX)

            groups(act, body)

        @block.gpsimd
        def _(pool):
            def gather(g):
                for c in range(GS):
                    pool.indirect_dma_start(back[:, g % 2, c, :], None, k.routed_y[:, :],
                                            bass.IndirectOffsetOnAxis(k.routed_pos[:, g * GS + c:g * GS + c + 1], 0))\
                        .then_inc(s_back[g % 2], 16)

            gather(0)
            gather(1)
            for g in range(NG):
                ln_rstd(k, pool, g)
                if g + 2 < NG:
                    gather(g + 2)

        @block.vector
        def _(dve):
            r_out.grant(dve)
            k.wait_weights(dve, "l3x")
            prep = Chain(dve, s_prep, 0, 0)
            for i, n in enumerate(("l3x_wq", "l3x_wk", "l3x_wv")):
                ins = dve.tensor_reduce(amax[:, i:i + 1], k.w[n][:, :], AX, ALU.max, apply_absolute_value=True)
            prep(ins)
            dve.wait_ge(s_amT, 1)
            prep(dve.tensor_reduce(amax_all[0:3, 0:1], bankM[0:3, 0:P], AX, ALU.max))
            prep(dve.tensor_scalar(wr[0:3, 0, 0:3], k.ident[0:3, 0:3], amax_all[0:3, 0:1], None, ALU.mult))
            dve.wait_ge(s_all, 1)
            prep(dve.tensor_scalar(step[:, :], bankM[:, P:P + 3], 2.0 / 256.0, None, ALU.mult))
            prep(dve.reciprocal(inv[:, :], step[:, :]))
            for i, n in enumerate(("l3x_wq", "l3x_wk", "l3x_wv")):
                prep(dve.tensor_scalar(wi[:, i, :], k.w[n][:, :], inv[:, i:i + 1], MAGIC, ALU.mult, ALU.add))
                ins = dve.tensor_scalar(wr[:, i, :], wi[:, i, :], -MAGIC, step[:, i:i + 1], ALU.add, ALU.mult)
            ins.then_inc(s_wr, 1)
            for c in range(GS):
                ins = dve.tensor_scalar(gbv[:, c, :], k.w["l3x_bv"][:, :], k.tanh_g[:, 3:4], None, ALU.mult)
            prep(ins)

            def add_routed(g, par):
                dve.wait_ge(s_back[par], (g - par) * 8 * GS + 16 * GS)
                dve.tensor_tensor(back[:, par, :, :], back[:, par, :, :],
                                  bcast(k.routed_gate[:, bass.ds(g * GS, GS)].unsqueeze(2), [P, GS, P]), ALU.mult)\
                   .then_inc(s_gated, 1)
                xs = k.x_sb[:, bass.ds(g * T, T)]
                dve.wait_ge(s_gated, g + 1)
                dve.tensor_tensor(xs, xs, back[:, par, :, :].rearrange("p c d -> p (c d)"), ALU.add)\
                   .then_inc(s_routed, 1)
                dve.wait_ge(s_routed, g + 1)
                dve.tensor_copy(k.one_cell[:, :], k.eps[:, 0:1])

            add_routed(0, 0)
            ln_stats(k, dve, 0)
            ln_apply(k, dve, 0)
            add_routed(1, 1)
            ln_stats(k, dve, 1)
            ln_apply(k, dve, 1)

            def body(g, par, more, chain):
                after = not isinstance(g, int)
                r_s.wait_done(dve, g)
                chain(dve.tensor_reduce(nmax[:, :], bankS.rearrange("p (c w) -> p c w", c=GS), AX, ALU.max,
                                        negate=True))
                dve.tensor_scalar(nmax_s[:, :], nmax[:, :], scale, None, ALU.mult).then_inc(s_nmax, 1)
                if after:
                    add_routed(g + 2, par)
                    ln_stats(k, dve, g + 2)
                    ln_apply(k, dve, g + 2)
                xs = k.x_sb[:, bass.ds(g * T, T)]
                dve.tensor_tensor(xs, xs, gbv[:, :, :].rearrange("p c d -> p (c d)"), ALU.add)
                r_p.wait_done(dve, g)
                chain(dve.reciprocal(rtot[:, :], total[:, :]))
                chain(dve.tensor_scalar(rg[:, :], rtot[:, :], k.tanh_g[:, 3:4], None, ALU.mult))
                r_o.wait_done(dve, g)
                for c in range(GS):
                    xc = k.x_sb[:, bass.ds((g * GS + c) * P, P)]
                    ins = dve.scalar_tensor_tensor(xc, bankO[:, seq(c)], rg[:, c:c + 1], xc, ALU.mult, ALU.add)
                ins.then_inc(r_out.sem, 1)

            groups(dve, body, s_chain, 6)


NE3 = 16


def layer3_ffn(nc, k):
    with ExitStack() as ctx:
        sb, sem = k.local(ctx, "l3f")
        ln_tensors(k, sb, sem)
        w = k.w
        sq = sb("sim_squared", [P, NE3], F32)
        cnorm = sb("column_norm", [P, NE3], F32)
        cinv = sb("column_rnorm", [P, NE3], F32)
        sn = sb("sim_normed", [P, NE3], F32)
        sig = sb("sigmoid_gates", [P, NE3], F32)
        sig_e = sb("exp_minus_gates", [P, NE3], F32)
        xsq = sb("xn_squared", [P, GS, P], F32)
        ssum = sb("xn_sum_squares", [P, GS], F32)
        rnorm = sb("xn_rnorm", [P, GS], F32)
        lg = sb("logits", [P, GS, NE3], F32)
        gated = sb("gated", [P, GS, NE3], F32)
        hard = sb("hard", [P, GS, NE3], F32)
        ta = sb("select_a", [P, GS, NE3], F32)
        tb = sb("select_b", [P, GS, NE3], F32)
        tc = sb("select_c", [P, GS, NE3], F32)
        top = sb("tops", [P, 8, GS], F32)
        ex = sb("gate_exp", [P, GS, NE3], F32)
        w3 = sb("w_parts", [P, GS, P], BF16)
        wr1 = sb("w_rest1", [P, GS, NE3], F32)
        wT = sb("w_partsT", [P, 2, T], BF16)
        wE = sb("w_e_kept", [P, 2, NE3, T], F32)
        xe = sb("weighted_T", [P, 2, T], F32)
        qT, kT, vT, oT = (sb(n, [P, T], F32) for n in ("qT", "kT", "vT", "oT"))
        v = sb("v", [P, GS, P], F32)
        nmax = sb("minus_max", [P, GS], F32)
        probs = sb("probs", [P, GS, P], F32)
        probsT = sb("probsT", [P, T], F32)
        attn = sb("attn", [P, GS, P], F32)
        total = sb("total", [P, GS], F32)
        rtot = sb("rtot", [P, GS], F32)
        yT = sb("yT", [P, T], F32)
        bankW = [k.bank(0), k.bank(1)]
        bankQ, bankK, bankV, bankX, bankS, bankM = (k.bank(i) for i in range(2, 8))
        scale = float(P) ** -0.5

        s_prep = sem("prep_step")
        s_csum = sem("column_sums")
        s_cpow = sem("column_rnorm_ready")
        s_sige = sem("exp_minus_gates_ready")
        s_chain = sem("dve_step")
        s_gates = sem("logits_in_psum")
        s_ss = sem("sum_squares_ready")
        s_rn0 = sem("sum_squares_clamped")
        s_rn = sem("xn_rnorm_ready")
        s_gx = sem("gated_shifted")
        s_ex = sem("gate_exp_ready")
        s_w3 = sem("w_parts_ready")
        s_wTp = sem("w_partsT_in_psum")
        r_wT = Ring(sem("w_partsT_ready"), 1)
        r_wTu = Ring(sem("w_partsT_used"), 2)
        s_we = sem("w_e_spread")
        r_xe = Ring(sem("weighted_ready"), 2)
        r_xu = Ring(sem("weighted_used"), 2)
        r_wE = Ring(sem("w_e_kept_ready"), 2)
        r_qkv = Ring(sem("qkv_ready"), 1)
        s_vt = sem("v_turned")
        r_v = Ring(sem("v_ready"), 1)
        s_s = sem("scores_in_psum")
        s_nmax = sem("minus_max_ready")
        s_p = sem("probs_ready")
        s_attn = sem("attn_ready")
        s_pt = sem("probsT_in_psum")
        s_pts = sem("probsT_ready")
        s_o = sem("oT_in_psum")
        s_oT = sem("oT_ready")
        s_y = sem("yT_in_psum")
        s_yT = sem("yT_ready")
        s_yt = sem("y_in_psum")
        r_out = Ring(sem("x_updated"), 1)

        block = ctx.enter_context(nc.Block())

        @block.tensor
        def _(pe):
            for r in (k.r_xnT_psum, k.r_xnT_used, r_wTu, r_xu):
                r.grant(pe)
            k.wait_weights(pe, "l3f")
            pe.wait_ge(s_prep, 1)
            pe.matmul(bankM[:, 0:NE3], k.ones[:, :], sq[:, :], start=True, stop=True).then_inc(s_csum, 1)
            ln_transpose(k, pe, 0, bankX)
            pe.wait_ge(s_prep, 3)

            def route(g, par):
                k.r_xnT.wait_done(pe, g)
                for c in range(GS):
                    ins = pe.matmul(bankM[:, c * NE3:(c + 1) * NE3], k.xnT[:, par, seq(c)], sn[:, :],
                                    start=True, stop=True)
                ins.then_inc(s_gates, 1)

            def turn_weights(g):
                pe.wait_ge(s_w3, g + 1)
                for c in range(GS):
                    ins = pe.transpose(bankM[:, 256:512].bitcast(BF16)[:, seq(c)], w3[:, c, :], k.ident_bf[:, :])
                ins.then_inc(s_wTp, 1)

            def experts(first, operands, banks, between, which=range(NE3)):
                for e in which:
                    r_xe.wait_done(pe, first + e)
                    between(e)
                    for name, bank in zip(operands, banks):
                        ins = pe.matmul(bank[:, :], w[name][:, e, :], xe[:, e % 2, :],
                                        start=(e == 0), stop=(e == NE3 - 1))
                    ins.then_inc(r_xu.sem, 1)

            def spread(g, par, e):
                r_wE.wait_free(pe, g * NE3 + e)
                pe.matmul(bankW[e % 2][:, :], k.select[:, e, :], wT[:, par, :], start=True, stop=True)\
                  .then_inc(s_we, 1)

            def first_spreads(g, par):
                r_wT.wait_done(pe, g)
                spread(g, par, 0)
                spread(g, par, 1)

            def qkv_experts(g, par, first, which, between=lambda e: None):
                def step(e):
                    if e + 2 < NE3:
                        spread(g, par, e + 2)

                for e in which:
                    experts(first, ("l3f_q", "l3f_k", "l3f_v"), (bankQ, bankK, bankV), step, (e,))
                    between(e)

            def first_expert(g, par, first):
                r_qkv.wait_free(pe, g)
                qkv_experts(g, par, first, (0,))

            def qkv_mixed(first):
                r_xu.wait_done(pe, first + NE3 - 1)
                pe.sem_inc(k.r_xnT_used.sem, 1)
                pe.sem_inc(r_wTu.sem, 1)

            def router_between(g, par, e):
                if e == 2:
                    ln_transpose(k, pe, g, bankX)
                if e == 4:
                    route(g, par)
                if e == NE3 - 2:
                    turn_weights(g)

            def attention_between(t, e):
                if e == 1:
                    r_qkv.wait_done(pe, t)
                    r_out.wait_free(pe, t)
                    for c in range(GS):
                        ins = pe.transpose(bankX[:, seq(c)], vT[:, seq(c)], k.ident[:, :])
                    ins.then_inc(s_vt, 1)
                    for c in range(GS):
                        ins = pe.matmul(bankS[:, seq(c)], qT[:, seq(c)], kT[:, seq(c)], start=True, stop=True)
                    ins.then_inc(s_s, 1)
                    r_v.wait_done(pe, t)
                if e == 5:
                    pe.wait_ge(s_attn, t + 1)
                    for c in range(GS):
                        ins = pe.transpose(bankS[:, seq(c)], attn[:, c, :], k.ident[:, :])
                    ins.then_inc(s_pt, 1)
                if e == 7:
                    pe.wait_ge(s_pts, t + 1)
                    for c in range(GS):
                        ins = pe.matmul(bankX[:, seq(c)], v[:, c, :], probsT[:, seq(c)], start=True, stop=True)
                    ins.then_inc(s_o, 1)

            route(0, 0)
            turn_weights(0)
            first_spreads(0, 0)
            first_expert(0, 0, 0)
            qkv_experts(0, 0, 0, range(1, NE3), lambda e: router_between(1, 1, e))
            first_spreads(1, 1)
            qkv_mixed(0)
            first_expert(1, 1, NE3)

            def body(t, par, more, chain):
                after = not isinstance(t, int)
                first = (2 * t + 1) * NE3

                def between(e):
                    attention_between(t, e)
                    if after:
                        router_between(t + 2, par, e)

                if more:
                    between(0)
                    qkv_experts(t + 1, 1 - par, first, range(1, NE3), between)
                    out_first = first + NE3
                else:
                    for e in range(NE3):
                        between(e)
                    out_first = first
                if after:
                    first_spreads(t + 2, par)
                experts(out_first, ("l3f_o",), (bankS,), lambda e: None)
                if more:
                    qkv_mixed(first)
                if after:
                    first_expert(t + 2, par, out_first + NE3)
                pe.wait_ge(s_yT, t + 1)
                for c in range(GS):
                    ins = pe.transpose(bankX[:, seq(c)], yT[:, seq(c)], k.ident[:, :])
                ins.then_inc(s_yt, 1)

            groups(pe, body)

        @block.scalar
        def _(act):
            for r in (k.r_xnT, r_wT, r_wE, r_qkv, r_v):
                r.grant(act)
            k.wait_weights(act, "l3f")
            act.activation(sig_e[:, :], w["l3f_gates"][:, :], ACT.Exp, scale=-1.0).then_inc(s_sige, 1)
            ln_evacuate(k, act, 0, 0, bankX)

            def gates_exp(g):
                act.wait_ge(s_gx, g + 1)
                act.activation(ex[:, :, :], tb[:, :, :], ACT.Exp).then_inc(s_ex, 1)

            def weights_out(g, par):
                act.wait_ge(s_wTp, g + 1)
                r_wTu.wait_free(act, g)
                act.activation(wT[:, par, :], bankM[:, 256:512].bitcast(BF16), ACT.Copy).then_inc(r_wT.sem, 1)

            def keep(g, par, experts):
                for e in experts:
                    act.wait_ge(s_we, g * NE3 + e + 1)
                    act.activation(wE[:, par, e, :], bankW[e % 2][:, :], ACT.Copy).then_inc(r_wE.sem, 1)

            def qkv_out(first):
                r_xu.wait_done(act, first + NE3 - 1)
                act.activation(vT[:, :], bankV[:, :], ACT.Copy)
                act.activation(qT[:, :], bankQ[:, :], ACT.Copy)
                act.activation(kT[:, :], bankK[:, :], ACT.Copy).then_inc(r_qkv.sem, 1)

            gates_exp(0)
            weights_out(0, 0)
            keep(0, 0, range(0, 5))
            ln_evacuate(k, act, 1, 1, bankX)
            keep(0, 0, range(5, 8))
            gates_exp(1)
            keep(0, 0, range(8, NE3))
            weights_out(1, 1)
            qkv_out(0)
            keep(1, 1, range(2))

            def body(t, par, more, chain):
                after = not isinstance(t, int)
                first = (2 * t + 1) * NE3

                def keep_next(*experts):
                    if more:
                        keep(t + 1, 1 - par, range(*experts))

                keep_next(2, 4)
                act.wait_ge(s_vt, t + 1)
                act.activation(v[:, :, :], bankX.rearrange("p (c d) -> p c d", c=GS), ACT.Copy)\
                   .then_inc(r_v.sem, 1)
                keep_next(4, 5)
                if after:
                    ln_evacuate(k, act, t + 2, par, bankX)
                act.wait_ge(s_nmax, t + 1)
                for c in range(GS):
                    ins = act.activation(probs[:, c, :], bankS[:, seq(c)], ACT.Exp, bias=nmax[:, c:c + 1],
                                         scale=scale, accum_out=total[:, c:c + 1])
                ins.then_inc(s_p, 1)
                keep_next(5, 8)
                act.wait_ge(s_pt, t + 1)
                act.activation(probsT[:, :], bankS[:, :], ACT.Copy).then_inc(s_pts, 1)
                if after:
                    gates_exp(t + 2)
                keep_next(8, 10)
                act.wait_ge(s_o, t + 1)
                act.activation(oT[:, :], bankX[:, :], ACT.Copy).then_inc(s_oT, 1)
                keep_next(10, NE3)
                if after:
                    weights_out(t + 2, par)
                if more:
                    qkv_out(first)
                if after:
                    r_xe.wait_done(act, first + NE3 + 1)
                    keep(t + 2, par, range(2))
                r_xu.wait_done(act, first + (2 if more else 1) * NE3 - 1)
                act.activation(yT[:, :], bankS[:, :], ACT.Copy).then_inc(s_yT, 1)

            groups(act, body)

        @block.gpsimd
        def _(pool):
            pool.wait_ge(s_prep, 2)
            pool.tensor_tensor(cinv[:, :], cnorm[:, :], k.minus_half[:, 0:NE3], ALU.pow).then_inc(s_cpow, 1)
            ln_rstd(k, pool, 0)

            def norms(g):
                pool.wait_ge(s_ss, g + 1)
                pool.tensor_tensor(rnorm[:, :], ssum[:, :], k.minus_half[:, 0:GS], ALU.pow).then_inc(s_rn, 1)

            norms(0)
            ln_rstd(k, pool, 1)
            norms(1)

            def body(t, par, more, chain):
                if not isinstance(t, int):
                    ln_rstd(k, pool, t + 2)
                    norms(t + 2)

            groups(pool, body)

        @block.vector
        def _(dve):
            r_xe.grant(dve)
            r_out.grant(dve)
            k.wait_weights(dve, "l3f")
            prep = Chain(dve, s_prep, 0, 0)
            prep(dve.tensor_tensor(sq[:, :], w["l3f_sim"][:, :], w["l3f_sim"][:, :], ALU.mult))
            ln_stats(k, dve, 0)
            dve.wait_ge(s_csum, 1)
            prep(dve.tensor_scalar(cnorm[:, :], bankM[:, 0:NE3], 1e-24, None, ALU.max))
            ln_apply(k, dve, 0)
            dve.wait_ge(s_cpow, 1)
            prep(dve.tensor_tensor(sn[:, :], w["l3f_sim"][:, :], cinv[:, :], ALU.mult))
            dve.wait_ge(s_sige, 1)
            prep(dve.tensor_scalar(sig_e[:, :], sig_e[:, :], 1.0, None, ALU.add))
            dve.memset(w3[:, :, :], 0.0)
            prep(dve.reciprocal(sig[:, :], sig_e[:, :]))

            first = Chain(dve, sem("first_gates_step"), 0, 0)

            def both(ap):
                return bcast(ap.unsqueeze(2), [P, GS, NE3])

            def norms(g, chain):
                dve.wait_ge(k.s_xn, g + 1)
                chain(dve.tensor_tensor(xsq[:, :, :], k.xn[:, :, :], k.xn[:, :, :], ALU.mult))
                chain(dve.tensor_reduce(top[:, 0, :], xsq[:, :, :], AX, ALU.add))
                dve.tensor_scalar(ssum[:, :], top[:, 0, :], 1e-24, None, ALU.max).then_inc(s_ss, 1)

            def logits(g, chain):
                raw = bankM[:, 0:GS * NE3].rearrange("p (c e) -> p c e", c=GS)
                dve.wait_ge(s_gates, g + 1)
                dve.wait_ge(s_rn, g + 1)
                chain(dve.tensor_tensor(ta[:, :, :], raw, both(rnorm[:, :]), ALU.mult))
                chain(dve.tensor_tensor(lg[:, :, :], ta[:, :, :], bcast(sig[:, :].unsqueeze(1), [P, GS, NE3]),
                                        ALU.subtract))
                dve.tensor_scalar(hard[:, :, :], lg[:, :, :], 0.0, None, ALU.is_gt)
                chain(dve.tensor_scalar(gated[:, :, :], lg[:, :, :], 0.0, None, ALU.max))
                chain(dve.tensor_reduce(top[:, 1, :], gated[:, :, :], AX, ALU.max))
                dve.tensor_tensor(tb[:, :, :], gated[:, :, :], both(top[:, 1, :]), ALU.subtract).then_inc(s_gx, 1)
                chain(dve.tensor_scalar(top[:, 2, :], top[:, 1, :], 0.0, None, ALU.is_le))

            def find_largest(chain):
                chain(dve.tensor_reduce(top[:, 3, :], lg[:, :, :], AX, ALU.max))
                chain(dve.tensor_tensor(ta[:, :, :], lg[:, :, :], both(top[:, 3, :]), ALU.is_equal))
                chain(dve.tensor_tensor(ta[:, :, :], ta[:, :, :], k.descending[:, :, :], ALU.mult))
                chain(dve.tensor_reduce(top[:, 4, :], ta[:, :, :], AX, ALU.max))
                chain(dve.tensor_tensor(tc[:, :, :], ta[:, :, :], both(top[:, 4, :]), ALU.is_equal))

            def take_largest(chain):
                chain(dve.scalar_tensor_tensor(lg[:, :, :], tc[:, :, :], -1e30, lg[:, :, :], ALU.mult, ALU.add))
                chain(dve.tensor_tensor(ta[:, :, :], tc[:, :, :], both(top[:, 2, :]), ALU.mult))
                chain(dve.tensor_tensor(hard[:, :, :], hard[:, :, :], ta[:, :, :], ALU.add))

            def token_weights(g, chain):
                dve.wait_ge(s_ex, g + 1)
                chain(dve.tensor_tensor(ta[:, :, :], ex[:, :, :], hard[:, :, :], ALU.mult))
                chain(dve.tensor_reduce(top[:, 5, :], ta[:, :, :], AX, ALU.add))
                chain(dve.reciprocal(top[:, 6, :], top[:, 5, :]))
                chain(dve.tensor_tensor(ta[:, :, :], ta[:, :, :], both(top[:, 6, :]), ALU.mult))

            def weight_parts(chain):
                chain(dve.tensor_copy(w3[:, :, 0:NE3], ta[:, :, :]))
                chain(dve.tensor_tensor(wr1[:, :, :], ta[:, :, :], w3[:, :, 0:NE3], ALU.subtract))
                chain(dve.tensor_copy(w3[:, :, NE3:2 * NE3], wr1[:, :, :]))
                dve.tensor_tensor(w3[:, :, 2 * NE3:3 * NE3], wr1[:, :, :], w3[:, :, NE3:2 * NE3], ALU.subtract)\
                   .then_inc(s_w3, 1)

            def router_between(g, e, chain):
                if e == 0:
                    ln_stats(k, dve, g)
                if e == 1:
                    ln_apply(k, dve, g)
                if e == 2:
                    norms(g, chain)
                if e == 5:
                    logits(g, chain)
                if e in (6, 8):
                    find_largest(chain)
                if e in (7, 9):
                    take_largest(chain)
                if e == 10:
                    token_weights(g, chain)
                if e == 11:
                    weight_parts(chain)

            def attention_between(t, e, chain):
                if e == 2:
                    dve.wait_ge(s_s, t + 1)
                    chain(dve.tensor_reduce(top[:, 7, :], bankS.rearrange("p (c t) -> p c t", c=GS), AX, ALU.max,
                                            negate=True))
                    dve.tensor_scalar(nmax[:, :], top[:, 7, :], scale, None, ALU.mult).then_inc(s_nmax, 1)
                if e == 4:
                    dve.wait_ge(s_p, t + 1)
                    chain(dve.reciprocal(rtot[:, :], total[:, :]))
                    dve.tensor_tensor(attn[:, :, :], probs[:, :, :], bcast(rtot[:, :].unsqueeze(2), [P, GS, P]),
                                      ALU.mult).then_inc(s_attn, 1)

            def weigh(g, par, first, src, which, between=lambda e: None):
                for e in which:
                    r_wE.wait_done(dve, g * NE3 + e)
                    r_xu.wait_free(dve, first + e)
                    dve.tensor_tensor(xe[:, e % 2, :], wE[:, par, e, :], src, ALU.mult).then_inc(r_xe.sem, 1)
                    between(e)

            for e in range(2, NE3):
                router_between(0, e, first)
            weigh(0, 0, 0, k.xnT[:, 0, :], range(NE3), lambda e: router_between(1, e, first))
            weigh(1, 1, NE3, k.xnT[:, 1, :], range(2))

            def body(t, par, more, chain):
                after = not isinstance(t, int)
                first = (2 * t + 1) * NE3

                def between(e):
                    attention_between(t, e, chain)
                    if after:
                        router_between(t + 2, e, chain)

                if more:
                    between(0)
                    between(1)
                    weigh(t + 1, 1 - par, first, k.xnT[:, 1 - par, :], range(2, NE3), between)
                    out_first = first + NE3
                else:
                    for e in range(NE3):
                        between(e)
                    out_first = first
                dve.wait_ge(s_oT, t + 1)
                weigh(t, par, out_first, oT[:, :], range(NE3))
                if after:
                    weigh(t + 2, par, out_first + NE3, k.xnT[:, par, :], range(2))
                dve.wait_ge(s_yt, t + 1)
                xs = k.x_sb[:, bass.ds(t * T, T)]
                dve.scalar_tensor_tensor(xs, bankX[:, :], k.tanh_g[:, 7:8], xs, ALU.mult, ALU.add)\
                   .then_inc(r_out.sem, 1)

            groups(dve, body, s_chain, (LINKS3, LINKS3_LAST))


LINKS3, LINKS3_LAST = 64, 4


def launch_constants():
    freq = (np.float32(1) / np.float32(10000) ** (np.arange(0, HD, 2, dtype=np.float32) / np.float32(HD)))
    angle = np.repeat(np.repeat(freq.astype(np.float32), 2), HEADS)[:, None] * np.arange(P, dtype=np.float32)[None]
    sign = np.tile(np.repeat(np.array([-1, 1], np.float32), HEADS), HD // 2)[:, None]
    part_of = np.zeros((P, NE3), np.float32)
    for e in range(NE3):
        part_of[e:3 * NE3:NE3, e] = 1
    return {
        "l0x_cos": np.tile(np.cos(angle), (1, GS)),
        "l0x_sin": np.tile(np.sin(angle) * sign, (1, GS)),
        "ident": np.eye(P, dtype=np.float32),
        "part_of": part_of,
        "before": np.triu(np.ones((P, P), np.float32), 1),
        "tile_index": np.tile(np.arange(NTILE, dtype=np.float32), (P, 1)),
        "descending": np.tile(np.arange(NE3, 0, -1, dtype=np.float32), (P, GS)),
    }


CONSTANTS = {"ident": [P, P], "part_of": [P, NE3], "before": [P, P], "tile_index": [P, NTILE],
             "descending": [P, GS * NE3]}


def width(shapes):
    return sum(shape[1] for shape in shapes.values())


def columns(tensor, shapes):
    at, views = 0, {}
    for name, shape in shapes.items():
        views[name] = tensor[:, at:at + shape[1]]
        at += shape[1]
    return views


class Global(Core):
    def __init__(self, nc, ctx, dram):
        self.nc, self.ctx, self.dram, self.w, self.loads = nc, ctx, dram, {}, {}
        self.rest_of_x_loaded = False
        sb = lambda name, shape, dt: ctx.enter_context(nc.sbuf_tensor(name, shape, dt))
        self.psum = ctx.enter_context(nc.psum_tensor("psum", [P, 8 * 512], F32))
        self.x_sb = sb("x_sb", [P, NSEQ * P], F32)
        self.constants = sb("constants", [P, width(CONSTANTS)], F32)
        at = columns(self.constants, CONSTANTS)
        self.ident, self.part_of = at["ident"], at["part_of"]
        self.before = at["before"]
        self.tile_index = at["tile_index"]
        self.descending = at["descending"].rearrange("p (c e) -> p c e", c=GS)
        self.ident_bf = sb("ident_bf", [P, P], BF16)
        self.select = sb("select", [P, NE3, P], BF16)
        self.minus_half = sb("minus_half", [P, 16], F32)
        self.ones = sb("ones", [P, P], F32)
        self.one_cell = sb("one_cell", [P, 1], F32)
        self.eps = sb("eps", [P, GS], F32)
        self.g_in = sb("g_in", [P, 8], F32)
        self.tanh_g = sb("tanh_g", [P, 8], F32)

    def bank(self, i):
        return self.psum[:, i * 512:(i + 1) * 512]

    def banks(self, i, n):
        return self.psum[:, i * 512:(i + n) * 512]

    def local(self, ctx, prefix):
        sb = lambda name, shape, dt: ctx.enter_context(self.nc.sbuf_tensor(f"{prefix}_{name}", shape, dt))
        used = []
        ctx.callback(self.nc.all_engine_barrier)
        ctx.callback(lambda: self.nc.clear_and_free_semaphores(used))

        def sem(name):
            used.append(self.nc.alloc_semaphore(f"{prefix}_{name}"))
            return used[-1]

        return sb, sem

    def weights(self, layer, ctx):
        for packed, shapes in PACKED.get(layer, {}).items():
            tensor = ctx.enter_context(self.nc.sbuf_tensor("w_" + packed, [P, width(shapes)], F32))
            self.w.update(columns(tensor, shapes))
            self.loads.setdefault(layer, []).append((packed, tensor))
        for name, shape in WEIGHTS[layer].items():
            self.w[name] = ctx.enter_context(self.nc.sbuf_tensor("w_" + name, shape, F32))
            self.loads.setdefault(layer, []).append((name, self.w[name]))

    def load_rest_of_x(self, sp):
        if not self.rest_of_x_loaded:
            sp.dma_start(self.x_sb[:, 2 * T:], self.dram["x"][:, 2 * T:]).then_inc(self.s_x, 16)
            self.rest_of_x_loaded = True

    def load_other_weights(self, sp):
        load_weights(self, sp, self.early)
        self.early = []

    def wait_weights(self, eng, layer):
        eng.wait_ge(self.s_weights[layer], 16 * len(self.loads[layer]))


ATTN = {"wq": [P, P], "wk": [P, P], "wv": [P, P], "wo": [P, P], "bq": [P, 1], "bk": [P, 1], "bv": [P, 1],
        "bo": [P, P]}
WEIGHTS = {
    "l0x": {"l0x_bo": [P, P]},
    "l1x": {"l1x_" + n: s for n, s in ATTN.items()},
    "l0f": {"l0f_w1": [P, HID], "l0f_w2": [P, NHB, P], "l0f_cw": [P, 3 * HID], "l0f_cb": [P, NHB]},
    "l2f": {"l2f_router": [P, NE2], "l2f_router_b": [P, GS * NE2], "l2f_w1": [P, NE2 * HID],
            "l2f_b1": [P, NE2 * HID], "l2f_w2": [P, NE2 * HID], "l2f_b2": [P, NE2 * P]},
    "l2x": {"l2x_w1": [P, 1], "l2x_w2": [P, 1], "l2x_w3": [P, 1], "l2x_bsim": [P, 1], "l2x_wqv": [P, 4, P],
            "l2x_bqv": [P, P]},
    "l3f": {"l3f_sim": [P, NE3], "l3f_gates": [P, NE3], "l3f_q": [P, NE3, P], "l3f_k": [P, NE3, P],
            "l3f_v": [P, NE3, P], "l3f_o": [P, NE3, P]},
    "l3x": {"l3x_wq": [P, P], "l3x_wk": [P, P], "l3x_wv": [P, P], "l3x_bq": [P, 1], "l3x_bk": [P, 1],
            "l3x_bv": [P, P]},
    "l1f": {"l1f_ar1": [P, NZL], "l1f_w1": [P, HID], "l1f_b1": [P, HID], "l1f_w2ar": [P, NHB, P + NZL],
            "l1f_b2": [P, P]},
}
PACKED = {"l0x": {
    "l0x_projections": {"l0x_" + n: ATTN[n.rstrip("s")] for n in ("wk", "wks", "wq", "wqs", "wv", "wo", "bk", "bks",
                                                                  "bq", "bqs", "bv")},
    "l0x_rotary": {"l0x_cos": [P, T], "l0x_sin": [P, T]}}}
LAYERS = {"l0x": layer0_attention, "l0f": layer0_ffn, "l1x": layer1_attention, "l1f": layer1_ffn,
          "l2x": layer2_attention, "l2f": layer2_ffn, "l3x": layer3_attention, "l3f": layer3_ffn}
LATE = ("l2f", "l3f")


def load_weights(k, sp, layers):
    for layer in layers:
        for name, w in k.loads[layer]:
            src = k.dram[name]
            if tuple(src.shape) != tuple(w.shape):
                src = bcast(src, w.shape)
            sp.dma_start(w[:], src).then_inc(k.s_weights[layer], 16)


def program(nc, dram, out, layers):
    with ExitStack() as ctx:
        k = Global(nc, ctx, dram)
        k.s_weights = {}
        for layer in layers:
            k.s_weights[layer] = ctx.enter_context(nc.semaphore(f"weights_{layer}_in"))
            if layer not in LATE:
                k.weights(layer, ctx)
        s_x_head = ctx.enter_context(nc.semaphore("x_head_in"))
        k.s_x = ctx.enter_context(nc.semaphore("x_rest_in"))
        s_const = ctx.enter_context(nc.semaphore("constants_in"))
        k.s_filled = ctx.enter_context(nc.semaphore("fills_ready"))
        s_tanh = ctx.enter_context(nc.semaphore("tanh_g_ready"))
        s_out = ctx.enter_context(nc.semaphore("x_out"))

        k.early = [layer for layer in layers[1:] if layer not in LATE]

        with nc.Block() as block:
            @block.sync
            def _(sp):
                sp.dma_start(k.constants[:, :], dram["constants"]).then_inc(s_const, 16)
                sp.dma_start(k.g_in[:, :], bcast(dram["gains"], [P, 8])).then_inc(s_const, 16)
                head = slice(0, 2 * T)
                sp.dma_start(k.x_sb[:, head], dram["x"][:, head]).then_inc(s_x_head, 16)
                load_weights(k, sp, layers[:1])
                if layers[0] not in ("l0x", "l1x"):
                    k.load_rest_of_x(sp)
                    k.load_other_weights(sp)

            @block.vector
            def _(dve):
                dve.memset(k.minus_half[:, :], -0.5).then_inc(k.s_filled, 1)
                dve.memset(k.ones[:, :], 1.0).then_inc(k.s_filled, 1)
                dve.memset(k.eps[:, :], LN_EPS).then_inc(k.s_filled, 1)
                dve.wait_ge(s_const, 32)
                dve.tensor_copy(k.ident_bf[:, :], k.ident[:, :]).then_inc(k.s_filled, 1)
                dve.tensor_copy(k.select[:, :, :], bcast(k.part_of[:, :].unsqueeze(2), [P, NE3, P]))\
                   .then_inc(k.s_filled, 1)
                dve.wait_ge(k.s_filled, 5)
                dve.wait_ge(s_x_head, 16)

            @block.scalar
            def _(act):
                act.wait_ge(s_const, 32)
                act.activation(k.tanh_g[:, :], k.g_in[:, :], ACT.Tanh).then_inc(s_tanh, 1)
                act.wait_ge(s_tanh, 1)

        early = [layer for layer in layers if layer in ("l0x", "l0f", "l1x")]
        late = [layer for layer in layers if layer in LATE]
        for layer in early:
            LAYERS[layer](nc, k)
        room = {layer: ctx.enter_context(ExitStack()) for layer in reversed(late)}
        for layer in reversed(late):
            k.weights(layer, room[layer])
        if "l2f" in late:
            k.routed_pos = room["l2f"].enter_context(nc.sbuf_tensor("routed_pos", [P, NSEQ], I32))
            k.routed_gate = room["l2f"].enter_context(nc.sbuf_tensor("routed_tanh_g_gates", [P, NSEQ], F32))
            k.routed_y = nc.dram_tensor("routed_y", (NTILE * P, P), F32).ap()
        with nc.Block() as block:
            @block.sync
            def _(sp):
                load_weights(k, sp, late)

        for layer in layers[len(early):]:
            LAYERS[layer](nc, k)
            if layer == "l3x":
                room["l2f"].close()

        with nc.Block() as block:
            @block.sync
            def _(sp):
                sp.dma_start(out, k.x_sb[:, :]).then_inc(s_out, 16)
                sp.wait_ge(s_out, 16)


def layouts(i):
    f = lambda a: np.ascontiguousarray(a, dtype=np.float32)
    pad = lambda a, rows: np.concatenate([a, np.zeros((rows - a.shape[0],) + a.shape[1:], np.float32)])
    tok = lambda a: f(np.transpose(a, (1, 0, 2)).reshape(P, NSEQ * P))
    d = launch_constants()
    d["x"] = tok(i["x"])
    d["ctx_tok"] = tok(i["ctx_1024"])
    d["ctxT"] = f(np.transpose(i["ctx_1024"], (2, 0, 1)).reshape(P, NSEQ * P))
    d["gains"] = f(np.concatenate([i["g_xattn"], i["g_ffn"]]).reshape(1, 8))
    swap = np.arange(P) ^ 1
    by_d = np.arange(P).reshape(HEADS, HD).T.ravel()
    for n in (0, 1):
        for m in "qk":
            wm, bm = i[f"L{n}_xattn_W{m}"], i[f"L{n}_xattn_b{m}"]
            d[f"l{n}x_w{m}"], d[f"l{n}x_b{m}"] = f(wm[by_d].T), f(bm[by_d].reshape(P, 1))
            if n == 0:
                d[f"l0x_w{m}s"], d[f"l0x_b{m}s"] = f(wm[swap][by_d].T), f(bm[swap][by_d].reshape(P, 1))
        d[f"l{n}x_wv"], d[f"l{n}x_wo"] = f(i[f"L{n}_xattn_Wv"].T), f(i[f"L{n}_xattn_Wo"].T)
        d[f"l{n}x_bv"], d[f"l{n}x_bo"] = f(i[f"L{n}_xattn_bv"].reshape(P, 1)), f(i[f"L{n}_xattn_bo"].reshape(1, P))
    d["l0f_w1"] = f(i["L0_ffn_w1"].T)
    d["l0f_w2"] = f(np.transpose(i["L0_ffn_w2"].T.reshape(NHB, P, P), (1, 0, 2)))
    d["l0f_cw"] = f(i["L0_ffn_conv_w"].reshape(HID, 3).T.reshape(1, 3 * HID))
    d["l0f_cb"] = f(i["L0_ffn_conv_b"].reshape(NHB, P).T)
    d["l2f_router"] = f(i["L2_ffn_router_W"])
    d["l2f_router_b"] = f(np.tile(i["L2_ffn_router_b"].reshape(1, NE2), (1, GS)))
    d["l2f_w1"] = f(np.transpose(i["L2_ffn_W1"], (1, 0, 2)).reshape(P, NE2 * HID))
    d["l2f_b1"] = f(i["L2_ffn_b1"].reshape(1, NE2 * HID))
    d["l2f_w2"] = f(np.transpose(i["L2_ffn_W2"].reshape(NE2, NHB, P, P), (2, 0, 1, 3)).reshape(P, NE2 * HID))
    d["l2f_b2"] = f(i["L2_ffn_b2"].reshape(1, NE2 * P))
    for n in range(3):
        d[f"l2x_w{n + 1}"] = f(i["L2_xattn_w_sim"][n * P:(n + 1) * P].reshape(P, 1))
    d["l2x_bsim"] = f(i["L2_xattn_b_sim"].reshape(1, 1))
    d["l2x_wqv"] = f(np.transpose(i["L2_xattn_W_qv"].reshape(4, P, P), (1, 0, 2)))
    d["l2x_bqv"] = f(i["L2_xattn_b_qv"].reshape(1, P))
    for n in "qkvo":
        d[f"l3f_{n}"] = f(np.transpose(i[f"L3_ffn_{n}_proj"], (1, 0, 2)))
    d["l3f_sim"] = f(i["L3_ffn_sim_matrix"])
    d["l3f_gates"] = f(i["L3_ffn_gates"].reshape(1, NE3))
    d["l3x_wq"], d["l3x_wk"], d["l3x_wv"] = (f(i[f"L3_xattn_W{n}"]) for n in "qkv")
    d["l3x_bq"], d["l3x_bk"] = (f(i[f"L3_xattn_b{n}"].reshape(P, 1)) for n in "qk")
    d["l3x_bv"] = f(i["L3_xattn_bv"].reshape(1, P))
    flat_a = lambda a: np.transpose(a, (1, 0, 2)).reshape(a.shape[1], NZ)
    d["l1f_ar1"] = f(np.concatenate([flat_a(i["L1_ffn_A1"]), i["L1_ffn_R1"]], 1))
    d["l1f_w1"] = f(i["L1_ffn_W1"])
    d["l1f_b1"] = f(pad(np.concatenate([i["L1_ffn_B1"].reshape(NZ, HID), i["L1_ffn_b1"][None]]), P))
    w2ar = np.concatenate([i["L1_ffn_W2"], flat_a(i["L1_ffn_A2"]), i["L1_ffn_R2"]], 1)
    d["l1f_w2ar"] = f(np.transpose(w2ar.reshape(NHB, P, P + NZL), (1, 0, 2)))
    d["l1f_b2"] = f(pad(np.concatenate([i["L1_ffn_B2"].reshape(NZ, P), i["L1_ffn_b2"][None]]), P))
    for name, shapes in [("constants", CONSTANTS)] + [item for packed in PACKED.values() for item in packed.items()]:
        d[name] = np.concatenate([d.pop(part) for part in shapes], 1)
    return d


def kernel(**inputs):
    import concourse.bacc as bacc
    from concourse.bass_utils import run_bass_kernel_spmd

    arrays = layouts({n: np.asarray(a) for n, a in inputs.items()})
    nc = bacc.Bacc("TRN2", target_bir_lowering=False, num_devices=1)
    dram = {n: nc.dram_tensor(f"in_{n}", a.shape, mybir.dt.from_np(a.dtype), kind="ExternalInput").ap()
            for n, a in arrays.items()}
    out = nc.dram_tensor("out_x", (P, NSEQ * P), F32, kind="ExternalOutput").ap()
    program(nc, dram, out, list(LAYERS))
    r = run_bass_kernel_spmd(nc, [{f"in_{n}": a for n, a in arrays.items()}], core_ids=[0])
    x = r.results[0]["out_x"]
    return np.ascontiguousarray(x.reshape(P, NSEQ, P).transpose(1, 0, 2))
```
